# Optimizing a Trainium2 kernel written in Bass

```python
import numpy as np
import jax
import jax.numpy as jnp

def _softmax(x, axis=-1):
    return jax.nn.softmax(x, axis=axis)

def _gelu(x):
    return jax.nn.gelu(x, approximate=True)

def _silu(x):
    return jax.nn.silu(x)

def _sigmoid(x):
    return jax.nn.sigmoid(x)

def _layernorm(x, axis=-1, eps=1e-05):
    m = jnp.mean(x, axis=axis, keepdims=True)
    v = jnp.var(x, axis=axis, keepdims=True)
    return (x - m) / jnp.sqrt(v + eps)

def _scatter_add(tgt, idx, src, axis=0):
    return tgt.at[idx].add(src)

def _segment_sum(src, seg, n):
    return jax.ops.segment_sum(src, seg, n)
kernel_name = 'mk_xattn_ffn_d2_seqx_r8_b48968'

def setup_inputs(seed: int=0):
    np.random.seed(seed)
    _w = jnp.asarray

    def _rec_inputs():
        import jax
        import jax.numpy as jnp
        _rk = jax.random.key(seed)
        x = -0.0002928 + 1 * jax.random.normal(jax.random.fold_in(_rk, 1), (8, 256, 128), jnp.float32)
        _lenS = 256 - jax.random.randint(jax.random.fold_in(_rk, 7), (8,), 0, max(1, 256 // 4) + 1, jnp.int32)
        _lenS2 = 1601 - jax.random.randint(jax.random.fold_in(_rk, 8), (8,), 0, max(1, 1601 // 4) + 1, jnp.int32)
        _ctx_1024P = jax.random.normal(jax.random.fold_in(_rk, 11), (8, 16, 128), jnp.float32)
        _ctx_1024c = jax.random.dirichlet(jax.random.fold_in(_rk, 511), 0.3 * jnp.ones((16,), jnp.float32), (8, 1601))
        _ctx_1024t = jnp.einsum('bsk,bkd->bsd', _ctx_1024c, _ctx_1024P)
        _ctx_1024t = _ctx_1024t * jax.lax.rsqrt(jnp.mean(jnp.square(_ctx_1024t)) + 1e-12) * 0.953939
        ctx_1024 = -1.39393e-06 + 0.999914 * (_ctx_1024t + 0.3 * jax.random.normal(jax.random.fold_in(_rk, 611), (8, 1601, 128), jnp.float32))
        itok_BxSx64_0_2047 = jax.random.randint(jax.random.fold_in(_rk, 12), (8, 256, 64), 0, 256, jnp.int32)
        return (x, ctx_1024, itok_BxSx64_0_2047)
    x, ctx_1024, itok_BxSx64_0_2047 = _rec_inputs()

    def _L0_xattn_setup():
        import jax, jax.numpy as jnp
        import numpy as np
        DIM = 128
        NUM_HEADS = 16
        HEAD_DIM = DIM // NUM_HEADS
        key = jax.random.key(seed)
        ks = jax.random.split(key, 8)
        B, N, N2 = (2, 256, 256)
        s = 1.0 / np.sqrt(DIM)
        return {'x': jax.random.normal(ks[0], (B, N, DIM), jnp.float32), 'y': jax.random.normal(ks[1], (B, N2, DIM), jnp.float32), 'Wq': jax.random.normal(ks[2], (DIM, DIM), jnp.float32) * s, 'bq': jnp.zeros((DIM,), jnp.float32), 'Wkv': jax.random.normal(ks[3], (DIM, 2 * DIM), jnp.float32) * s, 'bkv': jnp.zeros((2 * DIM,), jnp.float32), 'Wo': jax.random.normal(ks[4], (DIM, DIM), jnp.float32) * s, 'bo': jnp.zeros((DIM,), jnp.float32)}
    _L0_xattn_all = _L0_xattn_setup()
    _L0_xattn_in = {k: v for k, v in _L0_xattn_all.items() if k in ('Wq', 'bq', 'Wkv', 'bkv', 'Wo', 'bo')}
    del _L0_xattn_all

    def _L0_ffn_setup():
        import jax, jax.numpy as jnp
        import numpy as np
        TOP_K = 2
        ROUTE_SCALE = 1.0
        EPS = 1e-20
        key = jax.random.key(seed)
        ks = jax.random.split(key, 8)
        dim, hid, E, X = (128, 352, 8, 1)
        std = 0.02
        x = jax.random.normal(ks[0], (2, 256, dim), dtype=jnp.float32)
        w1 = jax.random.normal(ks[1], (E, hid, dim), dtype=jnp.float32) * std
        w2 = jax.random.normal(ks[2], (E, dim, hid), dtype=jnp.float32) * std
        w3 = jax.random.normal(ks[3], (E, hid, dim), dtype=jnp.float32) * std
        new_w1 = jax.random.normal(ks[4], (X, hid, dim), dtype=jnp.float32) * std
        new_w2 = jnp.zeros((X, dim, hid), dtype=jnp.float32)
        new_w3 = jax.random.normal(ks[5], (X, hid, dim), dtype=jnp.float32) * std
        gate_weight = jax.random.normal(ks[6], (E, dim), dtype=jnp.float32) * std
        new_gate_weight = jax.random.normal(ks[7], (X, dim), dtype=jnp.float32) * std
        gate_bias = jnp.zeros((X,), dtype=jnp.float32)
        return dict(x=x, w1=w1, w2=w2, w3=w3, new_w1=new_w1, new_w2=new_w2, new_w3=new_w3, gate_weight=gate_weight, new_gate_weight=new_gate_weight, gate_bias=gate_bias)
    _L0_ffn_all = _L0_ffn_setup()
    _L0_ffn_in = {k: v for k, v in _L0_ffn_all.items() if k in ('w1', 'w2', 'w3', 'new_w1', 'new_w2', 'new_w3', 'gate_weight', 'new_gate_weight', 'gate_bias')}
    del _L0_ffn_all

    def _L1_xattn_setup():
        import jax, jax.numpy as jnp
        import numpy as np
        B, NQ, NKV, K = (2, 128, 256, 64)
        D, H, LAT = (128, 16, 128)
        HD = D // H
        SCALE = 1.0 / np.sqrt(HD)
        key = jax.random.key(seed)
        ks = jax.random.split(key, 7)
        s = lambda fan_in: 1.0 / np.sqrt(fan_in)
        return {'x_q': jax.random.normal(ks[0], (B, NQ, D), jnp.float32), 'x_kv': jax.random.normal(ks[1], (B, NKV, D), jnp.float32), 'indices': jax.random.randint(ks[2], (B, NQ, K), 0, NKV), 'W_q': jax.random.normal(ks[3], (D, D), jnp.float32) * s(D), 'W_kv_down': jax.random.normal(ks[4], (LAT, D), jnp.float32) * s(D), 'W_kv_up': jax.random.normal(ks[5], (2 * D, LAT), jnp.float32) * s(LAT), 'W_out': jax.random.normal(ks[6], (D, D), jnp.float32) * s(D)}
    _L1_xattn_all = _L1_xattn_setup()
    _L1_xattn_in = {k: v for k, v in _L1_xattn_all.items() if k in ('W_q', 'W_kv_down', 'W_kv_up', 'W_out')}
    del _L1_xattn_all

    def _L1_ffn_setup():
        import jax, jax.numpy as jnp
        import numpy as np
        B, S, H = (2, 512, 128)
        E, K, I = (8, 2, 176)
        key = jax.random.key(seed)
        ks = jax.random.split(key, 9)
        sc = 0.02
        return {'hidden_states': jax.random.normal(ks[0], (B, S, H), jnp.float32), 'gate_w': jax.random.normal(ks[1], (E, H), jnp.float32) * sc, 'w_gate': jax.random.normal(ks[2], (E, H, I), jnp.float32) * sc, 'w_up': jax.random.normal(ks[3], (E, H, I), jnp.float32) * sc, 'w_down': jax.random.normal(ks[4], (E, I, H), jnp.float32) * sc, 'sw_gate': jax.random.normal(ks[5], (H, I), jnp.float32) * sc, 'sw_up': jax.random.normal(ks[6], (H, I), jnp.float32) * sc, 'sw_down': jax.random.normal(ks[7], (I, H), jnp.float32) * sc, 'shared_gate_w': jax.random.normal(ks[8], (1, H), jnp.float32) * sc}
    _L1_ffn_all = _L1_ffn_setup()
    _L1_ffn_in = {k: v for k, v in _L1_ffn_all.items() if k in ('gate_w', 'w_gate', 'w_up', 'w_down', 'sw_gate', 'sw_up', 'sw_down', 'shared_gate_w')}
    del _L1_ffn_all
    return {'x': x, 'ctx_1024': ctx_1024, 'itok_BxSx64_0_2047': itok_BxSx64_0_2047, 'L0_xattn_Wq': _L0_xattn_in['Wq'], 'L0_xattn_bq': _L0_xattn_in['bq'], 'L0_xattn_Wkv': _L0_xattn_in['Wkv'], 'L0_xattn_bkv': _L0_xattn_in['bkv'], 'L0_xattn_Wo': _L0_xattn_in['Wo'], 'L0_xattn_bo': _L0_xattn_in['bo'], 'L0_ffn_w1': _L0_ffn_in['w1'], 'L0_ffn_w2': _L0_ffn_in['w2'], 'L0_ffn_w3': _L0_ffn_in['w3'], 'L0_ffn_new_w1': _L0_ffn_in['new_w1'], 'L0_ffn_new_w2': _L0_ffn_in['new_w2'], 'L0_ffn_new_w3': _L0_ffn_in['new_w3'], 'L0_ffn_gate_weight': _L0_ffn_in['gate_weight'], 'L0_ffn_new_gate_weight': _L0_ffn_in['new_gate_weight'], 'L0_ffn_gate_bias': _L0_ffn_in['gate_bias'], 'L1_xattn_W_q': _L1_xattn_in['W_q'], 'L1_xattn_W_kv_down': _L1_xattn_in['W_kv_down'], 'L1_xattn_W_kv_up': _L1_xattn_in['W_kv_up'], 'L1_xattn_W_out': _L1_xattn_in['W_out'], 'L1_ffn_gate_w': _L1_ffn_in['gate_w'], 'L1_ffn_w_gate': _L1_ffn_in['w_gate'], 'L1_ffn_w_up': _L1_ffn_in['w_up'], 'L1_ffn_w_down': _L1_ffn_in['w_down'], 'L1_ffn_sw_gate': _L1_ffn_in['sw_gate'], 'L1_ffn_sw_up': _L1_ffn_in['sw_up'], 'L1_ffn_sw_down': _L1_ffn_in['sw_down'], 'L1_ffn_shared_gate_w': _L1_ffn_in['shared_gate_w']}

def reference(x, ctx_1024, itok_BxSx64_0_2047, L0_xattn_Wq, L0_xattn_bq, L0_xattn_Wkv, L0_xattn_bkv, L0_xattn_Wo, L0_xattn_bo, L0_ffn_w1, L0_ffn_w2, L0_ffn_w3, L0_ffn_new_w1, L0_ffn_new_w2, L0_ffn_new_w3, L0_ffn_gate_weight, L0_ffn_new_gate_weight, L0_ffn_gate_bias, L1_xattn_W_q, L1_xattn_W_kv_down, L1_xattn_W_kv_up, L1_xattn_W_out, L1_ffn_gate_w, L1_ffn_w_gate, L1_ffn_w_up, L1_ffn_w_down, L1_ffn_sw_gate, L1_ffn_sw_up, L1_ffn_sw_down, L1_ffn_shared_gate_w):
    import jax
    import jax.numpy as jnp

    def _L0_xattn_ref(x, y, Wq, bq, Wkv, bkv, Wo, bo):
        import jax, jax.numpy as jnp
        import numpy as np
        DIM = 128
        NUM_HEADS = 16
        HEAD_DIM = DIM // NUM_HEADS
        B, N, C = x.shape
        B2, N2, _ = y.shape
        H, hd = (NUM_HEADS, HEAD_DIM)
        scaling = hd ** (-0.5)
        q = (x @ Wq + bq).reshape(B, N, H, hd).transpose(0, 2, 1, 3)
        kv = (y @ Wkv + bkv).reshape(B2, N2, 2, H, hd).transpose(0, 3, 2, 1, 4)
        k, v = (kv[:, :, 0], kv[:, :, 1])
        attn = jnp.einsum('bhnd,bhmd->bhnm', q * scaling, k)
        attn = jax.nn.softmax(attn, axis=-1)
        out = jnp.einsum('bhnm,bhmd->bhnd', attn, v)
        out = out.transpose(0, 2, 1, 3).reshape(B, N, C)
        return out @ Wo + bo

    def _L0_ffn_ref(x, w1, w2, w3, new_w1, new_w2, new_w3, gate_weight, new_gate_weight, gate_bias):
        import jax, jax.numpy as jnp
        import numpy as np
        TOP_K = 2
        ROUTE_SCALE = 1.0
        EPS = 1e-20
        bs, slen, dim = x.shape
        x_flat = x.reshape(-1, dim)
        ew1 = jnp.concatenate([w1, new_w1], axis=0)
        ew2 = jnp.concatenate([w2, new_w2], axis=0)
        ew3 = jnp.concatenate([w3, new_w3], axis=0)
        gate = jnp.concatenate([gate_weight, new_gate_weight], axis=0)
        e_orig = w1.shape[0]
        e_tot = gate.shape[0]
        bias = jnp.concatenate([jnp.zeros((e_orig,), x.dtype), gate_bias])
        scores = jax.nn.sigmoid((x_flat @ gate.T + bias).astype(jnp.float32))
        top_scores, selected = jax.lax.top_k(scores, TOP_K)
        top_scores = top_scores / (jnp.sum(top_scores, axis=-1, keepdims=True) + EPS)
        top_scores = top_scores * ROUTE_SCALE
        onehot = jax.nn.one_hot(selected, e_tot, dtype=jnp.float32)
        cw = jnp.einsum('tk,tke->te', top_scores, onehot)
        out = jnp.zeros_like(x_flat)
        for e in range(e_tot):
            h = jax.nn.silu(x_flat @ ew1[e].T) * (x_flat @ ew3[e].T)
            out = out + cw[:, e:e + 1] * (h @ ew2[e].T)
        return out.reshape(bs, slen, dim)

    def _L1_xattn_ref(x_q, x_kv, indices, W_q, W_kv_down, W_kv_up, W_out):
        import jax, jax.numpy as jnp
        import numpy as np
        B, NQ, NKV, K = (2, 128, 256, 64)
        D, H, LAT = (128, 16, 128)
        HD = D // H
        SCALE = 1.0 / np.sqrt(HD)
        b, nq, d = x_q.shape
        q = (x_q @ W_q.T).reshape(b, nq, H, HD)
        c_kv = x_kv @ W_kv_down.T
        c_sel = c_kv[jnp.arange(b)[:, None, None], indices]
        kv = (c_sel @ W_kv_up.T).reshape(b, nq, K, 2, H, HD)
        k = kv[:, :, :, 0]
        v = kv[:, :, :, 1]
        scores = jnp.einsum('bqhd,bqkhd->bqkh', q, k) * SCALE
        attn = jax.nn.softmax(scores, axis=2)
        out = jnp.einsum('bqkh,bqkhd->bqhd', attn, v).reshape(b, nq, d)
        return out @ W_out.T

    def _L1_ffn_ref(hidden_states, gate_w, w_gate, w_up, w_down, sw_gate, sw_up, sw_down, shared_gate_w):
        import jax, jax.numpy as jnp
        import numpy as np
        B, S, H = (2, 512, 128)
        E, K, I = (8, 2, 176)
        b, s, h = hidden_states.shape
        x = hidden_states.reshape(-1, h)
        logits = jnp.einsum('th,eh->te', x, gate_w)
        probs = jax.nn.softmax(logits.astype(jnp.float32), axis=-1)
        topk_w, topk_i = jax.lax.top_k(probs, K)
        topk_w = topk_w / jnp.sum(topk_w, axis=-1, keepdims=True)
        combine = jnp.sum(jax.nn.one_hot(topk_i, E, dtype=topk_w.dtype) * topk_w[..., None], axis=1)
        combine = combine.astype(x.dtype)
        g = jnp.einsum('th,ehi->eti', x, w_gate)
        u = jnp.einsum('th,ehi->eti', x, w_up)
        eo = jnp.einsum('eti,eih->eth', jax.nn.silu(g) * u, w_down)
        out = jnp.einsum('te,eth->th', combine, eo)
        sg = jax.nn.sigmoid(jnp.einsum('th,oh->to', x, shared_gate_w))
        so = jax.nn.silu(x @ sw_gate) * (x @ sw_up) @ sw_down
        out = out + sg * so
        return out.reshape(b, s, h)
    x = x + _L0_xattn_ref(_layernorm(x, axis=-1), ctx_1024, L0_xattn_Wq, L0_xattn_bq, L0_xattn_Wkv, L0_xattn_bkv, L0_xattn_Wo, L0_xattn_bo)
    x = x + _L0_ffn_ref(_layernorm(x, axis=-1), L0_ffn_w1, L0_ffn_w2, L0_ffn_w3, L0_ffn_new_w1, L0_ffn_new_w2, L0_ffn_new_w3, L0_ffn_gate_weight, L0_ffn_new_gate_weight, L0_ffn_gate_bias)
    x = x + _L1_xattn_ref(_layernorm(x, axis=-1), ctx_1024, itok_BxSx64_0_2047, L1_xattn_W_q, L1_xattn_W_kv_down, L1_xattn_W_kv_up, L1_xattn_W_out)
    x = x + _L1_ffn_ref(_layernorm(x, axis=-1), L1_ffn_gate_w, L1_ffn_w_gate, L1_ffn_w_up, L1_ffn_w_down, L1_ffn_sw_gate, L1_ffn_sw_up, L1_ffn_sw_down, L1_ffn_shared_gate_w)
    return x

_drawn_inputs = setup_inputs


def setup_inputs(seed=0):
    import zlib

    import numpy as np

    out = dict(_drawn_inputs(seed))
    spreads = {'L0_xattn_bq': (0.0, 0.41),
     'L0_xattn_bkv': (0.0, 0.1),
     'L0_xattn_bo': (0.0, 0.1),
     'L0_ffn_new_w2': (0.0, 0.8)}
    factors = {'L0_ffn_w1': 8.0,
     'L0_ffn_w2': 8.0,
     'L0_ffn_w3': 8.0,
     'L0_ffn_new_w1': 6.755,
     'L0_ffn_new_w3': 6.581,
     'L0_ffn_gate_weight': 7.892,
     'L0_ffn_new_gate_weight': 6.958,
     'L1_ffn_gate_w': 8.0,
     'L1_ffn_w_gate': 8.0,
     'L1_ffn_w_up': 8.0,
     'L1_ffn_w_down': 8.0,
     'L1_ffn_sw_gate': 8.0,
     'L1_ffn_sw_up': 8.0,
     'L1_ffn_sw_down': 8.0,
     'L1_ffn_shared_gate_w': 8.0}
    for name, (base, spread) in spreads.items():
        noise = np.random.default_rng([zlib.crc32(name.encode()), seed]).standard_normal(out[name].shape)
        drawn = base * np.exp(spread * noise) if base else spread * noise
        out[name] = jnp.asarray(drawn.astype(out[name].dtype))
    for name, factor in factors.items():
        out[name] = (out[name] * factor).astype(out[name].dtype)
    return out
```

```python
import concourse.bass as bass
from concourse import mybir
from contextlib import ExitStack

P = 128
NB, NQ, D = 8, 256, 128
NS = NQ // P
NK = 1601
NK1 = 256
NIDX = 64
H, HD = 16, 8
NP = H // 2
SLOT = 64
KC = (NK + P - 1) // P
KLAST = NK - (KC - 1) * P
KC1 = NK1 // P
V1 = HD + 1
QPART = (0, 1, 2, 0, 1, 0)
KPART = (0, 0, 0, 1, 1, 2)
NT = len(QPART)
KROWS = NT * HD
MROWS = KROWS + 3
SCALE = float(HD) ** -0.5
EPS = 1e-5
NE = 9
I0, I1 = 352, 176
F0, F1 = NE * I0, NE * I1
NC0, NC1 = (F0 + P - 1) // P, (F1 + P - 1) // P
NEG = -1e30
CWP = 32
CWR = 2 * CWP + NE
MMAX = 512


def rows(c, total):
    return min(P, total - c * P)


def build(nc, x, ctx_in, itok, Wq, bq, Wkv, bkv, Wo, bo, w1, w2, w3, nw1, nw2, nw3, gw, ngw, gb,
          Wq1, Wd1, Wu1, Wout1, gw1, wg, wu, wd, swg, swu, swd, sgw, out):
    f32, bf16, i32, u32 = mybir.dt.float32, mybir.dt.bfloat16, mybir.dt.int32, mybir.dt.uint32
    ALU, ACT, AX = mybir.AluOpType, mybir.ActivationFunctionType, mybir.AxisListType.X
    k_parts = nc.dram_tensor("k_parts", [3, P, NK], bf16, kind="Internal").ap()
    k1_parts = nc.dram_tensor("k1_parts", [3, P, NK1], bf16, kind="Internal").ap()

    with ExitStack() as es:
        def sb(name, shape, dt=f32):
            return es.enter_context(nc.sbuf_tensor(name, shape, dt))

        def psum(name, width):
            return es.enter_context(nc.psum_tensor(name, [P, width], f32))

        wq_sb, wkv_sb, wo_sb = sb("wq_sb", [P, D]), sb("wkv_sb", [P, 2 * D]), sb("wo_sb", [P, D])
        wq1T, wd1T, wu1T, wo1T = sb("wq1T", [P, D]), sb("wd1T", [P, D]), sb("wu1T", [P, 2 * D]), sb("wo1T", [P, D])
        bqs = sb("bqs", [P, D])
        bv_bc, bo_bc = sb("bv_bc", [P, D]), sb("bo_bc", [P, D])
        bk_col = sb("bk_col", [P, 1])
        gb_bc = sb("gb_bc", [P, NE])
        gT = [sb("gT0", [P, NE]), sb("gT1", [P, NE])]
        gT_nat = [sb("g_nat0", [NE, P]), sb("g_nat1", [NE, P])]
        w1T, w3T, w2T = sb("w1T", [P, F0]), sb("w3T", [P, F0]), sb("w2T", [P, NC0, D])
        wg_sb, wu_sb, wd_sb = sb("wg_sb", [P, F1]), sb("wu_sb", [P, F1]), sb("wd_sb", [P, NC1, D])
        sel = [sb("sel0", [CWR, F0], bf16), sb("sel1", [CWR, F1], bf16)]
        sq_nat = sb("sq_nat", [P, 5, P])
        ident, identb = sb("ident", [P, P]), sb("identb", [P, P], bf16)
        iota_i, iota_f = sb("iota_i", [P, P], i32), sb("iota_f", [P, P])
        neg_half = sb("neg_half", [P, NS, 1])
        xs = [sb(f"x{k}", [P, NS, D]) for k in range(5)]
        x0b = sb("x0b", [P, NS, D])
        xn, xnT = sb("xn", [P, NS, D]), sb("xnT", [P, NQ])
        stats, mv = sb("stats", [P, NS, 6]), sb("mv", [P, NS, 2])
        veps, rstd = sb("veps", [P, NS, 1]), sb("rstd", [P, NS, 1])
        big = sb("big", [P, 8192])
        onehot = big[:, :].bitcast(bf16).rearrange("p (q r) -> p q r", r=P)
        kf, kres = big[:, 0:NK], big[:, 1602:1602 + NK]
        kpart = [big[:, 3204 + 802 * t:3204 + 802 * (t + 1)].bitcast(bf16)[:, 0:NK] for t in range(3)]
        w1_nat = big[:, 0:NC0 * P].rearrange("p (c d) -> p c d", d=P)
        w3_nat = big[:, 4096:4096 + NC0 * P].rearrange("p (c d) -> p c d", d=P)
        kst = sb("kst", [P, NP, NK + 1], bf16)
        w2_nat = kst[:, :, :].rearrange("p a k -> p (a k)").bitcast(f32)[:, 0:F0]
        k1st = sb("k1st", [P, NP, NK1], bf16)
        vaug, v1aug = sb("vaug", [P, KC, H, V1]), sb("v1aug", [P, KC1, H, V1])
        ctx_sb, ctxT = sb("ctx_sb", [P, KC, D]), sb("ctxT", [P, NK])
        cT = sb("cT", [P, NK1])
        kf1, kres1 = sb("kf1", [P, NK1]), sb("kres1", [P, NK1])
        kpart1 = [sb(f"kpart1_{t}", [P, NK1], bf16)[:, :] for t in range(3)]
        qs, qres = sb("qs", [P, NS, H, HD]), sb("qres", [P, NS, H, HD])
        qst = sb("qst", [P, NS, H, SLOT], bf16)
        qa = sb("qa", [P, NP, NS, P], bf16)
        qb = sb("qb", [P, 2, NQ], bf16)
        mx = sb("mx", [P, 2, NS, 2, 2])
        mx1 = sb("mx1", [P, NP, 2, NS])
        nm, nmr = sb("nm", [P, 2, NS, 2]), sb("nmr", [P, NS, 2])
        probs = sb("probs", [P, 4, 512])
        att, attT = sb("att", [P, NS, H, HD]), sb("attT", [P, NQ])
        rec = sb("rec", [P, NS, H])
        idx_i, idx_f = sb("idx_i", [P, NS, NIDX], i32), sb("idx_f", [P, NS, NIDX])
        idx_hi, idx_lo = sb("idx_hi", [P, P]), sb("idx_lo", [P, P])
        idx_c = sb("idx_c", [P, P, 2], bf16)
        cntT = sb("cntT", [P, KC1, NQ])
        maskT, maskq = sb("maskT", [P, KC1, NQ], bf16), sb("maskq", [P, NS, NK1], bf16)
        lz, le, ls = sb("lz", [P, NS, NE]), sb("le", [P, NS, NE]), sb("ls", [P, NS, NE])
        lneg, lsum, lrec = sb("lneg", [P, NS]), sb("lsum", [P, NS]), sb("lrec", [P, NS])
        top, topi, topf = sb("top", [P, NS, 8]), sb("topi", [P, NS, 8], u32), sb("topf", [P, NS, 8])
        wden, wrec, wtop = sb("wden", [P, NS]), sb("wrec", [P, NS]), sb("wtop", [P, NS, 2])
        cw, cw2, cwr = sb("cw", [P, NS, NE]), sb("cw2", [P, NS, NE]), sb("cwr", [P, NS, NE])
        cwp = sb("cwp", [P, NS, CWR], bf16)
        cwT = sb("cwT", [CWR, NQ], bf16)
        th, gt, hu = (big[:, 5632 + 768 * k:5632 + 768 * (k + 1)].rearrange("p (n q) -> p n q", q=NQ) for k in range(3))
        hid = sb("hid", [P, 4, NQ])
        a0, a1 = psum("a0", 1024), psum("a1", 1024)
        bs = [psum(f"b{k}", 512) for k in range(3)]
        ob = psum("ob", 512)
        quarter = [a0[:, 0:512], a0[:, 512:1024], a1[:, 0:512], a1[:, 512:1024]]
        gu_bank = quarter[0:3]
        cb_bank = bs[0:2]
        cnt_bank = [bs[1], ob]
        side_bank = [bs[2][:, :], quarter[3]]
        bsb = [b[:, :].bitcast(bf16) for b in bs]
        pv_out = ob[:, 0:NS * H * V1].rearrange("p (s h d) -> p s h d", s=NS, h=H)

        first_sem = [None]

        def sem(name):
            s = es.enter_context(nc.semaphore(name))
            if first_sem[0] is None:
                first_sem[0] = s.num
            last_sem[0] = s.num
            return s
        last_sem = [None]

        ctx_in_s, x_in, idx_in, kst_in, k1st_in = (sem(n) for n in ("ctx_in", "x_in", "idx_in", "kst_in", "k1st_in"))
        kw_done, kw1_done = sem("kw_done"), sem("kw1_done")
        mv_ready, rstd_ready, ln_ready, xT_psum, xT_ready = (sem(n) for n in ("mv_ready", "rstd_ready", "ln_ready", "xT_psum", "xT_ready"))
        q_psum, qst_ready, qst_read = sem("q_psum"), sem("qst_ready"), sem("qst_read")
        at_ready, atT_psum, atT_ready, o_psum, x_ready = (sem(n) for n in ("at_ready", "atT_psum", "atT_ready", "o_psum", "x_ready"))
        half_ready, half_read, nm_ready, m_ready = sem("half_ready"), sem("half_read"), sem("nm_ready"), sem("m_ready")
        b_ready, b_read, pv_done, att_done = sem("b_ready"), sem("b_read"), sem("pv_done"), sem("att_done")
        pair_ready, pair_read, m1_ready = sem("pair_ready"), sem("pair_read"), sem("m1_ready")
        b1_ready, b1_read, pv1_done, mulv, mulp = sem("b1_ready"), sem("b1_read"), sem("pv1_done"), sem("mulv"), sem("mulp")
        idxf_ready, idxT_psum, idxlo_ready, onehot_ready, cnt_psum, cnt_ready, maskq_psum, maskq_ready = (
            sem(n) for n in ("idxf_ready", "idxT_psum", "idxlo_ready", "onehot_ready", "cnt_psum", "cnt_ready", "maskq_psum", "maskq_ready"))
        gate_psum, lz_ready, le_ready, cwp_ready, cwT_psum, cwT_ready = (
            [sem(f"{n}{k}") for k in range(2)] for n in ("gate_psum", "lz_ready", "le_ready", "cwp_ready", "cwT_psum", "cwT_ready"))
        gu_ready, th_ready, gt_done, hu_done, cb_ready, hid_ready, down_done = (
            [sem(f"{n}{k}") for k in range(2)] for n in ("gu_ready", "th_ready", "gt_done", "hu_done", "cb_ready", "hid_ready", "down_done"))
        side_psum, side_act, side_dve = sem("side_psum"), sem("side_act"), sem("side_dve")
        side1_psum, side1_act = sem("side1_psum"), sem("side1_act")
        kp_ready, kres_ready, kp1_ready, kres1_ready = sem("kp_ready"), sem("kres_ready"), sem("kp1_ready"), sem("kres1_ready")
        dve_step, pool_step, act_step = sem("dve_step"), sem("pool_step"), sem("act_step")
        w_in, w2_in, stage_psum, stage_dve, stage_act, const_ready, pre_dve, kst_one = (
            sem(n) for n in ("w_in", "w2_in", "stage_psum", "stage_dve", "stage_act", "const_ready", "pre_dve", "kst_one"))
        xo_free = sem("xo_free")
        met = sem("met")
        round_sems = range(first_sem[0], last_sem[0] + 1)
        go = [sem(f"go{k}") for k in range(4)]
        out_stored = sem("out_stored")

        def meet(eng, k):
            eng.drain().then_inc(met, 1)
            eng.wait_ge(go[k], 1)
            eng.sem_clear(go[k])

        class Steps:

            def __init__(self, eng, s):
                self.eng, self.s, self.n = eng, s, 0

            def do(self, ins):
                self.n += 1
                ins.then_inc(self.s, 1)

            def wait(self):
                self.eng.wait_ge(self.s, self.n)

            def link(self, ins):
                self.do(ins)
                self.wait()

        block = es.enter_context(nc.Block())

        w1b = [(w1T, w1_nat), (w3T, w3_nat)]
        stages = []
        for dst, nat in w1b:
            for c in range(0, NC0, 4):
                src = [nat[0:rows(k, F0), k, :] for k in range(c, min(c + 4, NC0))]
                width = sum(rows(k, F0) for k in range(c, min(c + 4, NC0)))
                stages.append((dst[:, c * P:c * P + width], src))
        for c in range(0, NC0 - 1, 4):
            stages.append((w2T[:, c:c + 4, :].rearrange("p c d -> p (c d)"), [w2_nat[:, k * P:(k + 1) * P] for k in range(c, c + 4)]))
        stages.append((w2T[0:rows(NC0 - 1, F0), NC0 - 1, :], [w2_nat[:, (NC0 - 1) * P:F0]]))
        for dst, k in ((wq1T, 0), (wd1T, 1), (wo1T, 4)):
            stages.append((dst[:, :], [sq_nat[:, k, :]]))
        stages.append((wu1T[:, :], [sq_nat[:, 2, :], sq_nat[:, 3, :]]))
        for k in range(2):
            stages.append((gT[k][:, :], [gT_nat[k][:, :]]))

        @block.sync
        def _(sp):
            def load_x(b):
                sp.dma_start(xs[0][:, :, :], x[b].rearrange("a (s p) d -> p (a s) d", p=P)).then_inc(x_in, 16)
                sp.dma_start(idx_i[:, :, :], itok[b].rearrange("a (s p) k -> p (a s) k", p=P)).then_inc(idx_in, 16)

            def load_ctx(b):
                sp.dma_start(ctx_sb[:, 0:KC - 1, :],
                             ctx_in[b, 0:(KC - 1) * P, :].rearrange("a (c p) d -> p (a c) d", p=P)).then_inc(ctx_in_s, 16)
                sp.dma_start(ctx_sb[0:KLAST, KC - 1, :],
                             ctx_in[b, (KC - 1) * P:NK, :].rearrange("a k d -> (a k) d")).then_inc(ctx_in_s, 16)

            def spread(parts, scratch, dst, done, filled, ready):
                for t in range(3):
                    sp.wait_ge(ready, t + 1)
                    sp.dma_start(scratch[t], parts[t]).then_inc(done, 16)
                    sp.wait_ge(done, 16 * (t + 1))
                    src = scratch[t].rearrange("(a h d) k -> h d a k", h=2, d=HD)
                    for hh in range(2):
                        for term in range(NT):
                            if KPART[term] == t:
                                r = SLOT * hh + HD * term
                                sp.dma_start(dst[r:r + HD, :, 0:src.shape[3]], src[hh]).then_inc(filled, 16)

            sp.dma_start(w1_nat[:, 0:22, :], w1.rearrange("e i d -> (e i) d").rearrange("(c p) d -> p c d", p=P)).then_inc(w_in, 16)
            sp.dma_start(w1_nat[:, 22:24, :], nw1[0, 0:256, :].rearrange("(c p) d -> p c d", p=P)).then_inc(w_in, 16)
            sp.dma_start(w1_nat[0:96, 24, :], nw1[0, 256:I0, :]).then_inc(w_in, 16)
            sp.dma_start(w3_nat[:, 0:22, :], w3.rearrange("e i d -> (e i) d").rearrange("(c p) d -> p c d", p=P)).then_inc(w_in, 16)
            sp.dma_start(w3_nat[:, 22:24, :], nw3[0, 0:256, :].rearrange("(c p) d -> p c d", p=P)).then_inc(w_in, 16)
            sp.dma_start(w3_nat[0:96, 24, :], nw3[0, 256:I0, :]).then_inc(w_in, 16)
            sp.dma_start(w2_nat[:, 0:8 * I0].rearrange("p (e i) -> p e i", i=I0), w2.rearrange("e d i -> d e i")).then_inc(w_in, 16)
            sp.dma_start(w2_nat[:, 8 * I0:F0], nw2[0]).then_inc(w_in, 16)
            sp.dma_start(sq_nat[:, 0, :], Wq1).then_inc(w_in, 16)
            sp.dma_start(sq_nat[:, 1, :], Wd1).then_inc(w_in, 16)
            sp.dma_start(sq_nat[:, 2:4, :], Wu1.rearrange("(c p) d -> p c d", p=P)).then_inc(w_in, 16)
            sp.dma_start(sq_nat[:, 4, :], Wout1).then_inc(w_in, 16)
            for k, (a, b) in enumerate(((gw, ngw), (gw1, sgw))):
                sp.dma_start(gT_nat[k][0:8, :], a).then_inc(w_in, 16)
                sp.dma_start(gT_nat[k][8:9, :], b).then_inc(w_in, 16)
            load_ctx(slice(0, 1))
            sp.dma_start(wkv_sb[:, :], Wkv).then_inc(w2_in, 16)
            sp.dma_start(bk_col[:, :], bkv[0:D].rearrange("(p a) -> p a", a=1)).then_inc(w2_in, 16)
            sp.dma_start(bv_bc[:, :], bkv[D:2 * D].partition_broadcast(P)).then_inc(w2_in, 16)
            sp.dma_start(bo_bc[:, :], bo.partition_broadcast(P)).then_inc(w2_in, 16)
            sp.dma_start(bqs[:, :], bq.partition_broadcast(P)).then_inc(w2_in, 16)
            sp.dma_start(gb_bc[:, 8:9], gb.partition_broadcast(P)).then_inc(w2_in, 16)
            sp.dma_start(wq_sb[:, :], Wq).then_inc(w2_in, 16)
            sp.dma_start(wo_sb[:, :], Wo).then_inc(w2_in, 16)
            load_x(slice(0, 1))
            for dst, a, b in ((wg_sb, wg, swg), (wu_sb, wu, swu)):
                sp.dma_start(dst[:, 0:8 * I1].rearrange("p (e i) -> p e i", i=I1), a.rearrange("e d i -> d e i")).then_inc(w2_in, 16)
                sp.dma_start(dst[:, 8 * I1:F1], b).then_inc(w2_in, 16)
            sp.dma_start(wd_sb[:, 0:11, :], wd.rearrange("e i d -> (e i) d").rearrange("(c p) d -> p c d", p=P)).then_inc(w2_in, 16)
            sp.dma_start(wd_sb[:, 11, :], swd[0:P, :]).then_inc(w2_in, 16)
            sp.dma_start(wd_sb[0:I1 - P, 12, :], swd[P:I1, :]).then_inc(w2_in, 16)
            sp.wait_ge(kst_one, 1)
            spread(kpart, k_parts, kst, kw_done, kst_in, kp_ready)
            spread(kpart1, k1_parts, k1st, kw1_done, k1st_in, kp1_ready)

            def close():
                sp.wait_ge(kst_in, 16 * 2 * NT)
                sp.wait_ge(k1st_in, 16 * 2 * NT)
                sp.wait_ge(x_in, 16)
                sp.wait_ge(idx_in, 16)
                sp.wait_ge(ctx_in_s, 32)
                sp.wait_ge(met, 4)
                sp.sem_clear(round_sems)
                for g in go:
                    sp.sem_inc(g, 1)

            sp.wait_ge(w2_in, 16 * 15)
            close()
            sp.sem_inc(out_stored, 16)
            with sp.Fori(0, NB) as i:
                nxt = bass.ds((i + 1) % NB, 1)
                load_ctx(nxt)
                sp.wait_ge(x_ready, 1)
                sp.wait_ge(cnt_psum, 1)
                load_x(nxt)
                sp.wait_ge(out_stored, 16)
                sp.sem_clear(out_stored)
                sp.sem_inc(xo_free, 1)
                sp.wait_ge(att_done, 1)
                spread(kpart, k_parts, kst, kw_done, kst_in, kp_ready)
                sp.wait_ge(att_done, 2)
                spread(kpart1, k1_parts, k1st, kw1_done, k1st_in, kp1_ready)
                sp.wait_ge(x_ready, 4)
                sp.dma_start(out[bass.ds(i, 1)].rearrange("a (s p) d -> p (a s) d", p=P), xs[4][:, :, :]).then_inc(out_stored, 16)
                close()
            sp.wait_ge(out_stored, 16)

        NJ = (KC + 1) // 2
        NH0 = NP * 2 * NS * 2

        def ev_q(p):
            return 2 + (1 + 2 * NJ) * p

        def ev_e(x):
            p, r = divmod(x, 2 * NJ)
            return ev_q(p) + 1 + r

        NX = NP * 2 * NJ
        NX1 = H

        def ev1_q(p):
            return 2 + 3 * p

        def ev1_e(x):
            return ev1_q(x // 2) + 1 + x % 2

        def chunks(x):
            j = x % NJ
            return [(c, min(P, NK - c * P)) for c in range(2 * j, min(2 * j + 2, KC))]

        @block.tensor
        def _(pe):
            def norm_T(k):
                pe.wait_ge(ln_ready, k + 1)
                for s in range(NS):
                    m = pe.transpose(quarter[0][:, s * P:(s + 1) * P], xn[:, s, :], ident[:, :])
                m.then_inc(xT_psum, 1)
                pe.wait_ge(xT_ready, k + 1)

            def query_parts(layer, w):
                for s in range(NS):
                    m = pe.matmul(quarter[2][:, s * P:(s + 1) * P], xnT[:, s * P:(s + 1) * P], w, start=True, stop=True)
                m.then_inc(q_psum, 1)
                pe.wait_ge(qst_ready, layer + 1)
                for half in range(2):
                    for n in range(8):
                        p, s = divmod(half * 8 + n, NS)
                        m = pe.transpose(bsb[half][:, n * P:(n + 1) * P],
                                         qst[:, s, 2 * p:2 * p + 2, :].rearrange("p h r -> p (h r)"), identb[:, :])
                    m.then_inc((b_ready, b1_ready)[layer], 1)

            def pair_queries(p, e, ready, b_rdy, b_rd):
                pe.wait_ge(ready, p + 1)
                if e >= 3:
                    pe.wait_ge(b_rd, e - 2)
                for s in range(NS):
                    m = pe.transpose(bsb[e % 3][:, s * P:(s + 1) * P],
                                     qst[:, s, 2 * p:2 * p + 2, :].rearrange("p h r -> p (h r)"), identb[:, :])
                m.then_inc(b_rdy, 1)

            def attend_out(layer, w):
                pe.wait_ge(at_ready, layer + 1)
                for s in range(NS):
                    m = pe.transpose(quarter[0][:, s * P:(s + 1) * P], att[:, s, :, :].rearrange("p h d -> p (h d)"), ident[:, :])
                m.then_inc(atT_psum, 1)
                pe.wait_ge(atT_ready, layer + 1)
                for s in range(NS):
                    m = pe.matmul(quarter[2][:, s * P:(s + 1) * P], attT[:, s * P:(s + 1) * P], w, start=True, stop=True)
                m.then_inc(o_psum, 1)

            def max_half(k):
                u, half = divmod(k, 2)
                p, r = divmod(u, 4)
                hh, s = divmod(r, 2)
                o = SLOT * hh
                if k == 0:
                    pe.wait_ge(b_read, 1)
                if k == 32:
                    pe.wait_ge(b_read, 2)
                if k >= 2:
                    pe.wait_ge(half_read, k - 1)
                bank = (a0, a1)[half]
                for k0 in range(0, 1024, MMAX):
                    n = min(MMAX, NK - half * 1024 - k0)
                    m = pe.matmul(bank[:, k0:k0 + n], qa[o:o + KROWS, p, s, :],
                                  kst[o:o + KROWS, p, half * 1024 + k0:half * 1024 + k0 + n], start=True, stop=True)
                m.then_inc(half_ready, 1)

            def scores(x):
                e = ev_e(x)
                p, r = divmod(x, 2 * NJ)
                o = SLOT * (r // NJ)
                if x % (2 * NJ) == 0:
                    pe.wait_ge(b_read, ev_q(p) + 1)
                if e >= 3:
                    pe.wait_ge(b_read, e - 2)
                for n, (c, kn) in enumerate(chunks(x)):
                    m = pe.matmul(bs[e % 3][0:kn, n * NQ:(n + 1) * NQ], kst[o:o + MROWS, p, c * P:c * P + kn],
                                  qb[o:o + MROWS, p % 2, :], start=True, stop=True)
                m.then_inc(b_ready, 1)

            def weigh(x):
                pe.wait_ge(b_read, ev_e(x) + 1)
                p, r = divmod(x, 2 * NJ)
                h = 2 * p + r // NJ
                for s in range(NS):
                    for n, (c, kn) in enumerate(chunks(x)):
                        m = pe.matmul(pv_out[:, s, h, :], probs[0:kn, x % 4, n * NQ + s * P:n * NQ + (s + 1) * P],
                                      vaug[0:kn, c, h, :], start=(x == 0 and s == 0 and n == 0), stop=(c == KC - 1),
                                      skip_group_check=True)
                m.then_inc(pv_done, 1)

            def attention0():
                done = [0]

                def halves(upto):
                    while done[0] < min(upto, NH0):
                        max_half(done[0])
                        done[0] += 1
                halves(10)
                for x in range(NX + 2):
                    if x < NX:
                        p, r = divmod(x, 2 * NJ)
                        if r == 0:
                            pair_queries(p, ev_q(p), m_ready, b_ready, b_read)
                        scores(x)
                        halves(10 + (x + 1) * 8 // (2 * NJ))
                    if x >= 2:
                        weigh(x - 2)
                pe.drain().then_inc(att_done, 1)

            def count():
                pe.wait_ge(onehot_ready, 8)
                for q in range(P):
                    for s in range(NS):
                        cnt = cnt_bank[s][:, 0:P * KC1].rearrange("p (q c) -> p q c", c=KC1)
                        m = pe.matmul(cnt[:, q, :], onehot[s * NIDX:(s + 1) * NIDX, q, :], idx_c[s * NIDX:(s + 1) * NIDX, q, :],
                                      start=True, stop=True)
                m.then_inc(cnt_psum, 1)

            def attention1():
                pe.wait_ge(cnt_ready, 1)
                for n in range(NS * KC1):
                    s, c = divmod(n, KC1)
                    m = pe.transpose(ob[:, :].bitcast(bf16)[:, n * P:(n + 1) * P], maskT[:, c, s * P:(s + 1) * P], identb[:, :])
                m.then_inc(maskq_psum, 1)
                pe.wait_ge(maskq_ready, 1)
                pe.wait_ge(b1_read, 2)

                def max_pair(p):
                    bank = (a0, a1)[p % 2]
                    if p >= 2:
                        pe.wait_ge(pair_read, p - 1)
                    for hh in range(2):
                        o = SLOT * hh
                        cols = bank[:, hh * 512:(hh + 1) * 512].rearrange("p (s k) -> p s k", s=NS)
                        for s in range(NS):
                            pe.matmul(cols[:, s, :], identb[:, :], maskq[:, s, :], start=True, stop=False)
                            m = pe.matmul(cols[:, s, :], qa[o:o + KROWS, p, s, :], k1st[o:o + KROWS, p, :], start=False, stop=True)
                    m.then_inc(pair_ready, 1)

                def scores1(x):
                    e = ev1_e(x)
                    p, hh = divmod(x, 2)
                    o = SLOT * hh
                    if hh == 0:
                        pe.wait_ge(b1_read, ev1_q(p) + 1)
                    pe.wait_ge(b1_read, e - 2)
                    bank = bs[e % 3]
                    for c in range(KC1):
                        pe.matmul(bank[:, c * NQ:(c + 1) * NQ], identb[:, :], maskT[:, c, :], start=True, stop=False)
                        m = pe.matmul(bank[:, c * NQ:(c + 1) * NQ], k1st[o:o + MROWS, p, c * P:(c + 1) * P],
                                      qb[o:o + MROWS, p % 2, :], start=False, stop=True)
                    m.then_inc(b1_ready, 1)

                def weigh1(x):
                    pe.wait_ge((mulv, mulp)[x % 2], x // 2 + 1)
                    for s in range(NS):
                        for c in range(KC1):
                            m = pe.matmul(pv_out[:, s, x, :], probs[:, x % 4, c * NQ + s * P:c * NQ + (s + 1) * P],
                                          v1aug[:, c, x, :], start=(x == 0 and s == 0 and c == 0), stop=(c == KC1 - 1),
                                          skip_group_check=True)
                    m.then_inc(pv1_done, 1)

                max_pair(0)
                for p in range(NP):
                    if p + 1 < NP:
                        max_pair(p + 1)
                    pair_queries(p, ev1_q(p), m1_ready, b1_ready, b1_read)
                    for x in (2 * p, 2 * p + 1):
                        scores1(x)
                        if x >= 2:
                            weigh1(x - 2)
                weigh1(NX1 - 2)
                weigh1(NX1 - 1)
                pe.drain().then_inc(att_done, 1)

            def next_keys():
                pe.wait_ge(ctx_in_s, 32)
                for g in range(4):
                    if g >= 2:
                        pe.wait_ge(side_act, g - 1)
                    for c in range(4 * g, min(4 * g + 4, KC)):
                        kn = min(P, NK - c * P)
                        m = pe.transpose(side_bank[g % 2][:, (c % 4) * P:(c % 4) * P + kn], ctx_sb[0:kn, c, :], ident[0:kn, 0:kn])
                    m.then_inc(side_psum, 1)
                for g in range(4):
                    pe.wait_ge(side_act, g + 3)
                    n = min(MMAX, NK - g * MMAX)
                    pe.matmul(side_bank[g % 2][:, 0:n], wkv_sb[:, 0:D], ctxT[:, g * MMAX:g * MMAX + n],
                              start=True, stop=True).then_inc(side_psum, 1)
                for g in range(4):
                    if g < 2:
                        pe.wait_ge(side_act, g + 7)
                    else:
                        pe.wait_ge(side_dve, g - 1)
                    for c in range(4 * g, min(4 * g + 4, KC)):
                        kn = min(P, NK - c * P)
                        m = pe.matmul(side_bank[g % 2][0:kn, (c % 4) * P:(c % 4 + 1) * P], ctxT[:, c * P:c * P + kn], wkv_sb[:, D:2 * D],
                                      start=True, stop=True)
                    m.then_inc(side_psum, 1)

            def next_keys1():
                pe.wait_ge(side_dve, 4)
                pe.matmul(side_bank[0][:, 0:NK1], wd1T[:, :], ctxT[:, 0:NK1], start=True, stop=True).then_inc(side1_psum, 1)
                pe.wait_ge(side1_act, 1)
                pe.matmul(side_bank[1][:, 0:NK1], wu1T[:, 0:D], cT[:, :], start=True, stop=True).then_inc(side1_psum, 1)
                for c in range(KC1):
                    m = pe.matmul(side_bank[0][:, c * P:(c + 1) * P], cT[:, c * P:(c + 1) * P], wu1T[:, D:2 * D], start=True, stop=True)
                m.then_inc(side1_psum, 1)

            def experts(l):
                wga, wua, wda, nch, ftot = ((w1T, w3T, w2T, NC0, F0), (wg_sb, wu_sb, wd_sb, NC1, F1))[l]
                lag = 3
                for s in range(NS):
                    m = pe.matmul(bs[0][:, s * NE:(s + 1) * NE], xnT[:, s * P:(s + 1) * P], gT[l][:, :], start=True, stop=True)
                m.then_inc(gate_psum[l], 1)
                if l == 0:
                    count()
                    next_keys()
                else:
                    next_keys1()

                def gate_up(c):
                    if c >= 3:
                        pe.wait_ge(hu_done[l], c - 2)
                    n = rows(c, ftot)
                    pe.matmul(gu_bank[c % 3][0:n, 0:NQ], wga[:, c * P:c * P + n], xnT[:, :], start=True, stop=True)
                    pe.matmul(gu_bank[c % 3][0:n, NQ:2 * NQ], wua[:, c * P:c * P + n], xnT[:, :], start=True, stop=True).then_inc(gu_ready[l], 1)

                def weights(c):
                    if c >= 2:
                        pe.wait_ge(hid_ready[l], c - 1)
                    n = rows(c, ftot)
                    pe.matmul(cb_bank[c % 2][0:n, 0:NQ], sel[l][:, c * P:c * P + n], cwT[:, :], start=True, stop=True).then_inc(cb_ready[l], 1)

                def down(c):
                    pe.wait_ge(hid_ready[l], c + 1)
                    n = rows(c, ftot)
                    for s in range(NS):
                        m = pe.matmul(ob[:, s * P:(s + 1) * P], hid[0:n, c % 4, s * P:(s + 1) * P], wda[0:n, c, :],
                                      start=(c == 0 and s == 0), stop=(c == nch - 1), skip_group_check=True)
                    m.then_inc(down_done[l], 1)

                gate_up(0)
                gate_up(1)
                pe.wait_ge(cwp_ready[l], 1)
                for s in range(NS):
                    m = pe.transpose(bsb[1][0:CWR, s * P:(s + 1) * P], cwp[:, s, :], identb[:, :])
                m.then_inc(cwT_psum[l], 1)
                gate_up(2)
                pe.wait_ge(cwT_ready[l], 1)
                weights(0)
                weights(1)
                for c in range(3, nch + lag):
                    if c < nch:
                        gate_up(c)
                    if 2 <= c - 1 < nch:
                        weights(c - 1)
                    down(c - lag)

            pe.wait_ge(const_ready, 2)
            pe.wait_ge(w_in, 16 * 16)
            for g, (dst, srcs) in enumerate(stages):
                if g >= 4:
                    pe.wait_ge((stage_dve, stage_act)[g % 2], (g - 4) // 2 + 1)
                o = 0
                for src in srcs:
                    kp, n = src.shape
                    m = pe.transpose(quarter[g % 4][0:n, o:o + kp], src, ident[0:kp, 0:kp])
                    o += kp
                m.then_inc(stage_psum, 1)
            for k in range(2):
                pe.wait_ge((stage_dve, stage_act)[k], (len(stages) + 1 - k) // 2)
            pe.wait_ge(w2_in, 16 * 15)
            next_keys()
            next_keys1()
            meet(pe, 0)
            with pe.Fori(0, NB):
                norm_T(0)
                query_parts(0, wq_sb[:, :])
                pe.wait_ge(idxf_ready, 1)
                pe.transpose(quarter[1][:, 0:P], idx_f[:, :, :].rearrange("p s k -> p (s k)"), ident[:, :]).then_inc(idxT_psum, 1)
                pe.wait_ge(idxlo_ready, 1)
                attention0()
                attend_out(0, wo_sb[:, :])
                norm_T(1)
                experts(0)
                norm_T(2)
                query_parts(1, wq1T[:, :])
                attention1()
                attend_out(1, wo1T[:, :])
                norm_T(3)
                experts(1)
                meet(pe, 0)

        @block.scalar
        def _(act):
            steps = Steps(act, act_step)

            def copy(o, i):
                return act.activation(o, i, ACT.Copy)

            def all_queries(b_rdy, b_rd):
                for half in range(2):
                    act.wait_ge(b_rdy, half + 1)
                    copy(qa[:, 4 * half:4 * half + 4, :, :].rearrange("p a s q -> p (a s q)"), bsb[half][:, :]).then_inc(b_rd, 1)

            def pair_queries(p, e, b_rdy, b_rd):
                act.wait_ge(b_rdy, e + 1)
                copy(qb[:, p % 2, :], bsb[e % 3][:, 0:NQ]).then_inc(b_rd, 1)

            def attention0():
                all_queries(b_ready, b_read)
                for x in range(NX):
                    p, r = divmod(x, 2 * NJ)
                    if r == 0:
                        pair_queries(p, ev_q(p), b_ready, b_read)
                    e = ev_e(x)
                    act.wait_ge(b_ready, e + 1)
                    if x >= 4:
                        act.wait_ge(pv_done, x - 3)
                    ch = chunks(x)
                    kn, n = ch[0][1], len(ch) * NQ
                    act.activation(probs[0:kn, x % 4, 0:n], bs[e % 3][0:kn, 0:n], ACT.Exp).then_inc(b_read, 1)

            def attention1():
                all_queries(b1_ready, b1_read)
                for x in range(NX1):
                    p, hh = divmod(x, 2)
                    if hh == 0:
                        pair_queries(p, ev1_q(p), b1_ready, b1_read)
                    e = ev1_e(x)
                    act.wait_ge(b1_ready, e + 1)
                    if x >= 4:
                        act.wait_ge(pv1_done, x - 3)
                    act.activation(probs[:, x % 4, :], bs[e % 3][:, :], ACT.Exp).then_inc(b1_read, 1)

            def next_keys():
                for g in range(4):
                    n = min(MMAX, NK - g * MMAX)
                    act.wait_ge(side_psum, g + 1)
                    copy(ctxT[:, g * MMAX:g * MMAX + n], side_bank[g % 2][:, 0:n]).then_inc(side_act, 1)
                for g in range(4):
                    n = min(MMAX, NK - g * MMAX)
                    act.wait_ge(side_psum, g + 5)
                    act.activation(kf[:, g * MMAX:g * MMAX + n], side_bank[g % 2][:, 0:n], ACT.Identity,
                                   bias=bk_col[:, 0:1]).then_inc(side_act, 1)
                act.wait_ge(side_act, 8)
                copy(kpart[0], kf).then_inc(kp_ready, 1)

            def next_keys1():
                act.wait_ge(side1_psum, 1)
                copy(cT[:, :], side_bank[0][:, 0:NK1]).then_inc(side1_act, 1)
                act.wait_ge(side1_psum, 2)
                copy(kf1[:, :], side_bank[1][:, 0:NK1]).then_inc(side1_act, 1)
                act.wait_ge(side1_act, 2)
                copy(kpart1[0], kf1[:, :]).then_inc(kp1_ready, 1)
                act.wait_ge(side1_psum, 3)
                copy(v1aug[:, :, :, 0:HD], side_bank[0][:, 0:NK1].rearrange("p (c h d) -> p c h d", c=KC1, h=H)).then_inc(side1_act, 1)

            def experts(l):
                nch, ftot = ((NC0, F0), (NC1, F1))[l]
                act.wait_ge(lz_ready[l], 1)
                act.activation(le[:, :, :], lz[:, :, :], ACT.Exp).then_inc(le_ready[l], 1)
                if l == 0:
                    next_keys()
                else:
                    next_keys1()
                for c in range(nch):
                    n = rows(c, ftot)
                    act.wait_ge(gu_ready[l], c + 1)
                    if c >= 3:
                        act.wait_ge(gt_done[l], c - 2)
                    act.activation(th[0:n, c % 3, :], gu_bank[c % 3][0:n, 0:NQ], ACT.Tanh, scale=0.5).then_inc(th_ready[l], 1)

            for g, (dst, srcs) in enumerate(stages):
                if g % 2 == 1:
                    act.wait_ge(stage_psum, g + 1)
                    np_, w = dst.shape
                    copy(dst, quarter[g % 4][0:np_, 0:w]).then_inc(stage_act, 1)
            act.wait_ge(w2_in, 16 * 15)
            act.wait_ge(stage_psum, len(stages))
            next_keys()
            next_keys1()
            meet(act, 1)
            with act.Fori(0, NB):
                attention0()
                experts(0)
                attention1()
                experts(1)
                meet(act, 1)

        @block.vector
        def _(dve):
            def norm(k, src, st):
                for s in range(NS):
                    st.do(dve.bn_stats(stats[:, s, :], src[:, s, :]))
                st.wait()
                for s in range(NS):
                    m = dve.bn_aggr(mv[:, s, :], stats[:, s, :])
                m.then_inc(mv_ready, 1)
                dve.wait_ge(rstd_ready, k + 1)
                for s in range(NS):
                    m = dve.tensor_scalar(xn[:, s, :], src[:, s, :], mv[:, s, 0:1], rstd[:, s, :], ALU.subtract, ALU.mult)
                m.then_inc(ln_ready, 1)
                dve.wait_ge(xT_psum, k + 1)
                dve.tensor_copy(xnT[:, :], quarter[0][:, 0:NQ]).then_inc(xT_ready, 1)

            def query_parts(layer, st):
                dve.wait_ge(q_psum, layer + 1)
                src = quarter[2][:, 0:NQ].rearrange("p (s h d) -> p s h d", s=NS, h=H)
                if layer == 0:
                    st.link(dve.scalar_tensor_tensor(out=qs[:, :, :, :].rearrange("p s h d -> p s (h d)"),
                                                     in0=quarter[2][:, 0:NQ].rearrange("p (s n) -> p s n", s=NS), scalar=SCALE,
                                                     in1=bqs[:, :].unsqueeze(1).to_broadcast([P, NS, D]),
                                                     op0=ALU.mult, op1=ALU.add))
                else:
                    st.link(dve.tensor_scalar(qs[:, :, :, :], src, SCALE, None, ALU.mult))
                st.link(dve.tensor_copy(qst[:, :, :, 0:8], qs[:, :, :, :]))
                st.link(dve.tensor_tensor(qres[:, :, :, :], qs[:, :, :, :], qst[:, :, :, 0:8], ALU.subtract))
                st.link(dve.tensor_copy(qst[:, :, :, 8:16], qres[:, :, :, :]))
                st.do(dve.tensor_tensor(qst[:, :, :, 16:24], qres[:, :, :, :], qst[:, :, :, 8:16], ALU.subtract))
                st.do(dve.tensor_copy(qst[:, :, :, 24:40], qst[:, :, :, 0:16]))
                dve.tensor_copy(qst[:, :, :, 40:48], qst[:, :, :, 0:8]).then_inc(qst_ready, 1)

            def attend_out(layer, xin, xout, st):
                dve.wait_ge((pv_done, pv1_done)[layer], (NX, NX1)[layer])
                st.link(dve.reciprocal(rec[:, :, :], pv_out[:, :, :, HD]))
                dve.tensor_tensor(att[:, :, :, :], pv_out[:, :, :, 0:HD], rec[:, :, :].unsqueeze(3).to_broadcast([P, NS, H, HD]),
                                  ALU.mult).then_inc(at_ready, 1)
                dve.wait_ge(atT_psum, layer + 1)
                dve.tensor_copy(attT[:, :], quarter[0][:, 0:NQ]).then_inc(atT_ready, 1)
                dve.wait_ge(o_psum, layer + 1)
                dve.tensor_tensor(xout[:, :, :], quarter[2][:, 0:NQ].rearrange("p (s d) -> p s d", s=NS), xin[:, :, :],
                                  ALU.add).then_inc(x_ready, 1)
                dve.wait_ge(x_ready, 2 * layer + 1)

            def attention0():
                def join(p):
                    dve.wait_ge(half_read, 8 * (p + 1))
                    if p >= 2:
                        dve.wait_ge(m_ready, p - 1)
                    dve.tensor_tensor(nm[:, p % 2, :, :], mx[:, p % 2, :, :, 0], mx[:, p % 2, :, :, 1], ALU.min).then_inc(nm_ready, 1)

                for k in range(NH0):
                    u, half = divmod(k, 2)
                    p, r = divmod(u, 4)
                    hh, s = divmod(r, 2)
                    dve.wait_ge(half_ready, k + 1)
                    if k % 8 == 0 and p >= 2:
                        dve.wait_ge(nm_ready, p - 1)
                    n = min(1024, NK - half * 1024)
                    dve.tensor_reduce(mx[:, p % 2, s, hh, half:half + 1], (a0, a1)[half][:, 0:n], AX, ALU.max,
                                      negate=True).then_inc(half_read, 1)
                    if k % 8 == 0 and p >= 1:
                        join(p - 1)
                join(NP - 1)

            def attention1(st):
                dve.wait_ge(maskq_psum, 1)
                dve.tensor_copy(maskq[:, :, :].rearrange("p s k -> p (s k)"), ob[:, :].bitcast(bf16)[:, 0:NS * NK1]).then_inc(maskq_ready, 1)
                for p in range(NP + 1):
                    if p < NP:
                        dve.wait_ge(pair_ready, p + 1)
                        dve.tensor_reduce(mx1[:, p, :, :].rearrange("p h s -> p (h s)"), (a0, a1)[p % 2][:, :].rearrange("p (n k) -> p n k", k=NK1),
                                          AX, ALU.max, negate=True).then_inc(pair_read, 1)
                    if p >= 1:
                        x = 2 * (p - 1)
                        dve.wait_ge(b1_read, ev1_e(x) + 1)
                        dve.tensor_tensor(probs[:, x % 4, :], probs[:, x % 4, :], cntT[:, :, :].rearrange("p c q -> p (c q)"),
                                          ALU.mult).then_inc(mulv, 1)

            def routing(l, st):
                dve.wait_ge(gate_psum[l], 1)
                g = bs[0][:, 0:NS * NE].rearrange("p (s e) -> p s e", s=NS)
                if l == 0:
                    st.link(dve.tensor_tensor(ls[:, :, :], g, gb_bc[:, :].unsqueeze(1).to_broadcast([P, NS, NE]), ALU.add))
                    dve.tensor_scalar(lz[:, :, :], ls[:, :, :], -1.0, None, ALU.mult).then_inc(lz_ready[l], 1)
                    dve.wait_ge(le_ready[l], 1)
                    st.link(dve.tensor_scalar(lz[:, :, :], le[:, :, :], 1.0, None, ALU.add))
                    st.link(dve.reciprocal(ls[:, :, :], lz[:, :, :]))
                else:
                    st.link(dve.tensor_reduce(lneg[:, :], g[:, :, 0:8], AX, ALU.max, negate=True))
                    dve.tensor_tensor(lz[:, :, 0:8], g[:, :, 0:8], lneg[:, :].unsqueeze(2).to_broadcast([P, NS, 8]), ALU.add)
                    dve.tensor_scalar(lz[:, :, 8:9], g[:, :, 8:9], -1.0, None, ALU.mult).then_inc(lz_ready[l], 1)
                    dve.wait_ge(le_ready[l], 1)
                    st.link(dve.tensor_reduce(lsum[:, :], le[:, :, 0:8], AX, ALU.add))
                    st.link(dve.reciprocal(lrec[:, :], lsum[:, :]))
                    st.link(dve.tensor_tensor(ls[:, :, 0:8], le[:, :, 0:8], lrec[:, :].unsqueeze(2).to_broadcast([P, NS, 8]), ALU.mult))
                    st.link(dve.tensor_scalar(lz[:, :, 8:9], le[:, :, 8:9], 1.0, None, ALU.add))
                n = (NE, 8)[l]
                for s in range(NS):
                    st.do(dve.max(top[:, s, :], ls[:, s, 0:n]))
                st.wait()
                for s in range(NS):
                    st.do(dve.max_index(topi[:, s, :], top[:, s, :], ls[:, s, 0:n]))
                st.do(dve.tensor_tensor(wden[:, :], top[:, :, 0], top[:, :, 1], ALU.add))
                st.wait()
                if l == 0:
                    st.link(dve.tensor_scalar(wden[:, :], wden[:, :], 1e-20, None, ALU.add))
                st.do(dve.tensor_copy(topf[:, :, :], topi[:, :, :]))
                st.link(dve.reciprocal(wrec[:, :], wden[:, :]))
                st.link(dve.tensor_tensor(wtop[:, :, :], top[:, :, 0:2], wrec[:, :].unsqueeze(2).to_broadcast([P, NS, 2]), ALU.mult))
                for s in range(NS):
                    st.do(dve.tensor_scalar(cw[:, s, 0:n], iota_f[:, 0:n], topf[:, s, 0:1], wtop[:, s, 0:1], ALU.is_equal, ALU.mult))
                    st.do(dve.tensor_scalar(cw2[:, s, 0:n], iota_f[:, 0:n], topf[:, s, 1:2], wtop[:, s, 1:2], ALU.is_equal, ALU.mult))
                st.wait()
                st.do(dve.tensor_tensor(cwr[:, :, 0:n], cw[:, :, 0:n], cw2[:, :, 0:n], ALU.add))
                if l == 1:
                    st.do(dve.reciprocal(cwr[:, :, 8:9], lz[:, :, 8:9]))
                st.wait()
                st.link(dve.tensor_scalar(cw[:, :, :], cwr[:, :, :], 0.5, None, ALU.mult))
                st.link(dve.tensor_copy(cwp[:, :, 0:NE], cw[:, :, :]))
                st.link(dve.tensor_tensor(cwr[:, :, :], cw[:, :, :], cwp[:, :, 0:NE], ALU.subtract))
                st.link(dve.tensor_copy(cwp[:, :, CWP:CWP + NE], cwr[:, :, :]))
                dve.tensor_tensor(cwp[:, :, 2 * CWP:2 * CWP + NE], cwr[:, :, :], cwp[:, :, CWP:CWP + NE], ALU.subtract).then_inc(cwp_ready[l], 1)

            def next_values():
                for g in range(4):
                    dve.wait_ge(side_psum, g + 9)
                    nc_ = min(4, KC - 4 * g)
                    kn = min(P, NK - 4 * g * P)
                    dve.tensor_tensor(vaug[0:kn, 4 * g:4 * g + nc_, :, 0:HD],
                                      side_bank[g % 2][0:kn, 0:nc_ * P].rearrange("p (c h d) -> p c h d", c=nc_, h=H),
                                      bv_bc[0:kn, :].rearrange("p (h d) -> p h d", d=HD).unsqueeze(1).to_broadcast([kn, nc_, H, HD]),
                                      ALU.add).then_inc(side_dve, 1)

            def take_counts(st):
                dve.wait_ge(cnt_psum, 1)
                for s in range(NS):
                    st.do(dve.tensor_copy(cntT[:, :, s * P:(s + 1) * P].rearrange("p c q -> p q c"),
                                          cnt_bank[s][:, 0:P * KC1].rearrange("p (q c) -> p q c", c=KC1)))
                st.wait()
                dve.tensor_scalar(maskT[:, :, :], cntT[:, :, :], 0.0, NEG, ALU.is_equal, ALU.mult).then_inc(cnt_ready, 1)

            def experts(l, xin, xout, st):
                nch, ftot = ((NC0, F0), (NC1, F1))[l]
                routing(l, st)
                if l == 0:
                    take_counts(st)
                    next_values()
                dve.wait_ge(cwT_psum[l], 1)
                dve.tensor_copy(cwT[:, :], bsb[1][0:CWR, 0:NQ]).then_inc(cwT_ready[l], 1)

                def hidden(c):
                    n = rows(c, ftot)
                    dve.wait_ge(hu_done[l], c + 1)
                    dve.wait_ge(cb_ready[l], c + 1)
                    if c >= 4:
                        dve.wait_ge(down_done[l], c - 3)
                    dve.tensor_tensor(hid[0:n, c % 4, :], hu[0:n, c % 3, :], cb_bank[c % 2][0:n, 0:NQ], ALU.mult).then_inc(hid_ready[l], 1)

                for c in range(nch):
                    n = rows(c, ftot)
                    g = gu_bank[c % 3]
                    dve.wait_ge(th_ready[l], c + 1)
                    dve.scalar_tensor_tensor(out=gt[0:n, c % 3, :], in0=th[0:n, c % 3, :], scalar=1.0, in1=g[0:n, 0:NQ],
                                             op0=ALU.add, op1=ALU.mult).then_inc(gt_done[l], 1)
                    if c >= 1:
                        hidden(c - 1)
                    dve.wait_ge(gt_done[l], c + 1)
                    dve.tensor_tensor(hu[0:n, c % 3, :], gt[0:n, c % 3, :], g[0:n, NQ:2 * NQ], ALU.mult).then_inc(hu_done[l], 1)
                hidden(nch - 1)
                dve.wait_ge(down_done[l], nch)
                if l == 1:
                    dve.wait_ge(xo_free, 1)
                dve.tensor_tensor(xout[:, :, :], ob[:, 0:NQ].rearrange("p (s d) -> p s d", s=NS), xin[:, :, :], ALU.add).then_inc(x_ready, 1)
                dve.wait_ge(x_ready, 2 * l + 2)

            st = Steps(dve, dve_step)
            for g, (dst, srcs) in enumerate(stages):
                if g % 2 == 0:
                    dve.wait_ge(stage_psum, g + 1)
                    np_, w = dst.shape
                    dve.tensor_copy(dst, quarter[g % 4][0:np_, 0:w]).then_inc(stage_dve, 1)
            dve.wait_ge(stage_psum, len(stages))
            dve.memset(kst[:, :, :], 1.0).then_inc(kst_one, 1)
            dve.memset(k1st[:, :, :], 1.0).then_inc(kst_one, 1)
            dve.memset(gb_bc[:, 0:8], 0.0).then_inc(pre_dve, 1)
            dve.memset(vaug[:, :, :, :], 1.0).then_inc(pre_dve, 1)
            dve.memset(v1aug[:, :, :, HD:V1], 1.0).then_inc(pre_dve, 1)
            dve.memset(qst[:, :, :, :], 0.0).then_inc(pre_dve, 1)
            dve.memset(cwp[:, :, :], 0.0).then_inc(pre_dve, 1)
            dve.memset(neg_half[:, :, :], -0.5).then_inc(pre_dve, 1)
            dve.wait_ge(w2_in, 16 * 15)
            dve.wait_ge(pre_dve, 6)
            dve.tensor_scalar(bqs[:, :], bqs[:, :], SCALE, None, ALU.mult)
            next_values()
            meet(dve, 2)
            with dve.Fori(0, NB):
                st = Steps(dve, dve_step)
                norm(0, xs[0], st)
                query_parts(0, st)
                dve.tensor_copy(idx_f[:, :, :], idx_i[:, :, :]).then_inc(idxf_ready, 1)
                st.do(dve.tensor_tensor(x0b[:, :, :], xs[0][:, :, :], bo_bc[:, :].unsqueeze(1).to_broadcast([P, NS, D]), ALU.add))
                dve.wait_ge(idxT_psum, 1)
                st.do(dve.tensor_scalar(idx_c[:, :, 0], quarter[1][:, 0:P], float(P), None, ALU.is_lt))
                st.do(dve.tensor_scalar(idx_c[:, :, 1], quarter[1][:, 0:P], float(P), None, ALU.is_ge))
                st.do(dve.tensor_scalar(idx_hi[:, :], quarter[1][:, 0:P], float(P), None, ALU.is_ge))
                st.wait()
                dve.scalar_tensor_tensor(out=idx_lo[:, :], in0=idx_hi[:, :], scalar=-float(P), in1=quarter[1][:, 0:P],
                                         op0=ALU.mult, op1=ALU.add).then_inc(idxlo_ready, 1)
                attention0()
                attend_out(0, x0b, xs[1], st)
                norm(1, xs[1], st)
                experts(0, xs[1], xs[2], st)
                norm(2, xs[2], st)
                query_parts(1, st)
                attention1(st)
                attend_out(1, xs[2], xs[3], st)
                norm(3, xs[3], st)
                experts(1, xs[3], xs[4], st)
                meet(dve, 2)

        @block.gpsimd
        def _(pool):
            def rstd_of(k, st):
                pool.wait_ge(mv_ready, k + 1)
                st.link(pool.tensor_scalar(veps[:, :, :], mv[:, :, 1:2], EPS, None, ALU.add))
                pool.tensor_tensor(rstd[:, :, :], veps[:, :, :], neg_half[:, :, :], ALU.pow).then_inc(rstd_ready, 1)

            def max_parts(src, p, ready, st):
                def col(t):
                    return qst[:, :, 2 * p:2 * p + 2, KROWS + t]
                st.link(pool.tensor_copy(col(0), src))
                st.link(pool.tensor_tensor(nmr[:, :, :], src, col(0), ALU.subtract))
                st.link(pool.tensor_copy(col(1), nmr[:, :, :]))
                pool.tensor_tensor(col(2), nmr[:, :, :], col(1), ALU.subtract).then_inc(ready, 1)
                pool.wait_ge(ready, p + 1)

            def attention0(st):
                pool.wait_ge(idxlo_ready, 1)
                for p in range(NP):
                    for q in range(16 * p, 16 * p + 16):
                        m = pool.tensor_scalar(onehot[:, q, :], iota_f[:, :], idx_lo[:, q:q + 1], None, ALU.is_equal)
                    m.then_inc(onehot_ready, 1)
                    pool.wait_ge(nm_ready, p + 1)
                    max_parts(nm[:, p % 2, :, :], p, m_ready, st)

            def attention1(st):
                for p in range(NP + 1):
                    if p < NP:
                        pool.wait_ge(pair_read, p + 1)
                        max_parts(mx1[:, p, :, :].rearrange("p h s -> p s h"), p, m1_ready, st)
                    if p >= 1:
                        x = 2 * (p - 1) + 1
                        pool.wait_ge(b1_read, ev1_e(x) + 1)
                        pool.tensor_tensor(probs[:, x % 4, :], probs[:, x % 4, :], cntT[:, :, :].rearrange("p c q -> p (c q)"),
                                           ALU.mult).then_inc(mulp, 1)

            def split(src, res, parts, ready, res_ready):
                pool.wait_ge(ready, 1)
                pool.tensor_tensor(res, src, parts[0], ALU.subtract).then_inc(res_ready, 1)
                pool.wait_ge(res_ready, 1)
                pool.tensor_copy(parts[1], res).then_inc(ready, 1)
                pool.wait_ge(ready, 2)
                pool.tensor_tensor(parts[2], res, parts[1], ALU.subtract).then_inc(ready, 1)
                pool.wait_ge(ready, 3)

            def next_keys():
                split(kf, kres, kpart, kp_ready, kres_ready)

            def next_keys1():
                split(kf1[:, :], kres1[:, :], kpart1, kp1_ready, kres1_ready)

            st = Steps(pool, pool_step)
            st.do(pool.memset(ident[:, :], 0.0))
            st.do(pool.memset(identb[:, :], 0.0))
            st.do(pool.iota(iota_i[:, :], pattern=[[1, P]], base=0, channel_multiplier=0))
            st.wait()
            pool.affine_select(out=ident[:, :], in_=ident[:, :], compare_op=ALU.not_equal, fill=1.0, base=0,
                               pattern=[[-1, P]], channel_multiplier=1).then_inc(const_ready, 1)
            pool.affine_select(out=identb[:, :], in_=identb[:, :], compare_op=ALU.not_equal, fill=1.0, base=0,
                               pattern=[[-1, P]], channel_multiplier=1).then_inc(const_ready, 1)
            st.do(pool.tensor_copy(iota_f[:, :], iota_i[:, :]))
            for l, width, ftot in ((0, I0, F0), (1, I1, F1)):
                st.link(pool.memset(sel[l][:, :], 0.0))
                for t in range(3):
                    part = sel[l][CWP * t:CWP * t + NE, :]
                    st.link(pool.memset(part, 1.0))
                    st.link(pool.affine_select(out=part, in_=part, compare_op=ALU.is_ge, fill=0.0, base=0,
                                               pattern=[[1, ftot]], channel_multiplier=-width))
                    st.link(pool.affine_select(out=part, in_=part, compare_op=ALU.is_ge, fill=0.0, base=width - 1,
                                               pattern=[[-1, ftot]], channel_multiplier=width))
            next_keys()
            next_keys1()
            meet(pool, 3)
            with pool.Fori(0, NB):
                st = Steps(pool, pool_step)
                rstd_of(0, st)
                attention0(st)
                rstd_of(1, st)
                next_keys()
                rstd_of(2, st)
                attention1(st)
                rstd_of(3, st)
                next_keys1()
                meet(pool, 3)


_INS = ['x', 'ctx_1024', 'itok_BxSx64_0_2047', 'L0_xattn_Wq', 'L0_xattn_bq', 'L0_xattn_Wkv', 'L0_xattn_bkv', 'L0_xattn_Wo',
        'L0_xattn_bo', 'L0_ffn_w1', 'L0_ffn_w2', 'L0_ffn_w3', 'L0_ffn_new_w1', 'L0_ffn_new_w2', 'L0_ffn_new_w3',
        'L0_ffn_gate_weight', 'L0_ffn_new_gate_weight', 'L0_ffn_gate_bias', 'L1_xattn_W_q', 'L1_xattn_W_kv_down',
        'L1_xattn_W_kv_up', 'L1_xattn_W_out', 'L1_ffn_gate_w', 'L1_ffn_w_gate', 'L1_ffn_w_up', 'L1_ffn_w_down',
        'L1_ffn_sw_gate', 'L1_ffn_sw_up', 'L1_ffn_sw_down', 'L1_ffn_shared_gate_w']


def kernel(**inputs):
    import numpy as _np
    import concourse.bacc as _bacc
    from concourse.bass_utils import run_bass_kernel_spmd as _run

    nc = _bacc.Bacc("TRN2", target_bir_lowering=False, num_devices=1)
    arrays, args = {}, []
    for name in _INS:
        a = _np.ascontiguousarray(inputs[name])
        arrays[f"in_{name}"] = a
        args.append(nc.dram_tensor(f"in_{name}", a.shape, mybir.dt.from_np(a.dtype), kind="ExternalInput").ap())
    args.append(nc.dram_tensor("out_0", (NB, NQ, D), mybir.dt.float32, kind="ExternalOutput").ap())
    build(nc, *args)
    r = _run(nc, [arrays], core_ids=[0])
    return r.results[0]["out_0"]
```

```python
import concourse.bass as bass
from concourse import mybir
from contextlib import ExitStack

P = 128
NB, NQ, D = 8, 256, 128
NS = NQ // P
NK = 1601
NK1 = 256
NIDX = 64
H, HD = 16, 8
NP = H // 2
SLOT = 64
KC = (NK + P - 1) // P
KLAST = NK - (KC - 1) * P
KC1 = NK1 // P
V1 = HD + 1
QPART = (0, 1, 2, 0, 1, 0)
KPART = (0, 0, 0, 1, 1, 2)
NT = len(QPART)
KROWS = NT * HD
MROWS = KROWS + 3
SCALE = float(HD) ** -0.5
EPS = 1e-5
NE = 9
I0, I1 = 352, 176
F0, F1 = NE * I0, NE * I1
NC0, NC1 = (F0 + P - 1) // P, (F1 + P - 1) // P
NEG = -1e30
CWP = 32
CWR = 2 * CWP + NE
NPS = 6
NHV = 6
QD = 32
MMAX = 512


def rows(c, total):
    return min(P, total - c * P)


def build(nc, x, ctx_in, itok, Wq, bq, Wkv, bkv, Wo, bo, w1, w2, w3, nw1, nw2, nw3, gw, ngw, gb,
          Wq1, Wd1, Wu1, Wout1, gw1, wg, wu, wd, swg, swu, swd, sgw, out):
    f32, bf16, i32, u32 = mybir.dt.float32, mybir.dt.bfloat16, mybir.dt.int32, mybir.dt.uint32
    ALU, ACT, AX = mybir.AluOpType, mybir.ActivationFunctionType, mybir.AxisListType.X
    k_parts = nc.dram_tensor("k_parts", [3, P, NK], bf16, kind="Internal").ap()
    k1_parts = nc.dram_tensor("k1_parts", [3, P, NK1], bf16, kind="Internal").ap()

    with ExitStack() as es:
        def sb(name, shape, dt=f32):
            return es.enter_context(nc.sbuf_tensor(name, shape, dt))

        def psum(name, width):
            return es.enter_context(nc.psum_tensor(name, [P, width], f32))

        wq_sb, wkv_sb, wo_sb = sb("wq_sb", [P, D]), sb("wkv_sb", [P, 2 * D]), sb("wo_sb", [P, D])
        wq1T, wd1T, wu1T, wo1T = sb("wq1T", [P, D]), sb("wd1T", [P, D]), sb("wu1T", [P, 2 * D]), sb("wo1T", [P, D])
        bqs = sb("bqs", [P, D])
        bv_bc, bo_bc = sb("bv_bc", [P, D]), sb("bo_bc", [P, D])
        bk_col = sb("bk_col", [P, 1])
        gb_bc = sb("gb_bc", [P, NE])
        gT = [sb("gT0", [P, NE]), sb("gT1", [P, NE])]
        gT_nat = [sb("g_nat0", [NE, P]), sb("g_nat1", [NE, P])]
        w1T, w3T, w2T = sb("w1T", [P, F0]), sb("w3T", [P, F0]), sb("w2T", [P, NC0, D])
        wg_sb, wu_sb, wd_sb = sb("wg_sb", [P, F1]), sb("wu_sb", [P, F1]), sb("wd_sb", [P, NC1, D])
        sel = [sb("sel0", [CWR, F0], bf16), sb("sel1", [CWR, F1], bf16)]
        sq_nat = sb("sq_nat", [P, 5, P])
        ident, identb = sb("ident", [P, P]), sb("identb", [P, P], bf16)
        iota_i, iota_f, iotab = sb("iota_i", [P, P], i32), sb("iota_f", [P, P]), sb("iotab", [P, P], bf16)
        comb = sb("comb", [P, 2 * V1])
        neg_half = sb("neg_half", [P, NS, 1])
        xs = [sb(f"x{k}", [P, NS, D]) for k in range(5)]
        x0b = sb("x0b", [P, NS, D])
        xn, xnT = sb("xn", [P, NS, D]), sb("xnT", [P, NQ])
        stats, mv = sb("stats", [P, NS, 6]), sb("mv", [P, NS, 2])
        veps, rstd = sb("veps", [P, NS, 1]), sb("rstd", [P, NS, 1])
        big = sb("big", [P, 8192])
        onehot = big[:, :].bitcast(bf16).rearrange("p (q r) -> p q r", r=P)
        kf, kres = big[:, 0:NK], big[:, 1602:1602 + NK]
        kpart = [big[:, 3204 + 802 * t:3204 + 802 * (t + 1)].bitcast(bf16)[:, 0:NK] for t in range(3)]
        w1_nat = big[:, 0:NC0 * P].rearrange("p (c d) -> p c d", d=P)
        w3_nat = big[:, 4096:4096 + NC0 * P].rearrange("p (c d) -> p c d", d=P)
        kst = sb("kst", [P, NP, NK + 1], bf16)
        w2_nat = kst[:, :, :].rearrange("p a k -> p (a k)").bitcast(f32)[:, 0:F0]
        k1st = sb("k1st", [P, NP, NK1], bf16)
        vaug, v1aug = sb("vaug", [P, KC, H, V1]), sb("v1aug", [P, KC1, H, V1])
        ctx_sb, ctxT = sb("ctx_sb", [P, KC, D]), sb("ctxT", [P, NK])
        cT = sb("cT", [P, NK1])
        kpart1 = [sb(f"kpart1_{t}", [P, NK1], bf16)[:, :] for t in range(3)]
        qs, qres = sb("qs", [P, NS, H, HD]), sb("qres", [P, NS, H, HD])
        qst = sb("qst", [P, NS, H, SLOT], bf16)
        qa = sb("qa", [P, NP, NS, P], bf16)
        qb = sb("qb", [P, 2, 2, NQ], bf16)
        mx = sb("mx", [P, 2, NS, 2, 2])
        mx1 = sb("mx1", [P, NP, 2, NS])
        nm, nmr = sb("nm", [P, 2, NS, 2]), sb("nmr", [P, NS, 2])
        probs = sb("probs", [P, NPS, 512])
        kf1, kres1 = probs[:, 2, 0:NK1], probs[:, 2, NK1:2 * NK1]
        oT = sb("oT", [P, NQ])
        raw = sb("raw", [P, NS, H, V1])
        att, attT = sb("att", [P, NS, H, HD]), sb("attT", [P, NQ])
        rec = sb("rec", [P, NS, H])
        idx_i, idx_f = sb("idx_i", [P, NS, NIDX], i32), sb("idx_f", [P, NS, NIDX])
        idx_hi, idx_lo = sb("idx_hi", [P, P]), sb("idx_lo", [P, P])
        idx_c = sb("idx_c", [P, P, 2], bf16)
        cntT = sb("cntT", [P, KC1, NQ])
        maskT, maskq = sb("maskT", [P, KC1, NQ], bf16), sb("maskq", [P, NS, NK1], bf16)
        lz, le, ls = sb("lz", [P, NS, NE]), sb("le", [P, NS, NE]), sb("ls", [P, NS, NE])
        lneg, lsum, lrec = sb("lneg", [P, NS]), sb("lsum", [P, NS]), sb("lrec", [P, NS])
        top, topi, topf = sb("top", [P, NS, 8]), sb("topi", [P, NS, 8], u32), sb("topf", [P, NS, 8])
        wden, wrec, wtop = sb("wden", [P, NS]), sb("wrec", [P, NS]), sb("wtop", [P, NS, 2])
        cw, cw2, cwr = sb("cw", [P, NS, NE]), sb("cw2", [P, NS, NE]), sb("cwr", [P, NS, NE])
        cwp = sb("cwp", [P, NS, CWR], bf16)
        cwT = sb("cwT", [CWR, NQ], bf16)
        th, gt, hu = (big[:, 5632 + 768 * k:5632 + 768 * (k + 1)].rearrange("p (n q) -> p n q", q=NQ) for k in range(3))
        hid = probs[:, 0:2, :].rearrange("p a (b q) -> p (a b) q", b=2)
        a0, a1 = psum("a0", 1024), psum("a1", 1024)
        bs = [psum(f"b{k}", 512) for k in range(3)]
        ob = psum("ob", 512)
        quarter = [a0[:, 0:512], a0[:, 512:1024], a1[:, 0:512], a1[:, 512:1024]]
        gu_bank = quarter[0:3]
        cb_bank = bs[0:2]
        cnt_bank = [bs[1], ob]
        side_bank = [bs[2][:, :], quarter[3]]
        bsb = [b[:, :].bitcast(bf16) for b in bs]

        first_sem = [None]

        def sem(name):
            s = es.enter_context(nc.semaphore(name))
            if first_sem[0] is None:
                first_sem[0] = s.num
            last_sem[0] = s.num
            return s
        last_sem = [None]

        ctx_in_s, x_in, idx_in, kst_in, k1st_in = (sem(n) for n in ("ctx_in", "x_in", "idx_in", "kst_in", "k1st_in"))
        kw_done, kw1_done = sem("kw_done"), sem("kw1_done")
        mv_ready, rstd_ready, ln_ready, xT_psum, xT_ready = (sem(n) for n in ("mv_ready", "rstd_ready", "ln_ready", "xT_psum", "xT_ready"))
        q_psum, qst_ready, qst_read = sem("q_psum"), sem("qst_ready"), sem("qst_read")
        at_ready, atT_psum, atT_ready, o_psum, x_ready = (sem(n) for n in ("at_ready", "atT_psum", "atT_ready", "o_psum", "x_ready"))
        half_ready, half_read, nm_ready, m_ready = sem("half_ready"), sem("half_read"), sem("nm_ready"), sem("m_ready")
        b_ready, b_read, pv_done, oT_ready, att_done = (sem(n) for n in ("b_ready", "b_read", "pv_done", "oT_ready", "att_done"))
        pair_ready, pair_read, m1_ready = sem("pair_ready"), sem("pair_read"), sem("m1_ready")
        b1_ready, b1_read, pv1_done, oT1_ready = (sem(n) for n in ("b1_ready", "b1_read", "pv1_done", "oT1_ready"))
        mulv, mulp = sem("mulv"), sem("mulp")
        idxf_ready, idxT_psum, idxlo_ready, onehot_ready, onehotv_ready, cnt_psum, cnt_ready, maskq_psum, maskq_ready = (
            sem(n) for n in ("idxf_ready", "idxT_psum", "idxlo_ready", "onehot_ready", "onehotv_ready", "cnt_psum", "cnt_ready", "maskq_psum", "maskq_ready"))
        gate_psum, lz_ready, le_ready, cwp_ready, cwT_psum, cwT_ready = (
            [sem(f"{n}{k}") for k in range(2)] for n in ("gate_psum", "lz_ready", "le_ready", "cwp_ready", "cwT_psum", "cwT_ready"))
        gu_ready, th_ready, gt_done, hu_done, cb_ready, hid_ready, down_done = (
            [sem(f"{n}{k}") for k in range(2)] for n in ("gu_ready", "th_ready", "gt_done", "hu_done", "cb_ready", "hid_ready", "down_done"))
        side_psum, side_act, side_dve = sem("side_psum"), sem("side_act"), sem("side_dve")
        side1_psum, side1_act = sem("side1_psum"), sem("side1_act")
        kp_ready, kres_ready, kp1_ready, kres1_ready = sem("kp_ready"), sem("kres_ready"), sem("kp1_ready"), sem("kres1_ready")
        dve_step, pool_step, act_step = sem("dve_step"), sem("pool_step"), sem("act_step")
        w_in, w2_in, stage_psum, stage_dve, stage_act, const_ready, pre_dve, kst_one = (
            sem(n) for n in ("w_in", "w2_in", "stage_psum", "stage_dve", "stage_act", "const_ready", "pre_dve", "kst_one"))
        xo_free = sem("xo_free")
        met = sem("met")
        round_sems = range(first_sem[0], last_sem[0] + 1)
        go = [sem(f"go{k}") for k in range(4)]
        out_stored = sem("out_stored")

        def meet(eng, k):
            eng.drain().then_inc(met, 1)
            eng.wait_ge(go[k], 1)
            eng.sem_clear(go[k])

        class Steps:

            def __init__(self, eng, s):
                self.eng, self.s, self.n = eng, s, 0

            def do(self, ins):
                self.n += 1
                ins.then_inc(self.s, 1)

            def wait(self):
                self.eng.wait_ge(self.s, self.n)

            def link(self, ins):
                self.do(ins)
                self.wait()

        block = es.enter_context(nc.Block())

        w1b = [(w1T, w1_nat), (w3T, w3_nat)]
        stages = []
        for dst, nat in w1b:
            for c in range(0, NC0, 4):
                src = [nat[0:rows(k, F0), k, :] for k in range(c, min(c + 4, NC0))]
                width = sum(rows(k, F0) for k in range(c, min(c + 4, NC0)))
                stages.append((dst[:, c * P:c * P + width], src))
        for c in range(0, NC0 - 1, 4):
            stages.append((w2T[:, c:c + 4, :].rearrange("p c d -> p (c d)"), [w2_nat[:, k * P:(k + 1) * P] for k in range(c, c + 4)]))
        stages.append((w2T[0:rows(NC0 - 1, F0), NC0 - 1, :], [w2_nat[:, (NC0 - 1) * P:F0]]))
        for dst, k in ((wq1T, 0), (wd1T, 1), (wo1T, 4)):
            stages.append((dst[:, :], [sq_nat[:, k, :]]))
        stages.append((wu1T[:, :], [sq_nat[:, 2, :], sq_nat[:, 3, :]]))
        for k in range(2):
            stages.append((gT[k][:, :], [gT_nat[k][:, :]]))

        @block.sync
        def _(sp):
            def load_x(b):
                sp.dma_start(xs[0][:, :, :], x[b].rearrange("a (s p) d -> p (a s) d", p=P)).then_inc(x_in, 16)
                sp.dma_start(idx_i[:, :, :], itok[b].rearrange("a (s p) k -> p (a s) k", p=P)).then_inc(idx_in, 16)

            def load_ctx(b):
                sp.dma_start(ctx_sb[:, 0:KC - 1, :],
                             ctx_in[b, 0:(KC - 1) * P, :].rearrange("a (c p) d -> p (a c) d", p=P)).then_inc(ctx_in_s, 16)
                sp.dma_start(ctx_sb[0:KLAST, KC - 1, :],
                             ctx_in[b, (KC - 1) * P:NK, :].rearrange("a k d -> (a k) d")).then_inc(ctx_in_s, 16)

            def spread(parts, scratch, dst, done, filled, ready):
                for t in range(3):
                    sp.wait_ge(ready, t + 1)
                    sp.dma_start(scratch[t], parts[t]).then_inc(done, 16)
                    sp.wait_ge(done, 16 * (t + 1))
                    src = scratch[t].rearrange("(a h d) k -> h d a k", h=2, d=HD)
                    for hh in range(2):
                        for term in range(NT):
                            if KPART[term] == t:
                                r = SLOT * hh + HD * term
                                sp.dma_start(dst[r:r + HD, :, 0:src.shape[3]], src[hh]).then_inc(filled, 16)

            sp.dma_start(w1_nat[:, 0:22, :], w1.rearrange("e i d -> (e i) d").rearrange("(c p) d -> p c d", p=P)).then_inc(w_in, 16)
            sp.dma_start(w1_nat[:, 22:24, :], nw1[0, 0:256, :].rearrange("(c p) d -> p c d", p=P)).then_inc(w_in, 16)
            sp.dma_start(w1_nat[0:96, 24, :], nw1[0, 256:I0, :]).then_inc(w_in, 16)
            sp.dma_start(w3_nat[:, 0:22, :], w3.rearrange("e i d -> (e i) d").rearrange("(c p) d -> p c d", p=P)).then_inc(w_in, 16)
            sp.dma_start(w3_nat[:, 22:24, :], nw3[0, 0:256, :].rearrange("(c p) d -> p c d", p=P)).then_inc(w_in, 16)
            sp.dma_start(w3_nat[0:96, 24, :], nw3[0, 256:I0, :]).then_inc(w_in, 16)
            sp.dma_start(w2_nat[:, 0:8 * I0].rearrange("p (e i) -> p e i", i=I0), w2.rearrange("e d i -> d e i")).then_inc(w_in, 16)
            sp.dma_start(w2_nat[:, 8 * I0:F0], nw2[0]).then_inc(w_in, 16)
            sp.dma_start(sq_nat[:, 0, :], Wq1).then_inc(w_in, 16)
            sp.dma_start(sq_nat[:, 1, :], Wd1).then_inc(w_in, 16)
            sp.dma_start(sq_nat[:, 2:4, :], Wu1.rearrange("(c p) d -> p c d", p=P)).then_inc(w_in, 16)
            sp.dma_start(sq_nat[:, 4, :], Wout1).then_inc(w_in, 16)
            for k, (a, b) in enumerate(((gw, ngw), (gw1, sgw))):
                sp.dma_start(gT_nat[k][0:8, :], a).then_inc(w_in, 16)
                sp.dma_start(gT_nat[k][8:9, :], b).then_inc(w_in, 16)
            load_ctx(slice(0, 1))
            sp.dma_start(wkv_sb[:, :], Wkv).then_inc(w2_in, 16)
            sp.dma_start(bk_col[:, :], bkv[0:D].rearrange("(p a) -> p a", a=1)).then_inc(w2_in, 16)
            sp.dma_start(bv_bc[:, :], bkv[D:2 * D].partition_broadcast(P)).then_inc(w2_in, 16)
            sp.dma_start(bo_bc[:, :], bo.partition_broadcast(P)).then_inc(w2_in, 16)
            sp.dma_start(bqs[:, :], bq.partition_broadcast(P)).then_inc(w2_in, 16)
            sp.dma_start(gb_bc[:, 8:9], gb.partition_broadcast(P)).then_inc(w2_in, 16)
            sp.dma_start(wq_sb[:, :], Wq).then_inc(w2_in, 16)
            sp.dma_start(wo_sb[:, :], Wo).then_inc(w2_in, 16)
            load_x(slice(0, 1))
            for dst, a, b in ((wg_sb, wg, swg), (wu_sb, wu, swu)):
                sp.dma_start(dst[:, 0:8 * I1].rearrange("p (e i) -> p e i", i=I1), a.rearrange("e d i -> d e i")).then_inc(w2_in, 16)
                sp.dma_start(dst[:, 8 * I1:F1], b).then_inc(w2_in, 16)
            sp.dma_start(wd_sb[:, 0:11, :], wd.rearrange("e i d -> (e i) d").rearrange("(c p) d -> p c d", p=P)).then_inc(w2_in, 16)
            sp.dma_start(wd_sb[:, 11, :], swd[0:P, :]).then_inc(w2_in, 16)
            sp.dma_start(wd_sb[0:I1 - P, 12, :], swd[P:I1, :]).then_inc(w2_in, 16)
            sp.wait_ge(kst_one, 1)
            spread(kpart, k_parts, kst, kw_done, kst_in, kp_ready)
            spread(kpart1, k1_parts, k1st, kw1_done, k1st_in, kp1_ready)

            def close():
                sp.wait_ge(kst_in, 16 * 2 * NT)
                sp.wait_ge(k1st_in, 16 * 2 * NT)
                sp.wait_ge(x_in, 16)
                sp.wait_ge(idx_in, 16)
                sp.wait_ge(ctx_in_s, 32)
                sp.wait_ge(met, 4)
                sp.sem_clear(round_sems)
                for g in go:
                    sp.sem_inc(g, 1)

            sp.wait_ge(w2_in, 16 * 15)
            close()
            sp.sem_inc(out_stored, 16)
            with sp.Fori(0, NB) as i:
                nxt = bass.ds((i + 1) % NB, 1)
                load_ctx(nxt)
                sp.wait_ge(x_ready, 1)
                sp.wait_ge(cnt_psum, 1)
                load_x(nxt)
                sp.wait_ge(out_stored, 16)
                sp.sem_clear(out_stored)
                sp.sem_inc(xo_free, 1)
                sp.wait_ge(att_done, 1)
                spread(kpart, k_parts, kst, kw_done, kst_in, kp_ready)
                sp.wait_ge(att_done, 2)
                spread(kpart1, k1_parts, k1st, kw1_done, k1st_in, kp1_ready)
                sp.wait_ge(x_ready, 4)
                sp.dma_start(out[bass.ds(i, 1)].rearrange("a (s p) d -> p (a s) d", p=P), xs[4][:, :, :]).then_inc(out_stored, 16)
                close()
            sp.wait_ge(out_stored, 16)

        NH0 = NP * 2 * NS * 2
        NG = (KC + 1) // 2
        NX = NP * KC
        Q_AT, O_AT, C_AT = KC - 3, 1, 5
        LEAD, LAG = 12, 3
        fills0 = [("all", 0), ("all", 1), ("q", 0)]
        for x in range(NX):
            p, c = divmod(x, KC)
            fills0.append(("e", x))
            if c == C_AT and p >= 1:
                fills0.append(("c", p - 1))
            if c == Q_AT and p + 1 < NP:
                fills0.append(("q", p + 1))
        fills0.append(("c", NP - 1))
        fills1 = [("all", 0), ("all", 1)]
        for p in range(NP):
            fills1 += [("q", p), ("e", 2 * p), ("e", 2 * p + 1)]
            if p >= 2:
                fills1.append(("c", p - 2))
        fills1 += [("c", NP - 2), ("c", NP - 1)]
        fill0, fill1 = ({f: n for n, f in enumerate(fills)} for fills in (fills0, fills1))

        def group(x):
            return NG * (x // KC) + x % KC // 2

        def pair_rows(x):
            return probs[:, x % NPS, :].rearrange("p (h q) -> p h q", h=2)

        @block.tensor
        def _(pe):
            def norm_T(k):
                pe.wait_ge(ln_ready, k + 1)
                for s in range(NS):
                    m = pe.transpose(quarter[0][:, s * P:(s + 1) * P], xn[:, s, :], ident[:, :])
                m.then_inc(xT_psum, 1)
                pe.wait_ge(xT_ready, k + 1)

            def query_parts(layer, w):
                for s in range(NS):
                    m = pe.matmul(quarter[2][:, s * P:(s + 1) * P], xnT[:, s * P:(s + 1) * P], w, start=True, stop=True)
                m.then_inc(q_psum, 1)
                pe.wait_ge(qst_ready, layer + 1)
                for half in range(2):
                    for n in range(8):
                        p, s = divmod(half * 8 + n, NS)
                        m = pe.transpose(bsb[half][:, n * P:(n + 1) * P],
                                         qst[:, s, 2 * p:2 * p + 2, :].rearrange("p h r -> p (h r)"), identb[:, :])
                    m.then_inc((b_ready, b1_ready)[layer], 1)

            def pair_queries(p, e, ready, b_rdy, b_rd):
                pe.wait_ge(ready, p + 1)
                pe.wait_ge(b_rd, max(e - 2, 1))
                for s in range(NS):
                    m = pe.transpose(bsb[e % 3][:, s * P:(s + 1) * P],
                                     qst[:, s, 2 * p:2 * p + 2, :].rearrange("p h r -> p (h r)"), identb[:, :])
                m.then_inc(b_rdy, 1)

            def attend_out(layer, w):
                pe.wait_ge(at_ready, layer + 1)
                for s in range(NS):
                    m = pe.transpose(quarter[0][:, s * P:(s + 1) * P], att[:, s, :, :].rearrange("p h d -> p (h d)"), ident[:, :])
                m.then_inc(atT_psum, 1)
                pe.wait_ge(atT_ready, layer + 1)
                for s in range(NS):
                    m = pe.matmul(quarter[2][:, s * P:(s + 1) * P], attT[:, s * P:(s + 1) * P], w, start=True, stop=True)
                m.then_inc(o_psum, 1)

            def max_half(k):
                u, half = divmod(k, 2)
                p, r = divmod(u, 4)
                hh, s = divmod(r, 2)
                o = SLOT * hh
                if k == 0:
                    pe.wait_ge(b_read, 1)
                if k == 32:
                    pe.wait_ge(b_read, 2)
                if k >= 2:
                    pe.wait_ge(half_read, k - 1)
                bank = (a0, a1)[half]
                for k0 in range(0, 1024, MMAX):
                    n = min(MMAX, NK - half * 1024 - k0)
                    m = pe.matmul(bank[:, k0:k0 + n], qa[o:o + SLOT, p, s, :],
                                  kst[o:o + SLOT, p, half * 1024 + k0:half * 1024 + k0 + n], start=True, stop=True)
                m.then_inc(half_ready, 1)

            def combine(p, e, o_rdy, b_rdy, b_rd):
                pe.wait_ge(o_rdy, p + 1)
                pe.wait_ge(b_rd, e - 2)
                for s in range(NS):
                    m = pe.matmul(bs[e % 3][:, s * 2 * V1:(s + 1) * 2 * V1], oT[:, s * P:(s + 1) * P], comb[:, :],
                                  start=True, stop=True)
                m.then_inc(b_rdy, 1)

            def scores(x):
                e = fill0["e", x]
                p, c = divmod(x, KC)
                kn = rows(c, NK)
                if c == 0:
                    pe.wait_ge(b_read, fill0["q", p] + 1)
                pe.wait_ge(b_read, e - 2)
                pe.matmul(bs[e % 3][0:kn, :], kst[:, p, c * P:c * P + kn], qb[:, p % 2, :, :].rearrange("p h q -> p (h q)"),
                          start=True, stop=True).then_inc(b_ready, 1)

            def weigh(g):
                p, j = divmod(g, NG)
                last = min(2 * j + 1, KC - 1)
                pe.wait_ge(b_read, fill0["e", KC * p + last] + 1)
                if j == 0 and p >= 1:
                    pe.wait_ge(oT_ready, p)
                for c in range(2 * j, last + 1):
                    kn = rows(c, NK)
                    for hh in range(2):
                        q = QD * (2 * hh + c % 2)
                        m = pe.matmul(ob[q:q + V1, 0:NQ], vaug[0:kn, c, 2 * p + hh, :],
                                      probs[0:kn, (KC * p + c) % NPS, hh * NQ:(hh + 1) * NQ],
                                      start=(j == 0), stop=(c + 2 >= KC), skip_group_check=True, tile_position=(0, q))
                m.then_inc(pv_done, 1)

            def attention0():
                done = [0]

                def halves(upto):
                    while done[0] < min(upto, NH0):
                        max_half(done[0])
                        done[0] += 1
                halves(LEAD)
                weighed = [0]
                for kind, n in fills0[2:]:
                    if kind == "q":
                        pair_queries(n, fill0[kind, n], m_ready, b_ready, b_read)
                    elif kind == "c":
                        if n == NP - 1:
                            for g in range(weighed[0], NP * NG):
                                weigh(g)
                        combine(n, fill0[kind, n], oT_ready, b_ready, b_read)
                    else:
                        scores(n)
                        halves(LEAD + (n + 1) * 8 // KC)
                        if n >= LAG and group(n - LAG + 1) > group(n - LAG):
                            weigh(weighed[0])
                            weighed[0] += 1
                pe.drain().then_inc(att_done, 1)

            def count():
                pe.wait_ge(onehot_ready, NP)
                pe.wait_ge(onehotv_ready, NP)
                for q in range(P):
                    for s in range(NS):
                        cnt = cnt_bank[s][:, 0:P * KC1].rearrange("p (q c) -> p q c", c=KC1)
                        m = pe.matmul(cnt[:, q, :], onehot[s * NIDX:(s + 1) * NIDX, q, :], idx_c[s * NIDX:(s + 1) * NIDX, q, :],
                                      start=True, stop=True)
                m.then_inc(cnt_psum, 1)

            def attention1():
                pe.wait_ge(cnt_ready, 1)
                for n in range(NS * KC1):
                    s, c = divmod(n, KC1)
                    m = pe.transpose(ob[:, :].bitcast(bf16)[:, n * P:(n + 1) * P], maskT[:, c, s * P:(s + 1) * P], identb[:, :])
                m.then_inc(maskq_psum, 1)
                pe.wait_ge(maskq_ready, 1)
                pe.wait_ge(b1_read, 2)

                def max_pair(p):
                    bank = (a0, a1)[p % 2]
                    if p >= 2:
                        pe.wait_ge(pair_read, p - 1)
                    for hh in range(2):
                        o = SLOT * hh
                        cols = bank[:, hh * 512:(hh + 1) * 512].rearrange("p (s k) -> p s k", s=NS)
                        for s in range(NS):
                            pe.matmul(cols[:, s, :], identb[:, :], maskq[:, s, :], start=True, stop=False)
                            m = pe.matmul(cols[:, s, :], qa[o:o + SLOT, p, s, :], k1st[o:o + SLOT, p, :], start=False, stop=True)
                    m.then_inc(pair_ready, 1)

                def scores1(x):
                    e = fill1["e", x]
                    p, c = divmod(x, KC1)
                    if c == 0:
                        pe.wait_ge(b1_read, fill1["q", p] + 1)
                    pe.wait_ge(b1_read, e - 2)
                    pe.matmul(bs[e % 3][:, :], identb[:, :], maskT[:, c, :].unsqueeze(1).to_broadcast([P, 2, NQ]), start=True, stop=False)
                    pe.matmul(bs[e % 3][:, :], k1st[:, p, c * P:(c + 1) * P], qb[:, p % 2, :, :].rearrange("p h q -> p (h q)"),
                              start=False, stop=True).then_inc(b1_ready, 1)

                def weigh1(p):
                    pe.wait_ge(mulv, p + 1)
                    pe.wait_ge(mulp, p + 1)
                    if p >= 1:
                        pe.wait_ge(oT1_ready, p)
                    for c in range(KC1):
                        for hh in range(2):
                            q = QD * (2 * hh + c)
                            m = pe.matmul(ob[q:q + V1, 0:NQ], v1aug[:, c, 2 * p + hh, :],
                                          probs[:, (KC1 * p + c) % NPS, hh * NQ:(hh + 1) * NQ],
                                          start=True, stop=True, tile_position=(0, q))
                    m.then_inc(pv1_done, 1)

                max_pair(0)
                for kind, n in fills1[2:]:
                    if kind == "q":
                        if n + 1 < NP:
                            max_pair(n + 1)
                        pair_queries(n, fill1[kind, n], m1_ready, b1_ready, b1_read)
                    elif kind == "e":
                        scores1(n)
                        if n % 2 == 1 and n >= 3:
                            weigh1(n // 2 - 1)
                    else:
                        if n == NP - 1:
                            weigh1(NP - 1)
                        combine(n, fill1[kind, n], oT1_ready, b1_ready, b1_read)
                pe.drain().then_inc(att_done, 1)

            def next_keys():
                pe.wait_ge(ctx_in_s, 32)
                for g in range(4):
                    if g >= 2:
                        pe.wait_ge(side_act, g - 1)
                    for c in range(4 * g, min(4 * g + 4, KC)):
                        kn = min(P, NK - c * P)
                        m = pe.transpose(side_bank[g % 2][:, (c % 4) * P:(c % 4) * P + kn], ctx_sb[0:kn, c, :], ident[0:kn, 0:kn])
                    m.then_inc(side_psum, 1)
                for g in range(4):
                    pe.wait_ge(side_act, g + 3)
                    n = min(MMAX, NK - g * MMAX)
                    pe.matmul(side_bank[g % 2][:, 0:n], wkv_sb[:, 0:D], ctxT[:, g * MMAX:g * MMAX + n],
                              start=True, stop=True).then_inc(side_psum, 1)
                for g in range(4):
                    if g < 2:
                        pe.wait_ge(side_act, g + 7)
                    else:
                        pe.wait_ge(side_dve, g - 1)
                    for c in range(4 * g, min(4 * g + 4, KC)):
                        kn = min(P, NK - c * P)
                        m = pe.matmul(side_bank[g % 2][0:kn, (c % 4) * P:(c % 4 + 1) * P], ctxT[:, c * P:c * P + kn], wkv_sb[:, D:2 * D],
                                      start=True, stop=True)
                    m.then_inc(side_psum, 1)

            def next_keys1():
                pe.wait_ge(side_dve, 4)
                pe.matmul(side_bank[0][:, 0:NK1], wd1T[:, :], ctxT[:, 0:NK1], start=True, stop=True).then_inc(side1_psum, 1)
                pe.wait_ge(side1_act, 1)
                pe.matmul(side_bank[1][:, 0:NK1], wu1T[:, 0:D], cT[:, :], start=True, stop=True).then_inc(side1_psum, 1)
                for c in range(KC1):
                    m = pe.matmul(side_bank[0][:, c * P:(c + 1) * P], cT[:, c * P:(c + 1) * P], wu1T[:, D:2 * D], start=True, stop=True)
                m.then_inc(side1_psum, 1)

            def experts(l):
                wga, wua, wda, nch, ftot = ((w1T, w3T, w2T, NC0, F0), (wg_sb, wu_sb, wd_sb, NC1, F1))[l]
                lag = 3
                for s in range(NS):
                    m = pe.matmul(bs[0][:, s * NE:(s + 1) * NE], xnT[:, s * P:(s + 1) * P], gT[l][:, :], start=True, stop=True)
                m.then_inc(gate_psum[l], 1)
                if l == 0:
                    count()
                    next_keys()
                else:
                    next_keys1()

                def gate_up(c):
                    if c >= 3:
                        pe.wait_ge(hu_done[l], c - 2)
                    n = rows(c, ftot)
                    pe.matmul(gu_bank[c % 3][0:n, 0:NQ], wga[:, c * P:c * P + n], xnT[:, :], start=True, stop=True)
                    pe.matmul(gu_bank[c % 3][0:n, NQ:2 * NQ], wua[:, c * P:c * P + n], xnT[:, :], start=True, stop=True).then_inc(gu_ready[l], 1)

                def weights(c):
                    if c >= 2:
                        pe.wait_ge(hid_ready[l], c - 1)
                    n = rows(c, ftot)
                    pe.matmul(cb_bank[c % 2][0:n, 0:NQ], sel[l][:, c * P:c * P + n], cwT[:, :], start=True, stop=True).then_inc(cb_ready[l], 1)

                def down(c):
                    pe.wait_ge(hid_ready[l], c + 1)
                    n = rows(c, ftot)
                    for s in range(NS):
                        m = pe.matmul(ob[:, s * P:(s + 1) * P], hid[0:n, c % 4, s * P:(s + 1) * P], wda[0:n, c, :],
                                      start=(c == 0 and s == 0), stop=(c == nch - 1), skip_group_check=True)
                    m.then_inc(down_done[l], 1)

                gate_up(0)
                gate_up(1)
                pe.wait_ge(cwp_ready[l], 1)
                for s in range(NS):
                    m = pe.transpose(bsb[1][0:CWR, s * P:(s + 1) * P], cwp[:, s, :], identb[:, :])
                m.then_inc(cwT_psum[l], 1)
                gate_up(2)
                pe.wait_ge(cwT_ready[l], 1)
                weights(0)
                weights(1)
                for c in range(3, nch + lag):
                    if c < nch:
                        gate_up(c)
                    if 2 <= c - 1 < nch:
                        weights(c - 1)
                    down(c - lag)

            pe.wait_ge(const_ready, 2)
            pe.wait_ge(w_in, 16 * 16)
            for g, (dst, srcs) in enumerate(stages):
                if g >= 4:
                    pe.wait_ge((stage_dve, stage_act)[g % 2], (g - 4) // 2 + 1)
                o = 0
                for src in srcs:
                    kp, n = src.shape
                    m = pe.transpose(quarter[g % 4][0:n, o:o + kp], src, ident[0:kp, 0:kp])
                    o += kp
                m.then_inc(stage_psum, 1)
            for k in range(2):
                pe.wait_ge((stage_dve, stage_act)[k], (len(stages) + 1 - k) // 2)
            pe.wait_ge(w2_in, 16 * 15)
            next_keys()
            next_keys1()
            meet(pe, 0)
            with pe.Fori(0, NB):
                norm_T(0)
                query_parts(0, wq_sb[:, :])
                pe.wait_ge(idxf_ready, 1)
                pe.transpose(quarter[1][:, 0:P], idx_f[:, :, :].rearrange("p s k -> p (s k)"), ident[:, :]).then_inc(idxT_psum, 1)
                pe.wait_ge(idxlo_ready, 1)
                attention0()
                attend_out(0, wo_sb[:, :])
                norm_T(1)
                experts(0)
                norm_T(2)
                query_parts(1, wq1T[:, :])
                attention1()
                attend_out(1, wo1T[:, :])
                norm_T(3)
                experts(1)
                meet(pe, 0)

        @block.scalar
        def _(act):
            steps = Steps(act, act_step)

            def copy(o, i):
                return act.activation(o, i, ACT.Copy)

            def all_queries(b_rdy, b_rd):
                for half in range(2):
                    act.wait_ge(b_rdy, half + 1)
                    copy(qa[:, 4 * half:4 * half + 4, :, :].rearrange("p a s q -> p (a s q)"), bsb[half][:, :]).then_inc(b_rd, 1)

            def pair_queries(p, e, b_rdy, b_rd):
                act.wait_ge(b_rdy, e + 1)
                act.activation(qb[0:SLOT, p % 2, 0, :], bsb[e % 3][0:SLOT, 0:NQ], ACT.Copy)
                copy(qb[SLOT:P, p % 2, 1, :], bsb[e % 3][SLOT:P, 0:NQ]).then_inc(b_rd, 1)

            def evacuate(p, pv, o_rdy, count):
                act.wait_ge(pv, count)
                copy(oT[:, :], ob[:, 0:NQ]).then_inc(o_rdy, 1)

            def combined(p, e, b_rdy, b_rd):
                act.wait_ge(b_rdy, e + 1)
                copy(raw[:, :, 2 * p:2 * p + 2, :].rearrange("p s h d -> p s (h d)"),
                     bs[e % 3][:, 0:NS * 2 * V1].rearrange("p (s n) -> p s n", s=NS)).then_inc(b_rd, 1)

            def attention0():
                all_queries(b_ready, b_read)
                for kind, n in fills0[2:]:
                    e = fill0[kind, n]
                    if kind == "q":
                        pair_queries(n, e, b_ready, b_read)
                    elif kind == "c":
                        if n == NP - 1:
                            evacuate(n, pv_done, oT_ready, NG * NP)
                        combined(n, e, b_ready, b_read)
                    else:
                        act.wait_ge(b_ready, e + 1)
                        if n >= NPS:
                            act.wait_ge(pv_done, group(n - NPS) + 1)
                        p, c = divmod(n, KC)
                        kn = rows(c, NK)
                        act.activation(probs[0:kn, n % NPS, :], bs[e % 3][0:kn, :], ACT.Exp).then_inc(b_read, 1)
                        if c == O_AT and p >= 1:
                            evacuate(p - 1, pv_done, oT_ready, NG * p)

            def attention1():
                all_queries(b1_ready, b1_read)
                for kind, n in fills1[2:]:
                    e = fill1[kind, n]
                    if kind == "q":
                        pair_queries(n, e, b1_ready, b1_read)
                        if n >= 2:
                            evacuate(n - 2, pv1_done, oT1_ready, n - 1)
                    elif kind == "c":
                        if n >= NP - 2:
                            evacuate(n, pv1_done, oT1_ready, n + 1)
                        combined(n, e, b1_ready, b1_read)
                    else:
                        act.wait_ge(b1_ready, e + 1)
                        if n >= NPS:
                            act.wait_ge(pv1_done, (n - NPS) // 2 + 1)
                        act.activation(probs[:, n % NPS, :], bs[e % 3][:, :], ACT.Exp).then_inc(b1_read, 1)

            def next_keys():
                for g in range(4):
                    n = min(MMAX, NK - g * MMAX)
                    act.wait_ge(side_psum, g + 1)
                    copy(ctxT[:, g * MMAX:g * MMAX + n], side_bank[g % 2][:, 0:n]).then_inc(side_act, 1)
                for g in range(4):
                    n = min(MMAX, NK - g * MMAX)
                    act.wait_ge(side_psum, g + 5)
                    act.activation(kf[:, g * MMAX:g * MMAX + n], side_bank[g % 2][:, 0:n], ACT.Identity,
                                   bias=bk_col[:, 0:1]).then_inc(side_act, 1)
                act.wait_ge(side_act, 8)
                copy(kpart[0], kf).then_inc(kp_ready, 1)

            def next_keys1():
                act.wait_ge(side1_psum, 1)
                copy(cT[:, :], side_bank[0][:, 0:NK1]).then_inc(side1_act, 1)
                act.wait_ge(side1_psum, 2)
                copy(kf1, side_bank[1][:, 0:NK1]).then_inc(side1_act, 1)
                act.wait_ge(side1_act, 2)
                copy(kpart1[0], kf1).then_inc(kp1_ready, 1)
                act.wait_ge(side1_psum, 3)
                copy(v1aug[:, :, :, 0:HD], side_bank[0][:, 0:NK1].rearrange("p (c h d) -> p c h d", c=KC1, h=H)).then_inc(side1_act, 1)

            def experts(l):
                nch, ftot = ((NC0, F0), (NC1, F1))[l]
                act.wait_ge(lz_ready[l], 1)
                act.activation(le[:, :, :], lz[:, :, :], ACT.Exp).then_inc(le_ready[l], 1)
                if l == 0:
                    next_keys()
                else:
                    next_keys1()
                for c in range(nch):
                    n = rows(c, ftot)
                    act.wait_ge(gu_ready[l], c + 1)
                    if c >= 3:
                        act.wait_ge(gt_done[l], c - 2)
                    act.activation(th[0:n, c % 3, :], gu_bank[c % 3][0:n, 0:NQ], ACT.Tanh, scale=0.5).then_inc(th_ready[l], 1)

            for g, (dst, srcs) in enumerate(stages):
                if g % 2 == 1:
                    act.wait_ge(stage_psum, g + 1)
                    np_, w = dst.shape
                    copy(dst, quarter[g % 4][0:np_, 0:w]).then_inc(stage_act, 1)
            act.wait_ge(w2_in, 16 * 15)
            act.wait_ge(stage_psum, len(stages))
            next_keys()
            next_keys1()
            meet(act, 1)
            with act.Fori(0, NB):
                attention0()
                experts(0)
                attention1()
                experts(1)
                meet(act, 1)

        @block.vector
        def _(dve):
            def norm(k, src, st):
                for s in range(NS):
                    st.do(dve.bn_stats(stats[:, s, :], src[:, s, :]))
                st.wait()
                for s in range(NS):
                    m = dve.bn_aggr(mv[:, s, :], stats[:, s, :])
                m.then_inc(mv_ready, 1)
                dve.wait_ge(rstd_ready, k + 1)
                for s in range(NS):
                    m = dve.tensor_scalar(xn[:, s, :], src[:, s, :], mv[:, s, 0:1], rstd[:, s, :], ALU.subtract, ALU.mult)
                m.then_inc(ln_ready, 1)
                dve.wait_ge(xT_psum, k + 1)
                dve.tensor_copy(xnT[:, :], quarter[0][:, 0:NQ]).then_inc(xT_ready, 1)

            def query_parts(layer, st):
                st.link(dve.memset(qst[:, :, :, KROWS:MROWS], 0.0))
                dve.wait_ge(q_psum, layer + 1)
                src = quarter[2][:, 0:NQ].rearrange("p (s h d) -> p s h d", s=NS, h=H)
                if layer == 0:
                    st.link(dve.scalar_tensor_tensor(out=qs[:, :, :, :].rearrange("p s h d -> p s (h d)"),
                                                     in0=quarter[2][:, 0:NQ].rearrange("p (s n) -> p s n", s=NS), scalar=SCALE,
                                                     in1=bqs[:, :].unsqueeze(1).to_broadcast([P, NS, D]),
                                                     op0=ALU.mult, op1=ALU.add))
                else:
                    st.link(dve.tensor_scalar(qs[:, :, :, :], src, SCALE, None, ALU.mult))
                st.link(dve.tensor_copy(qst[:, :, :, 0:8], qs[:, :, :, :]))
                st.link(dve.tensor_tensor(qres[:, :, :, :], qs[:, :, :, :], qst[:, :, :, 0:8], ALU.subtract))
                st.link(dve.tensor_copy(qst[:, :, :, 8:16], qres[:, :, :, :]))
                st.do(dve.tensor_tensor(qst[:, :, :, 16:24], qres[:, :, :, :], qst[:, :, :, 8:16], ALU.subtract))
                st.do(dve.tensor_copy(qst[:, :, :, 24:40], qst[:, :, :, 0:16]))
                dve.tensor_copy(qst[:, :, :, 40:48], qst[:, :, :, 0:8]).then_inc(qst_ready, 1)

            def attend_out(layer, xin, xout, st):
                dve.wait_ge((b_read, b1_read)[layer], (len(fills0), len(fills1))[layer])
                st.link(dve.reciprocal(rec[:, :, :], raw[:, :, :, HD]))
                dve.tensor_tensor(att[:, :, :, :], raw[:, :, :, 0:HD], rec[:, :, :].unsqueeze(3).to_broadcast([P, NS, H, HD]),
                                  ALU.mult).then_inc(at_ready, 1)
                dve.wait_ge(atT_psum, layer + 1)
                dve.tensor_copy(attT[:, :], quarter[0][:, 0:NQ]).then_inc(atT_ready, 1)
                dve.wait_ge(o_psum, layer + 1)
                dve.tensor_tensor(xout[:, :, :], quarter[2][:, 0:NQ].rearrange("p (s d) -> p s d", s=NS), xin[:, :, :],
                                  ALU.add).then_inc(x_ready, 1)
                dve.wait_ge(x_ready, 2 * layer + 1)

            def attention0():
                def join(p):
                    dve.wait_ge(half_read, 8 * (p + 1))
                    if p >= 2:
                        dve.wait_ge(m_ready, p - 1)
                    dve.tensor_tensor(nm[:, p % 2, :, :], mx[:, p % 2, :, :, 0], mx[:, p % 2, :, :, 1], ALU.min).then_inc(nm_ready, 1)

                for k in range(NH0):
                    u, half = divmod(k, 2)
                    p, r = divmod(u, 4)
                    hh, s = divmod(r, 2)
                    dve.wait_ge(half_ready, k + 1)
                    if k % 8 == 0 and p >= 2:
                        dve.wait_ge(nm_ready, p - 1)
                    n = min(1024, NK - half * 1024)
                    dve.tensor_reduce(mx[:, p % 2, s, hh, half:half + 1], (a0, a1)[half][:, 0:n], AX, ALU.max,
                                      negate=True).then_inc(half_read, 1)
                    if k % 8 == 7:
                        join(p)
                    if k % 8 < NHV:
                        q = 16 * p + k % 8
                        m = dve.tensor_scalar(onehot[:, q, :], iotab[:, :], idx_lo[:, q:q + 1], None, ALU.is_equal)
                        if k % 8 == NHV - 1:
                            m.then_inc(onehotv_ready, 1)

            def attention1(st):
                dve.wait_ge(maskq_psum, 1)
                dve.tensor_copy(maskq[:, :, :].rearrange("p s k -> p (s k)"), ob[:, :].bitcast(bf16)[:, 0:NS * NK1]).then_inc(maskq_ready, 1)
                for p in range(NP + 1):
                    if p < NP:
                        dve.wait_ge(pair_ready, p + 1)
                        dve.tensor_reduce(mx1[:, p, :, :].rearrange("p h s -> p (h s)"), (a0, a1)[p % 2][:, :].rearrange("p (n k) -> p n k", k=NK1),
                                          AX, ALU.max, negate=True).then_inc(pair_read, 1)
                    if p >= 1:
                        x = 2 * (p - 1)
                        dve.wait_ge(b1_read, fill1["e", x] + 1)
                        dve.tensor_tensor(pair_rows(x), pair_rows(x),
                                          cntT[:, 0, :].unsqueeze(1).to_broadcast([P, 2, NQ]), ALU.mult).then_inc(mulv, 1)

            def routing(l, st):
                dve.wait_ge(gate_psum[l], 1)
                g = bs[0][:, 0:NS * NE].rearrange("p (s e) -> p s e", s=NS)
                if l == 0:
                    st.link(dve.tensor_tensor(ls[:, :, :], g, gb_bc[:, :].unsqueeze(1).to_broadcast([P, NS, NE]), ALU.add))
                    dve.tensor_scalar(lz[:, :, :], ls[:, :, :], -1.0, None, ALU.mult).then_inc(lz_ready[l], 1)
                    dve.wait_ge(le_ready[l], 1)
                    st.link(dve.tensor_scalar(lz[:, :, :], le[:, :, :], 1.0, None, ALU.add))
                    st.link(dve.reciprocal(ls[:, :, :], lz[:, :, :]))
                else:
                    st.link(dve.tensor_reduce(lneg[:, :], g[:, :, 0:8], AX, ALU.max, negate=True))
                    dve.tensor_tensor(lz[:, :, 0:8], g[:, :, 0:8], lneg[:, :].unsqueeze(2).to_broadcast([P, NS, 8]), ALU.add)
                    dve.tensor_scalar(lz[:, :, 8:9], g[:, :, 8:9], -1.0, None, ALU.mult).then_inc(lz_ready[l], 1)
                    dve.wait_ge(le_ready[l], 1)
                    st.link(dve.tensor_reduce(lsum[:, :], le[:, :, 0:8], AX, ALU.add))
                    st.link(dve.reciprocal(lrec[:, :], lsum[:, :]))
                    st.link(dve.tensor_tensor(ls[:, :, 0:8], le[:, :, 0:8], lrec[:, :].unsqueeze(2).to_broadcast([P, NS, 8]), ALU.mult))
                    st.link(dve.tensor_scalar(lz[:, :, 8:9], le[:, :, 8:9], 1.0, None, ALU.add))
                n = (NE, 8)[l]
                for s in range(NS):
                    st.do(dve.max(top[:, s, :], ls[:, s, 0:n]))
                st.wait()
                for s in range(NS):
                    st.do(dve.max_index(topi[:, s, :], top[:, s, :], ls[:, s, 0:n]))
                st.do(dve.tensor_tensor(wden[:, :], top[:, :, 0], top[:, :, 1], ALU.add))
                st.wait()
                if l == 0:
                    st.link(dve.tensor_scalar(wden[:, :], wden[:, :], 1e-20, None, ALU.add))
                st.do(dve.tensor_copy(topf[:, :, :], topi[:, :, :]))
                st.link(dve.reciprocal(wrec[:, :], wden[:, :]))
                st.link(dve.tensor_tensor(wtop[:, :, :], top[:, :, 0:2], wrec[:, :].unsqueeze(2).to_broadcast([P, NS, 2]), ALU.mult))
                for s in range(NS):
                    st.do(dve.tensor_scalar(cw[:, s, 0:n], iota_f[:, 0:n], topf[:, s, 0:1], wtop[:, s, 0:1], ALU.is_equal, ALU.mult))
                    st.do(dve.tensor_scalar(cw2[:, s, 0:n], iota_f[:, 0:n], topf[:, s, 1:2], wtop[:, s, 1:2], ALU.is_equal, ALU.mult))
                st.wait()
                st.do(dve.tensor_tensor(cwr[:, :, 0:n], cw[:, :, 0:n], cw2[:, :, 0:n], ALU.add))
                if l == 1:
                    st.do(dve.reciprocal(cwr[:, :, 8:9], lz[:, :, 8:9]))
                st.wait()
                st.link(dve.tensor_scalar(cw[:, :, :], cwr[:, :, :], 0.5, None, ALU.mult))
                st.link(dve.tensor_copy(cwp[:, :, 0:NE], cw[:, :, :]))
                st.link(dve.tensor_tensor(cwr[:, :, :], cw[:, :, :], cwp[:, :, 0:NE], ALU.subtract))
                st.link(dve.tensor_copy(cwp[:, :, CWP:CWP + NE], cwr[:, :, :]))
                dve.tensor_tensor(cwp[:, :, 2 * CWP:2 * CWP + NE], cwr[:, :, :], cwp[:, :, CWP:CWP + NE], ALU.subtract).then_inc(cwp_ready[l], 1)

            def next_values():
                for g in range(4):
                    dve.wait_ge(side_psum, g + 9)
                    nc_ = min(4, KC - 4 * g)
                    kn = min(P, NK - 4 * g * P)
                    dve.tensor_tensor(vaug[0:kn, 4 * g:4 * g + nc_, :, 0:HD],
                                      side_bank[g % 2][0:kn, 0:nc_ * P].rearrange("p (c h d) -> p c h d", c=nc_, h=H),
                                      bv_bc[0:kn, :].rearrange("p (h d) -> p h d", d=HD).unsqueeze(1).to_broadcast([kn, nc_, H, HD]),
                                      ALU.add).then_inc(side_dve, 1)

            def take_counts(st):
                dve.wait_ge(cnt_psum, 1)
                for s in range(NS):
                    st.do(dve.tensor_copy(cntT[:, :, s * P:(s + 1) * P].rearrange("p c q -> p q c"),
                                          cnt_bank[s][:, 0:P * KC1].rearrange("p (q c) -> p q c", c=KC1)))
                st.wait()
                dve.tensor_scalar(maskT[:, :, :], cntT[:, :, :], 0.0, NEG, ALU.is_equal, ALU.mult).then_inc(cnt_ready, 1)

            def experts(l, xin, xout, st):
                nch, ftot = ((NC0, F0), (NC1, F1))[l]
                routing(l, st)
                if l == 0:
                    take_counts(st)
                    next_values()
                dve.wait_ge(cwT_psum[l], 1)
                dve.tensor_copy(cwT[:, :], bsb[1][0:CWR, 0:NQ]).then_inc(cwT_ready[l], 1)

                def hidden(c):
                    n = rows(c, ftot)
                    dve.wait_ge(hu_done[l], c + 1)
                    dve.wait_ge(cb_ready[l], c + 1)
                    if c >= 4:
                        dve.wait_ge(down_done[l], c - 3)
                    dve.tensor_tensor(hid[0:n, c % 4, :], hu[0:n, c % 3, :], cb_bank[c % 2][0:n, 0:NQ], ALU.mult).then_inc(hid_ready[l], 1)

                for c in range(nch):
                    n = rows(c, ftot)
                    g = gu_bank[c % 3]
                    dve.wait_ge(th_ready[l], c + 1)
                    dve.scalar_tensor_tensor(out=gt[0:n, c % 3, :], in0=th[0:n, c % 3, :], scalar=1.0, in1=g[0:n, 0:NQ],
                                             op0=ALU.add, op1=ALU.mult).then_inc(gt_done[l], 1)
                    if c >= 1:
                        hidden(c - 1)
                    dve.wait_ge(gt_done[l], c + 1)
                    dve.tensor_tensor(hu[0:n, c % 3, :], gt[0:n, c % 3, :], g[0:n, NQ:2 * NQ], ALU.mult).then_inc(hu_done[l], 1)
                hidden(nch - 1)
                dve.wait_ge(down_done[l], nch)
                if l == 1:
                    dve.wait_ge(xo_free, 1)
                dve.tensor_tensor(xout[:, :, :], ob[:, 0:NQ].rearrange("p (s d) -> p s d", s=NS), xin[:, :, :], ALU.add).then_inc(x_ready, 1)
                dve.wait_ge(x_ready, 2 * l + 2)

            st = Steps(dve, dve_step)
            for g, (dst, srcs) in enumerate(stages):
                if g % 2 == 0:
                    dve.wait_ge(stage_psum, g + 1)
                    np_, w = dst.shape
                    dve.tensor_copy(dst, quarter[g % 4][0:np_, 0:w]).then_inc(stage_dve, 1)
            dve.wait_ge(stage_psum, len(stages))
            dve.memset(kst[:, :, :], 1.0).then_inc(kst_one, 1)
            dve.memset(k1st[:, :, :], 1.0).then_inc(kst_one, 1)
            dve.memset(gb_bc[:, 0:8], 0.0).then_inc(pre_dve, 1)
            dve.memset(vaug[:, :, :, :], 1.0).then_inc(pre_dve, 1)
            dve.memset(v1aug[:, :, :, HD:V1], 1.0).then_inc(pre_dve, 1)
            dve.memset(qst[:, :, :, :], 0.0).then_inc(pre_dve, 1)
            dve.memset(cwp[:, :, :], 0.0).then_inc(pre_dve, 1)
            dve.memset(qb[:, :, :, :], 0.0).then_inc(pre_dve, 1)
            dve.memset(neg_half[:, :, :], -0.5).then_inc(pre_dve, 1)
            dve.memset(ob[:, :], 0.0).then_inc(pre_dve, 1)
            dve.wait_ge(w2_in, 16 * 15)
            dve.wait_ge(pre_dve, 8)
            dve.tensor_scalar(bqs[:, :], bqs[:, :], SCALE, None, ALU.mult)
            next_values()
            meet(dve, 2)
            with dve.Fori(0, NB):
                st = Steps(dve, dve_step)
                norm(0, xs[0], st)
                query_parts(0, st)
                dve.tensor_copy(idx_f[:, :, :], idx_i[:, :, :]).then_inc(idxf_ready, 1)
                st.do(dve.tensor_tensor(x0b[:, :, :], xs[0][:, :, :], bo_bc[:, :].unsqueeze(1).to_broadcast([P, NS, D]), ALU.add))
                dve.wait_ge(idxT_psum, 1)
                st.do(dve.tensor_scalar(idx_c[:, :, 0], quarter[1][:, 0:P], float(P), None, ALU.is_lt))
                st.do(dve.tensor_scalar(idx_c[:, :, 1], quarter[1][:, 0:P], float(P), None, ALU.is_ge))
                st.do(dve.tensor_scalar(idx_hi[:, :], quarter[1][:, 0:P], float(P), None, ALU.is_ge))
                st.wait()
                dve.scalar_tensor_tensor(out=idx_lo[:, :], in0=idx_hi[:, :], scalar=-float(P), in1=quarter[1][:, 0:P],
                                         op0=ALU.mult, op1=ALU.add).then_inc(idxlo_ready, 1)
                attention0()
                attend_out(0, x0b, xs[1], st)
                norm(1, xs[1], st)
                experts(0, xs[1], xs[2], st)
                norm(2, xs[2], st)
                query_parts(1, st)
                attention1(st)
                attend_out(1, xs[2], xs[3], st)
                norm(3, xs[3], st)
                experts(1, xs[3], xs[4], st)
                meet(dve, 2)

        @block.gpsimd
        def _(pool):
            def rstd_of(k, st):
                pool.wait_ge(mv_ready, k + 1)
                st.link(pool.tensor_scalar(veps[:, :, :], mv[:, :, 1:2], EPS, None, ALU.add))
                pool.tensor_tensor(rstd[:, :, :], veps[:, :, :], neg_half[:, :, :], ALU.pow).then_inc(rstd_ready, 1)

            def max_parts(src, p, ready, st):
                def col(t):
                    return qst[:, :, 2 * p:2 * p + 2, KROWS + t]
                st.link(pool.tensor_copy(col(0), src))
                st.link(pool.tensor_tensor(nmr[:, :, :], src, col(0), ALU.subtract))
                st.link(pool.tensor_copy(col(1), nmr[:, :, :]))
                pool.tensor_tensor(col(2), nmr[:, :, :], col(1), ALU.subtract).then_inc(ready, 1)
                pool.wait_ge(ready, p + 1)

            def attention0(st):
                pool.wait_ge(idxlo_ready, 1)
                for p in range(NP):
                    pool.wait_ge(nm_ready, p + 1)
                    max_parts(nm[:, p % 2, :, :], p, m_ready, st)
                    for q in range(16 * p + NHV, 16 * p + 16):
                        m = pool.tensor_scalar(onehot[:, q, :], iotab[:, :], idx_lo[:, q:q + 1], None, ALU.is_equal)
                    m.then_inc(onehot_ready, 1)

            def attention1(st):
                for p in range(NP + 1):
                    if p < NP:
                        pool.wait_ge(pair_read, p + 1)
                        max_parts(mx1[:, p, :, :].rearrange("p h s -> p s h"), p, m1_ready, st)
                    if p >= 1:
                        x = 2 * (p - 1) + 1
                        pool.wait_ge(b1_read, fill1["e", x] + 1)
                        pool.tensor_tensor(pair_rows(x), pair_rows(x),
                                          cntT[:, 1, :].unsqueeze(1).to_broadcast([P, 2, NQ]), ALU.mult).then_inc(mulp, 1)

            def split(src, res, parts, ready, res_ready):
                pool.wait_ge(ready, 1)
                pool.tensor_tensor(res, src, parts[0], ALU.subtract).then_inc(res_ready, 1)
                pool.wait_ge(res_ready, 1)
                pool.tensor_copy(parts[1], res).then_inc(ready, 1)
                pool.wait_ge(ready, 2)
                pool.tensor_tensor(parts[2], res, parts[1], ALU.subtract).then_inc(ready, 1)
                pool.wait_ge(ready, 3)

            def next_keys():
                split(kf, kres, kpart, kp_ready, kres_ready)

            def next_keys1():
                split(kf1, kres1, kpart1, kp1_ready, kres1_ready)

            st = Steps(pool, pool_step)
            st.do(pool.memset(ident[:, :], 0.0))
            st.do(pool.memset(identb[:, :], 0.0))
            st.do(pool.iota(iota_i[:, :], pattern=[[1, P]], base=0, channel_multiplier=0))
            st.wait()
            pool.affine_select(out=ident[:, :], in_=ident[:, :], compare_op=ALU.not_equal, fill=1.0, base=0,
                               pattern=[[-1, P]], channel_multiplier=1).then_inc(const_ready, 1)
            pool.affine_select(out=identb[:, :], in_=identb[:, :], compare_op=ALU.not_equal, fill=1.0, base=0,
                               pattern=[[-1, P]], channel_multiplier=1).then_inc(const_ready, 1)
            st.do(pool.tensor_copy(iota_f[:, :], iota_i[:, :]))
            st.do(pool.tensor_copy(iotab[:, :], iota_i[:, :]))
            st.link(pool.memset(comb[:, :], 0.0))
            for t in range(4):
                part = comb[QD * t:QD * (t + 1), V1 * (t // 2):V1 * (t // 2 + 1)]
                st.link(pool.affine_select(out=part, in_=part, compare_op=ALU.not_equal, fill=1.0, base=0,
                                           pattern=[[-1, V1]], channel_multiplier=1))
            for l, width, ftot in ((0, I0, F0), (1, I1, F1)):
                st.link(pool.memset(sel[l][:, :], 0.0))
                for t in range(3):
                    part = sel[l][CWP * t:CWP * t + NE, :]
                    st.link(pool.memset(part, 1.0))
                    st.link(pool.affine_select(out=part, in_=part, compare_op=ALU.is_ge, fill=0.0, base=0,
                                               pattern=[[1, ftot]], channel_multiplier=-width))
                    st.link(pool.affine_select(out=part, in_=part, compare_op=ALU.is_ge, fill=0.0, base=width - 1,
                                               pattern=[[-1, ftot]], channel_multiplier=width))
            next_keys()
            next_keys1()
            meet(pool, 3)
            with pool.Fori(0, NB):
                st = Steps(pool, pool_step)
                rstd_of(0, st)
                attention0(st)
                rstd_of(1, st)
                next_keys()
                rstd_of(2, st)
                attention1(st)
                rstd_of(3, st)
                next_keys1()
                meet(pool, 3)


_INS = ['x', 'ctx_1024', 'itok_BxSx64_0_2047', 'L0_xattn_Wq', 'L0_xattn_bq', 'L0_xattn_Wkv', 'L0_xattn_bkv', 'L0_xattn_Wo',
        'L0_xattn_bo', 'L0_ffn_w1', 'L0_ffn_w2', 'L0_ffn_w3', 'L0_ffn_new_w1', 'L0_ffn_new_w2', 'L0_ffn_new_w3',
        'L0_ffn_gate_weight', 'L0_ffn_new_gate_weight', 'L0_ffn_gate_bias', 'L1_xattn_W_q', 'L1_xattn_W_kv_down',
        'L1_xattn_W_kv_up', 'L1_xattn_W_out', 'L1_ffn_gate_w', 'L1_ffn_w_gate', 'L1_ffn_w_up', 'L1_ffn_w_down',
        'L1_ffn_sw_gate', 'L1_ffn_sw_up', 'L1_ffn_sw_down', 'L1_ffn_shared_gate_w']


def kernel(**inputs):
    import numpy as _np
    import concourse.bacc as _bacc
    from concourse.bass_utils import run_bass_kernel_spmd as _run

    nc = _bacc.Bacc("TRN2", target_bir_lowering=False, num_devices=1)
    arrays, args = {}, []
    for name in _INS:
        a = _np.ascontiguousarray(inputs[name])
        arrays[f"in_{name}"] = a
        args.append(nc.dram_tensor(f"in_{name}", a.shape, mybir.dt.from_np(a.dtype), kind="ExternalInput").ap())
    args.append(nc.dram_tensor("out_0", (NB, NQ, D), mybir.dt.float32, kind="ExternalOutput").ap())
    build(nc, *args)
    r = _run(nc, [arrays], core_ids=[0])
    return r.results[0]["out_0"]
```

```python
import numpy as np

import concourse.bass as bass
from concourse import mybir
from contextlib import ExitStack

P = 128
NB, NQ, D = 8, 256, 128
NS = NQ // P
NK = 1601
NK1 = 256
NIDX = 64
H, HD = 16, 8
NP = H // 2
SLOT = 64
KC = (NK + P - 1) // P
KLAST = NK - (KC - 1) * P
KC1 = NK1 // P
V1 = HD + 1
QPART = (0, 1, 2, 0, 1, 0)
KPART = (0, 0, 0, 1, 1, 2)
NT = len(QPART)
KROWS = NT * HD
MROWS = KROWS + 3
SCALE = float(HD) ** -0.5
EPS = 1e-5
NE = 9
I0, I1 = 352, 176
F0, F1 = NE * I0, NE * I1
NC0, NC1 = (F0 + P - 1) // P, (F1 + P - 1) // P
NEG = -1e30
CWP = 32
CWR = 2 * CWP + NE
NPS = 6
NHV = 6
QD = 32
TWO_ONES = float(np.array([1.0, 1.0], np.float32).view(np.uint16)[1::2].copy().view(np.float32)[0])
NM = 4
KM = (NK + NM - 1) // NM
MMAX = 512


def rows(c, total):
    return min(P, total - c * P)


def build(nc, x, ctx_in, itok, Wq, bq, Wkv, bkv, Wo, bo, w1, w2, w3, nw1, nw2, nw3, gw, ngw, gb,
          Wq1, Wd1, Wu1, Wout1, gw1, wg, wu, wd, swg, swu, swd, sgw, out):
    f32, bf16, i32, u32 = mybir.dt.float32, mybir.dt.bfloat16, mybir.dt.int32, mybir.dt.uint32
    ALU, ACT, AX = mybir.AluOpType, mybir.ActivationFunctionType, mybir.AxisListType.X
    k_parts = nc.dram_tensor("k_parts", [3, P, NK], bf16, kind="Internal").ap()
    k1_parts = nc.dram_tensor("k1_parts", [3, P, NK1], bf16, kind="Internal").ap()

    with ExitStack() as es:
        def sb(name, shape, dt=f32):
            return es.enter_context(nc.sbuf_tensor(name, shape, dt))

        def psum(name, width):
            return es.enter_context(nc.psum_tensor(name, [P, width], f32))

        wq_sb, wkv_sb, wo_sb = sb("wq_sb", [P, D]), sb("wkv_sb", [P, 2 * D]), sb("wo_sb", [P, D])
        wq1T, wd1T, wu1T, wo1T = sb("wq1T", [P, D]), sb("wd1T", [P, D]), sb("wu1T", [P, 2 * D]), sb("wo1T", [P, D])
        bqs = sb("bqs", [P, D])
        bo_bc = sb("bo_bc", [P, D])
        bk_col, bv_col = sb("bk_col", [P, 1]), sb("bv_col", [P, 1])
        gb_bc = sb("gb_bc", [P, NE])
        gT = [sb("gT0", [P, NE]), sb("gT1", [P, NE])]
        gT_nat = [sb("g_nat0", [NE, P]), sb("g_nat1", [NE, P])]
        w1T, w3T, w2T = sb("w1T", [P, F0]), sb("w3T", [P, F0]), sb("w2T", [P, NC0, D])
        wg_sb, wu_sb, wd_sb = sb("wg_sb", [P, F1]), sb("wu_sb", [P, F1]), sb("wd_sb", [P, NC1, D])
        sel = [sb("sel0", [CWR, F0], bf16), sb("sel1", [CWR, F1], bf16)]
        sq_nat = sb("sq_nat", [P, 5, P])
        ident, identb = sb("ident", [P, P]), sb("identb", [P, P], bf16)
        iota_i, iota_f, iotab = sb("iota_i", [P, P], i32), sb("iota_f", [P, P]), sb("iotab", [P, P], bf16)
        comb = sb("comb", [P, 2 * V1])
        xs = [sb(f"x{k}", [P, NS, D]) for k in range(5)]
        x0b = sb("x0b", [P, NS, D])
        xn, xnT = sb("xn", [P, NS, D]), sb("xnT", [P, NQ])
        stats, mv = sb("stats", [P, NS, 6]), sb("mv", [P, NS, 2])
        veps, rstd, neg_half = (sb(n, [P, NS, 1]) for n in ("veps", "rstd", "neg_half"))
        big = sb("big", [P, 8192])
        onehot = big[:, :].bitcast(bf16).rearrange("p (q r) -> p q r", r=P)
        kf, kres = big[:, 0:NK], big[:, 1602:1602 + NK]
        kpart = [big[:, 3204 + 802 * t:3204 + 802 * (t + 1)].bitcast(bf16)[:, 0:NK] for t in range(3)]
        w1_nat = big[:, 0:NC0 * P].rearrange("p (c d) -> p c d", d=P)
        w3_nat = big[:, 4096:4096 + NC0 * P].rearrange("p (c d) -> p c d", d=P)
        kst = sb("kst", [P, NP, NK + 1], bf16)
        w2_nat = kst[:, :, :].rearrange("p a k -> p (a k)").bitcast(f32)[:, 0:F0]
        k1st = sb("k1st", [P, NP, NK1], bf16)
        vaug, v1aug = sb("vaug", [P, KC, H, V1]), sb("v1aug", [P, KC1, H, V1])
        ctx_sb, ctxT = sb("ctx_sb", [P, KC, D]), sb("ctxT", [P, NK])
        cT = sb("cT", [P, NK1])
        kpart1 = [sb(f"kpart1_{t}", [P, NK1], bf16)[:, :] for t in range(3)]
        qs, qres = sb("qs", [P, NS, H, HD]), sb("qres", [P, NS, H, HD])
        qst = sb("qst", [P, NS, H, SLOT], bf16)
        qa = sb("qa", [P, NP, NS, P], bf16)
        qb = sb("qb", [P, 2, 2, NQ], bf16)
        mx = sb("mx", [P, 2, NS, 2, NM])
        mx1 = sb("mx1", [P, NP, 2, NS])
        nm, nmr = sb("nm", [P, 2, NS, 2]), sb("nmr", [P, NS, 2])
        probs = sb("probs", [P, NPS, 512])
        kf1, kres1 = probs[:, 2, 0:NK1], probs[:, 2, NK1:2 * NK1]
        oT = sb("oT", [P, NQ])
        raw = sb("raw", [P, NS, H, V1])
        att, attT = sb("att", [P, NS, H, HD]), sb("attT", [P, NQ])
        rec = sb("rec", [P, NS, H])
        idx_i, idx_f = sb("idx_i", [P, NS, NIDX], i32), sb("idx_f", [P, NS, NIDX])
        idx_t, idx_hi, idx_lo = (sb(n, [P, P]) for n in ("idx_t", "idx_hi", "idx_lo"))
        idx_c = sb("idx_c", [P, P, 2], bf16)
        cntT = sb("cntT", [P, KC1, NQ])
        maskT, maskq = sb("maskT", [P, KC1, NQ], bf16), sb("maskq", [P, NS, NK1], bf16)
        lz, le, ls = sb("lz", [P, NS, NE]), sb("le", [P, NS, NE]), sb("ls", [P, NS, NE])
        lneg, lsum, lrec = sb("lneg", [P, NS]), sb("lsum", [P, NS]), sb("lrec", [P, NS])
        top, topi, topf = sb("top", [P, NS, 8]), sb("topi", [P, NS, 8], u32), sb("topf", [P, NS, 2])
        wden, wrec, wtop = sb("wden", [P, NS]), sb("wrec", [P, NS]), sb("wtop", [P, NS, 2])
        pick = sb("pick", [P, NS, 2, NE])
        cw, cwr = sb("cw", [P, NS, NE]), sb("cwr", [P, NS, NE])
        cwp = sb("cwp", [P, NS, CWR], bf16)
        cwT = sb("cwT", [CWR, NQ], bf16)
        th, gt, hu = (big[:, 5632 + 768 * k:5632 + 768 * (k + 1)].rearrange("p (n q) -> p n q", q=NQ) for k in range(3))
        hid = probs[:, 0:2, :].rearrange("p a (b q) -> p (a b) q", b=2)
        a0, a1 = psum("a0", 1024), psum("a1", 1024)
        bs = [psum(f"b{k}", 512) for k in range(3)]
        ob = psum("ob", 512)
        quarter = [a0[:, 0:512], a0[:, 512:1024], a1[:, 0:512], a1[:, 512:1024]]
        gu_bank = quarter[0:3]
        cb_bank = bs[0:2]
        cnt_bank = [bs[1], ob]
        side_bank = [bs[2][:, :], quarter[3]]
        bsb = [b[:, :].bitcast(bf16) for b in bs]
        all_bank = [(bs[2][:, :].bitcast(bf16), quarter[3].bitcast(bf16)), (bsb[0], bsb[1])]
        norm_bank, q_bank = [quarter[3], quarter[0]], [bs[2][:, :], quarter[2]]

        first_sem = [None]

        def sem(name):
            s = es.enter_context(nc.semaphore(name))
            if first_sem[0] is None:
                first_sem[0] = s.num
            last_sem[0] = s.num
            return s
        last_sem = [None]

        ctx_in_s, x_in, idx_in, kst_in, k1st_in = (sem(n) for n in ("ctx_in", "x_in", "idx_in", "kst_in", "k1st_in"))
        kw_done, kw1_done = sem("kw_done"), sem("kw1_done")
        mv_ready, rstd_ready, ln_ready, xT_psum, xT_ready = (sem(n) for n in ("mv_ready", "rstd_ready", "ln_ready", "xT_psum", "xT_ready"))
        q_psum, qst_ready, all_psum, all_read = (sem(n) for n in ("q_psum", "qst_ready", "all_psum", "all_read"))
        at_ready, atT_psum, atT_ready, o_psum, x_ready = (sem(n) for n in ("at_ready", "atT_psum", "atT_ready", "o_psum", "x_ready"))
        part_ready, part_read, nm_ready, m_ready = sem("part_ready"), sem("part_read"), sem("nm_ready"), sem("m_ready")
        b_ready, b_read, pv_done, oT_ready, att_done = (sem(n) for n in ("b_ready", "b_read", "pv_done", "oT_ready", "att_done"))
        pair_ready, pair_read, m1_ready = sem("pair_ready"), sem("pair_read"), sem("m1_ready")
        b1_ready, b1_read, pv1_done, oT1_ready = (sem(n) for n in ("b1_ready", "b1_read", "pv1_done", "oT1_ready"))
        mulv, mulp = sem("mulv"), sem("mulp")
        idxf_ready, idxT_psum, idxt_ready, qres_ready, onehot_ready, onehotv_ready, cnt_psum, cnt_ready, maskq_psum, maskq_ready = (
            sem(n) for n in ("idxf_ready", "idxT_psum", "idxt_ready", "qres_ready", "onehot_ready", "onehotv_ready", "cnt_psum", "cnt_ready", "maskq_psum", "maskq_ready"))
        gate_psum, lz_ready, le_ready, cwp_ready, cwT_psum, cwT_ready = (
            [sem(f"{n}{k}") for k in range(2)] for n in ("gate_psum", "lz_ready", "le_ready", "cwp_ready", "cwT_psum", "cwT_ready"))
        gu_ready, th_ready, gt_done, hu_done, cb_ready, hid_ready, down_done = (
            [sem(f"{n}{k}") for k in range(2)] for n in ("gu_ready", "th_ready", "gt_done", "hu_done", "cb_ready", "hid_ready", "down_done"))
        ctxT_psum, ctxT_ready, side_psum, side_act = (sem(n) for n in ("ctxT_psum", "ctxT_ready", "side_psum", "side_act"))
        side1_psum, side1_act = sem("side1_psum"), sem("side1_act")
        kp_ready, kres_ready, kp1_ready, kres1_ready = sem("kp_ready"), sem("kres_ready"), sem("kp1_ready"), sem("kres1_ready")
        dve_step, pool_step = sem("dve_step"), sem("pool_step")
        w_in, w2_in, stage_psum, stage_dve, stage_act, const_ready, pre_dve, kst_one, pre_bv, pre_psum, pre_bo, sel_zero, sel_part, sel_done = (
            sem(n) for n in ("w_in", "w2_in", "stage_psum", "stage_dve", "stage_act", "const_ready", "pre_dve", "kst_one", "pre_bv", "pre_psum", "pre_bo", "sel_zero", "sel_part", "sel_done"))
        xo_free = sem("xo_free")
        met = sem("met")
        round_sems = range(first_sem[0], last_sem[0] + 1)
        go = [sem(f"go{k}") for k in range(4)]
        out_stored = sem("out_stored")

        def meet(eng, k):
            eng.drain().then_inc(met, 1)
            eng.wait_ge(go[k], 1)
            eng.sem_clear(go[k])

        class Steps:

            def __init__(self, eng, s):
                self.eng, self.s, self.n = eng, s, 0

            def do(self, ins):
                self.n += 1
                ins.then_inc(self.s, 1)

            def wait(self):
                self.eng.wait_ge(self.s, self.n)

            def link(self, ins):
                self.do(ins)
                self.wait()

        block = es.enter_context(nc.Block())

        w1b = [(w1T, w1_nat), (w3T, w3_nat)]
        stages = []
        for dst, nat in w1b:
            for c in range(0, NC0, 4):
                src = [nat[0:rows(k, F0), k, :] for k in range(c, min(c + 4, NC0))]
                width = sum(rows(k, F0) for k in range(c, min(c + 4, NC0)))
                stages.append((dst[:, c * P:c * P + width], src))
        for c in range(0, NC0 - 1, 4):
            stages.append((w2T[:, c:c + 4, :].rearrange("p c d -> p (c d)"), [w2_nat[:, k * P:(k + 1) * P] for k in range(c, c + 4)]))
        stages.append((w2T[0:rows(NC0 - 1, F0), NC0 - 1, :], [w2_nat[:, (NC0 - 1) * P:F0]]))
        for dst, k in ((wq1T, 0), (wd1T, 1), (wo1T, 4)):
            stages.append((dst[:, :], [sq_nat[:, k, :]]))
        stages.append((wu1T[:, :], [sq_nat[:, 2, :], sq_nat[:, 3, :]]))
        for k in range(2):
            stages.append((gT[k][:, :], [gT_nat[k][:, :]]))

        @block.sync
        def _(sp):
            def load_x(b):
                sp.dma_start(xs[0][:, :, :], x[b].rearrange("a (s p) d -> p (a s) d", p=P)).then_inc(x_in, 16)
                sp.dma_start(idx_i[:, :, :], itok[b].rearrange("a (s p) k -> p (a s) k", p=P)).then_inc(idx_in, 16)

            def load_ctx(b):
                sp.dma_start(ctx_sb[:, 0:KC - 1, :],
                             ctx_in[b, 0:(KC - 1) * P, :].rearrange("a (c p) d -> p (a c) d", p=P)).then_inc(ctx_in_s, 16)
                sp.dma_start(ctx_sb[0:KLAST, KC - 1, :],
                             ctx_in[b, (KC - 1) * P:NK, :].rearrange("a k d -> (a k) d")).then_inc(ctx_in_s, 16)

            def spread(parts, scratch, dst, done, filled, ready):
                for t in range(3):
                    sp.wait_ge(ready, t + 1)
                    sp.dma_start(scratch[t], parts[t]).then_inc(done, 16)
                    sp.wait_ge(done, 16 * (t + 1))
                    src = scratch[t].rearrange("(a h d) k -> h d a k", h=2, d=HD)
                    for hh in range(2):
                        for term in range(NT):
                            if KPART[term] == t:
                                r = SLOT * hh + HD * term
                                sp.dma_start(dst[r:r + HD, :, 0:src.shape[3]], src[hh]).then_inc(filled, 16)

            sp.dma_start(w1_nat[:, 0:22, :], w1.rearrange("e i d -> (e i) d").rearrange("(c p) d -> p c d", p=P)).then_inc(w_in, 16)
            sp.dma_start(w1_nat[:, 22:24, :], nw1[0, 0:256, :].rearrange("(c p) d -> p c d", p=P)).then_inc(w_in, 16)
            sp.dma_start(w1_nat[0:96, 24, :], nw1[0, 256:I0, :]).then_inc(w_in, 16)
            sp.dma_start(w3_nat[:, 0:22, :], w3.rearrange("e i d -> (e i) d").rearrange("(c p) d -> p c d", p=P)).then_inc(w_in, 16)
            sp.dma_start(w3_nat[:, 22:24, :], nw3[0, 0:256, :].rearrange("(c p) d -> p c d", p=P)).then_inc(w_in, 16)
            sp.dma_start(w3_nat[0:96, 24, :], nw3[0, 256:I0, :]).then_inc(w_in, 16)
            sp.dma_start(w2_nat[:, 0:8 * I0].rearrange("p (e i) -> p e i", i=I0), w2.rearrange("e d i -> d e i")).then_inc(w_in, 16)
            sp.dma_start(w2_nat[:, 8 * I0:F0], nw2[0]).then_inc(w_in, 16)
            sp.dma_start(sq_nat[:, 0, :], Wq1).then_inc(w_in, 16)
            sp.dma_start(sq_nat[:, 1, :], Wd1).then_inc(w_in, 16)
            sp.dma_start(sq_nat[:, 2:4, :], Wu1.rearrange("(c p) d -> p c d", p=P)).then_inc(w_in, 16)
            sp.dma_start(sq_nat[:, 4, :], Wout1).then_inc(w_in, 16)
            for k, (a, b) in enumerate(((gw, ngw), (gw1, sgw))):
                sp.dma_start(gT_nat[k][0:8, :], a).then_inc(w_in, 16)
                sp.dma_start(gT_nat[k][8:9, :], b).then_inc(w_in, 16)
            load_ctx(slice(0, 1))
            sp.dma_start(wkv_sb[:, :], Wkv).then_inc(w2_in, 16)
            sp.dma_start(bk_col[:, :], bkv[0:D].rearrange("(p a) -> p a", a=1)).then_inc(w2_in, 16)
            sp.dma_start(bv_col[:, :], bkv[D:2 * D].rearrange("(p a) -> p a", a=1)).then_inc(w2_in, 16)
            sp.dma_start(bo_bc[:, :], bo.partition_broadcast(P)).then_inc(w2_in, 16)
            sp.dma_start(bqs[:, :], bq.partition_broadcast(P)).then_inc(w2_in, 16)
            sp.dma_start(gb_bc[:, 8:9], gb.partition_broadcast(P)).then_inc(w2_in, 16)
            sp.dma_start(wq_sb[:, :], Wq).then_inc(w2_in, 16)
            sp.dma_start(wo_sb[:, :], Wo).then_inc(w2_in, 16)
            load_x(slice(0, 1))
            for dst, a, b in ((wg_sb, wg, swg), (wu_sb, wu, swu)):
                sp.dma_start(dst[:, 0:8 * I1].rearrange("p (e i) -> p e i", i=I1), a.rearrange("e d i -> d e i")).then_inc(w2_in, 16)
                sp.dma_start(dst[:, 8 * I1:F1], b).then_inc(w2_in, 16)
            sp.dma_start(wd_sb[:, 0:11, :], wd.rearrange("e i d -> (e i) d").rearrange("(c p) d -> p c d", p=P)).then_inc(w2_in, 16)
            sp.dma_start(wd_sb[:, 11, :], swd[0:P, :]).then_inc(w2_in, 16)
            sp.dma_start(wd_sb[0:I1 - P, 12, :], swd[P:I1, :]).then_inc(w2_in, 16)
            sp.wait_ge(ctxT_ready, 4)
            load_ctx(slice(1, 2))
            sp.wait_ge(kst_one, 2)
            spread(kpart, k_parts, kst, kw_done, kst_in, kp_ready)
            spread(kpart1, k1_parts, k1st, kw1_done, k1st_in, kp1_ready)

            def close():
                sp.wait_ge(kst_in, 16 * 2 * NT)
                sp.wait_ge(k1st_in, 16 * 2 * NT)
                sp.wait_ge(x_in, 16)
                sp.wait_ge(idx_in, 16)
                sp.wait_ge(ctx_in_s, 32)
                sp.wait_ge(met, 4)
                sp.sem_clear(round_sems)
                for g in go:
                    sp.sem_inc(g, 1)

            sp.wait_ge(w2_in, 16 * 15)
            sp.wait_ge(ctx_in_s, 64)
            close()
            sp.sem_inc(out_stored, 16)
            with sp.Fori(0, NB) as i:
                nxt = bass.ds((i + 1) % NB, 1)
                sp.wait_ge(ctxT_ready, 4)
                load_ctx(bass.ds((i + 2) % NB, 1))
                sp.wait_ge(x_ready, 1)
                sp.wait_ge(cnt_psum, 1)
                load_x(nxt)
                sp.wait_ge(out_stored, 16)
                sp.sem_clear(out_stored)
                sp.sem_inc(xo_free, 1)
                sp.wait_ge(att_done, 1)
                spread(kpart, k_parts, kst, kw_done, kst_in, kp_ready)
                sp.wait_ge(att_done, 2)
                spread(kpart1, k1_parts, k1st, kw1_done, k1st_in, kp1_ready)
                sp.wait_ge(x_ready, 4)
                sp.dma_start(out[bass.ds(i, 1)].rearrange("a (s p) d -> p (a s) d", p=P), xs[4][:, :, :]).then_inc(out_stored, 16)
                close()
            sp.wait_ge(out_stored, 16)

        NH0 = NP * NS * NM
        PARTS = NS * NM
        NG = (KC + 1) // 2
        NX, NX1 = NP * KC, NP * KC1
        Q_AT, O_AT, C_AT = KC - 3, 1, 5
        CTX = 2
        START, LEAD, LAG = 10, 12, 3
        fills0 = [("q", 0)]
        for x in range(NX):
            p, c = divmod(x, KC)
            fills0.append(("e", x))
            if c == C_AT and p >= 1:
                fills0.append(("c", p - 1))
            if c == Q_AT and p + 1 < NP:
                fills0.append(("q", p + 1))
        fills0.append(("c", NP - 1))
        fills1 = [("q", 0)]
        for p in range(NP):
            fills1 += [("e", 2 * p), ("e", 2 * p + 1)]
            if p + 1 < NP:
                fills1.append(("q", p + 1))
            if p >= 2:
                fills1.append(("c", p - 2))
        fills1 += [("c", NP - 2), ("c", NP - 1)]
        COUNT = (20, 36, 96, 108)
        fill0, fill1 = ({f: n for n, f in enumerate(fills)} for fills in (fills0, fills1))

        def group(x):
            return NG * (x // KC) + x % KC // 2

        def pair_rows(x):
            return probs[:, x % NPS, :].rearrange("p (h q) -> p h q", h=2)

        @block.tensor
        def _(pe):
            def keep_clock(n):
                for _ in range(n):
                    pe.matmul(quarter[1], identb[:, :], identb[:, :].unsqueeze(1).to_broadcast([P, 4, P]), start=True, stop=True)

            def norm_T(n, last):
                pe.wait_ge(ln_ready, n)
                for s in range(NS):
                    m = pe.transpose(norm_bank[not last][:, s * P:(s + 1) * P], xn[:, s, :], ident[:, :])
                m.then_inc(xT_psum, 1)

            def project(n, src, w, last):
                pe.wait_ge(xT_ready, n)
                for s in range(NS):
                    m = pe.matmul(q_bank[not last][:, s * P:(s + 1) * P], src[:, s * P:(s + 1) * P], w, start=True, stop=True)
                m.then_inc(q_psum, 1)

            def all_queries(n, layer):
                pe.wait_ge(qst_ready, n)
                for half in range(2):
                    for k in range(8):
                        p, s = divmod(half * 8 + k, NS)
                        m = pe.transpose(all_bank[layer][half][:, k * P:(k + 1) * P],
                                         qst[:, s, 2 * p:2 * p + 2, :].rearrange("p h r -> p (h r)"), identb[:, :])
                    m.then_inc(all_psum, 1)

            def index_T():
                pe.wait_ge(idxf_ready, 1)
                pe.transpose(quarter[3][:, NQ:NQ + P], idx_f[:, :, :].rearrange("p s k -> p (s k)"), ident[:, :]).then_inc(idxT_psum, 1)

            def pair_queries(p, e, ready, b_rdy, b_rd):
                pe.wait_ge(ready, p + 1)
                if e >= 3:
                    pe.wait_ge(b_rd, e - 2)
                for s in range(NS):
                    m = pe.transpose(bsb[e % 3][:, s * P:(s + 1) * P],
                                     qst[:, s, 2 * p:2 * p + 2, :].rearrange("p h r -> p (h r)"), identb[:, :])
                m.then_inc(b_rdy, 1)

            def attend_T(layer):
                pe.wait_ge(at_ready, layer + 1)
                for s in range(NS):
                    m = pe.transpose(quarter[0][:, s * P:(s + 1) * P], att[:, s, :, :].rearrange("p h d -> p (h d)"), ident[:, :])
                m.then_inc(atT_psum, 1)

            def attend_out(layer, w):
                pe.wait_ge(atT_ready, layer + 1)
                for s in range(NS):
                    m = pe.matmul(quarter[2][:, s * P:(s + 1) * P], attT[:, s * P:(s + 1) * P], w, start=True, stop=True)
                m.then_inc(o_psum, 1)

            def max_part(k):
                u, j = divmod(k, NM)
                p, s = divmod(u, NS)
                if k >= 2:
                    pe.wait_ge(part_read, k - 1)
                n = min(KM, NK - j * KM)
                for hh in range(2):
                    o = SLOT * hh
                    m = pe.matmul((a0, a1)[k % 2][:, hh * MMAX:hh * MMAX + n], qa[o:o + SLOT, p, s, :],
                                  kst[o:o + SLOT, p, j * KM:j * KM + n], start=True, stop=True)
                m.then_inc(part_ready, 1)

            def combine(p, e, o_rdy, b_rdy, b_rd):
                pe.wait_ge(o_rdy, p + 1)
                pe.wait_ge(b_rd, e - 2)
                for s in range(NS):
                    m = pe.matmul(bs[e % 3][:, s * 2 * V1:(s + 1) * 2 * V1], oT[:, s * P:(s + 1) * P], comb[:, :],
                                  start=True, stop=True)
                m.then_inc(b_rdy, 1)

            def scores(x):
                e = fill0["e", x]
                p, c = divmod(x, KC)
                kn = rows(c, NK)
                if c == 0:
                    pe.wait_ge(b_read, fill0["q", p] + 1)
                if e >= 3:
                    pe.wait_ge(b_read, e - 2)
                pe.matmul(bs[e % 3][0:kn, :], kst[:, p, c * P:c * P + kn], qb[:, p % 2, :, :].rearrange("p h q -> p (h q)"),
                          start=True, stop=True).then_inc(b_ready, 1)

            def weigh(g):
                p, j = divmod(g, NG)
                last = min(2 * j + 1, KC - 1)
                pe.wait_ge(b_read, fill0["e", KC * p + last] + 1)
                if j == 0 and p >= 1:
                    pe.wait_ge(oT_ready, p)
                for c in range(2 * j, last + 1):
                    kn = rows(c, NK)
                    for hh in range(2):
                        q = QD * (2 * hh + c % 2)
                        m = pe.matmul(ob[q:q + V1, 0:NQ], vaug[0:kn, c, 2 * p + hh, :],
                                      probs[0:kn, (KC * p + c) % NPS, hh * NQ:(hh + 1) * NQ],
                                      start=(j == 0), stop=(c + 2 >= KC), skip_group_check=True, tile_position=(0, q))
                m.then_inc(pv_done, 1)

            def attention0():
                done = [0]

                def parts(upto):
                    while done[0] < min(upto, NH0):
                        max_part(done[0])
                        done[0] += 1
                for g in range(4):
                    parts(START + 2 * (g - CTX))
                    context_T(g)
                parts(START)
                pe.wait_ge(ctxT_ready, 4)
                weighed = [0]
                for kind, n in fills0:
                    if kind == "q":
                        pair_queries(n, fill0[kind, n], m_ready, b_ready, b_read)
                    elif kind == "c":
                        if n == NP - 1:
                            for g in range(weighed[0], NP * NG):
                                weigh(g)
                        combine(n, fill0[kind, n], oT_ready, b_ready, b_read)
                    else:
                        scores(n)
                        parts(min(START + (n + 1) * (PARTS + LEAD - START) // KC, LEAD + (n + 1) * PARTS // KC))
                        if n >= LAG and group(n - LAG + 1) > group(n - LAG):
                            weigh(weighed[0])
                            weighed[0] += 1
                pe.drain().then_inc(att_done, 1)

            def context_T(g):
                if g == 3:
                    pe.wait_ge(ctxT_ready, 1)
                for c in range(4 * g, min(4 * g + 4, KC)):
                    kn = rows(c, NK)
                    m = pe.transpose(bs[g % 3][:, (c % 4) * P:(c % 4) * P + kn], ctx_sb[0:kn, c, :], ident[0:kn, 0:kn])
                m.then_inc(ctxT_psum, 1)

            def count(q0, q1):
                if q0 == 0:
                    pe.wait_ge(onehot_ready, NP)
                    pe.wait_ge(onehotv_ready, NP)
                    pe.wait_ge(b_read, len(fills0))
                for q in range(q0, q1):
                    for s in range(NS):
                        cnt = cnt_bank[s][:, 0:P * KC1].rearrange("p (q c) -> p q c", c=KC1)
                        m = pe.matmul(cnt[:, q, :], onehot[s * NIDX:(s + 1) * NIDX, q, :], idx_c[s * NIDX:(s + 1) * NIDX, q, :],
                                      start=True, stop=True)
                if q1 == P:
                    m.then_inc(cnt_psum, 1)

            def mask_T():
                pe.wait_ge(x_ready, 2)
                for n in range(NS * KC1):
                    s, c = divmod(n, KC1)
                    m = pe.transpose(ob[:, :].bitcast(bf16)[:, n * P:(n + 1) * P], maskT[:, c, s * P:(s + 1) * P], identb[:, :])
                m.then_inc(maskq_psum, 1)

            def attention1():
                pe.wait_ge(maskq_ready, 1)
                pe.wait_ge(side_act, 8)

                def max_pair(p):
                    bank = (a0, a1)[p % 2]
                    if p % 4 == 0:
                        pe.wait_ge(all_read, p // 4 + 1)
                    if p >= 2:
                        pe.wait_ge(pair_read, p - 1)
                    for hh in range(2):
                        o = SLOT * hh
                        cols = bank[:, hh * 512:(hh + 1) * 512].rearrange("p (s k) -> p s k", s=NS)
                        for s in range(NS):
                            pe.matmul(cols[:, s, :], identb[:, :], maskq[:, s, :], start=True, stop=False)
                            m = pe.matmul(cols[:, s, :], qa[o:o + SLOT, p, s, :], k1st[o:o + SLOT, p, :], start=False, stop=True)
                    m.then_inc(pair_ready, 1)

                def scores1(x):
                    e = fill1["e", x]
                    p, c = divmod(x, KC1)
                    if c == 0:
                        pe.wait_ge(b1_read, fill1["q", p] + 1)
                    if e >= 3:
                        pe.wait_ge(b1_read, e - 2)
                    pe.matmul(bs[e % 3][:, :], identb[:, :], maskT[:, c, :].unsqueeze(1).to_broadcast([P, 2, NQ]), start=True, stop=False)
                    pe.matmul(bs[e % 3][:, :], k1st[:, p, c * P:(c + 1) * P], qb[:, p % 2, :, :].rearrange("p h q -> p (h q)"),
                              start=False, stop=True).then_inc(b1_ready, 1)

                def weigh1(p):
                    pe.wait_ge(mulv, p + 1)
                    pe.wait_ge(mulp, p + 1)
                    if p >= 1:
                        pe.wait_ge(oT1_ready, p)
                    for c in range(KC1):
                        for hh in range(2):
                            q = QD * (2 * hh + c)
                            m = pe.matmul(ob[q:q + V1, 0:NQ], v1aug[:, c, 2 * p + hh, :],
                                          probs[:, (KC1 * p + c) % NPS, hh * NQ:(hh + 1) * NQ],
                                          start=True, stop=True, tile_position=(0, q))
                    m.then_inc(pv1_done, 1)

                max_pair(0)
                max_pair(1)
                for kind, n in fills1:
                    if kind == "q":
                        pair_queries(n, fill1[kind, n], m1_ready, b1_ready, b1_read)
                        if n == 0:
                            max_pair(2)
                        if n >= 2:
                            weigh1(n - 2)
                    elif kind == "e":
                        scores1(n)
                        if n % 2 == 1 and n // 2 + 3 < NP:
                            max_pair(n // 2 + 3)
                        if n == NX1 - 1:
                            weigh1(NP - 2)
                    else:
                        if n == NP - 1:
                            weigh1(NP - 1)
                        combine(n, fill1[kind, n], oT1_ready, b1_ready, b1_read)
                pe.drain().then_inc(att_done, 1)

            def next_keys(g):
                if g == 0:
                    pe.wait_ge(ctxT_ready, 4)
                if g >= 2:
                    pe.wait_ge(side_act, g - 1)
                n = min(MMAX, NK - g * MMAX)
                pe.matmul(side_bank[g % 2][:, 0:n], wkv_sb[:, 0:D], ctxT[:, g * MMAX:g * MMAX + n],
                          start=True, stop=True).then_inc(side_psum, 1)

            def next_values(g0, g1):
                for g in range(g0, g1):
                    pe.wait_ge(side_act, g + 3)
                    for c in range(4 * g, min(4 * g + 4, KC)):
                        kn = rows(c, NK)
                        m = pe.matmul(side_bank[g % 2][0:kn, (c % 4) * P:(c % 4 + 1) * P], ctxT[:, c * P:c * P + kn], wkv_sb[:, D:2 * D],
                                      start=True, stop=True)
                    m.then_inc(side_psum, 1)

            def next_latent1():
                pe.wait_ge(side_act, 8)
                pe.matmul(side_bank[0][:, 0:NK1], wd1T[:, :], ctxT[:, 0:NK1], start=True, stop=True).then_inc(side1_psum, 1)

            def next_keys1():
                pe.wait_ge(side1_act, 1)
                pe.matmul(side_bank[1][:, 0:NK1], wu1T[:, 0:D], cT[:, :], start=True, stop=True).then_inc(side1_psum, 1)
                for c in range(KC1):
                    m = pe.matmul(side_bank[0][:, c * P:(c + 1) * P], cT[:, c * P:(c + 1) * P], wu1T[:, D:2 * D], start=True, stop=True)
                m.then_inc(side1_psum, 1)

            def experts(l):
                wga, wua, wda, nch, ftot = ((w1T, w3T, w2T, NC0, F0), (wg_sb, wu_sb, wd_sb, NC1, F1))[l]
                lag = 3
                pe.wait_ge(xT_ready, 2 * l + 1)
                for s in range(NS):
                    m = pe.matmul(bs[0][:, s * NE:(s + 1) * NE], xnT[:, s * P:(s + 1) * P], gT[l][:, :], start=True, stop=True)
                m.then_inc(gate_psum[l], 1)
                if l == 0:
                    count(COUNT[3], P)

                def gate_up(c):
                    if c >= 3:
                        pe.wait_ge(hu_done[l], c - 2)
                    n = rows(c, ftot)
                    pe.matmul(gu_bank[c % 3][0:n, 0:NQ], wga[:, c * P:c * P + n], xnT[:, :], start=True, stop=True)
                    pe.matmul(gu_bank[c % 3][0:n, NQ:2 * NQ], wua[:, c * P:c * P + n], xnT[:, :], start=True, stop=True).then_inc(gu_ready[l], 1)

                def weights(c):
                    if c >= 2:
                        pe.wait_ge(hid_ready[l], c - 1)
                    n = rows(c, ftot)
                    pe.matmul(cb_bank[c % 2][0:n, 0:NQ], sel[l][:, c * P:c * P + n], cwT[:, :], start=True, stop=True).then_inc(cb_ready[l], 1)

                def down(c):
                    pe.wait_ge(hid_ready[l], c + 1)
                    n = rows(c, ftot)
                    for s in range(NS):
                        m = pe.matmul(ob[:, s * P:(s + 1) * P], hid[0:n, c % 4, s * P:(s + 1) * P], wda[0:n, c, :],
                                      start=(c == 0 and s == 0), stop=(c == nch - 1), skip_group_check=True)
                    m.then_inc(down_done[l], 1)

                gate_up(0)
                gate_up(1)
                gate_up(2)
                pe.wait_ge(cwp_ready[l], 1)
                for s in range(NS):
                    m = pe.transpose(bsb[0][0:CWR, s * P:(s + 1) * P], cwp[:, s, :], identb[:, :])
                m.then_inc(cwT_psum[l], 1)
                pe.wait_ge(cwT_ready[l], 1)
                weights(0)
                if l == 0:
                    pe.wait_ge(cnt_ready, 1)
                weights(1)
                for c in range(3, nch + lag):
                    if c < nch:
                        gate_up(c)
                    if 2 <= c - 1 < nch:
                        weights(c - 1)
                    down(c - lag)
                    if l == 0 and 4 <= c < 8:
                        next_keys(c - 4)
                    if l == 1 and c == 6:
                        pe.wait_ge(side1_act, 3)
                        norm_T(4, True)
                        index_T()
                    if l == 1 and c == 8:
                        project(4, attT, wq_sb[:, :], True)
                    if l == 1 and c == 14:
                        all_queries(2, 0)

            pe.wait_ge(const_ready, 2)
            pe.wait_ge(w_in, 16 * 16)
            for g, (dst, srcs) in enumerate(stages):
                if g >= 4:
                    pe.wait_ge((stage_dve, stage_act)[g % 2], (g - 4) // 2 + 1)
                o = 0
                for src in srcs:
                    kp, n = src.shape
                    m = pe.transpose(quarter[g % 4][0:n, o:o + kp], src, ident[0:kp, 0:kp])
                    o += kp
                m.then_inc(stage_psum, 1)
            for k in range(2):
                pe.wait_ge((stage_dve, stage_act)[k], (len(stages) + 1 - k) // 2)
            pe.wait_ge(w2_in, 16 * 15)
            pe.wait_ge(pre_bv, 1)
            pe.matmul(quarter[1][:, 0:D], xn[:, 0, :], wo_sb[:, :], start=True, stop=True).then_inc(pre_psum, 1)
            pe.wait_ge(ctx_in_s, 32)
            for g in range(4):
                context_T(g)
            pe.wait_ge(ctxT_ready, 4)
            for g in range(4):
                next_keys(g)
            next_values(0, 4)
            next_latent1()
            next_keys1()
            pe.wait_ge(side1_act, 3)
            norm_T(1, True)
            index_T()
            project(1, attT, wq_sb[:, :], True)
            all_queries(1, 0)
            meet(pe, 0)
            with pe.Fori(0, NB):
                attention0()
                count(0, COUNT[0])
                attend_T(0)
                count(COUNT[0], COUNT[1])
                attend_out(0, wo_sb[:, :])
                count(COUNT[1], COUNT[2])
                norm_T(1, False)
                count(COUNT[2], COUNT[3])
                experts(0)
                next_values(0, 2)
                mask_T()
                next_values(2, 4)
                norm_T(2, False)
                keep_clock(2)
                project(2, xnT, wq1T[:, :], False)
                keep_clock(8)
                all_queries(1, 1)
                keep_clock(3)
                attention1()
                keep_clock(3)
                attend_T(1)
                keep_clock(2)
                attend_out(1, wo1T[:, :])
                next_latent1()
                next_keys1()
                keep_clock(10)
                norm_T(3, False)
                keep_clock(2)
                experts(1)
                meet(pe, 0)

        @block.scalar
        def _(act):
            def copy(o, i):
                return act.activation(o, i, ACT.Copy)

            def all_queries(n, layer):
                for half in range(2):
                    act.wait_ge(all_psum, n + half + 1)
                    copy(qa[:, 4 * half:4 * half + 4, :, :].rearrange("p a s q -> p (a s q)"), all_bank[layer][half]).then_inc(all_read, 1)

            def pair_queries(p, e, b_rdy, b_rd):
                act.wait_ge(b_rdy, e + 1)
                act.activation(qb[0:SLOT, p % 2, 0, :], bsb[e % 3][0:SLOT, 0:NQ], ACT.Copy)
                copy(qb[SLOT:P, p % 2, 1, :], bsb[e % 3][SLOT:P, 0:NQ]).then_inc(b_rd, 1)

            def evacuate(p, pv, o_rdy, count):
                act.wait_ge(pv, count)
                copy(oT[:, :], ob[:, 0:NQ]).then_inc(o_rdy, 1)

            def combined(p, e, b_rdy, b_rd):
                act.wait_ge(b_rdy, e + 1)
                copy(raw[:, :, 2 * p:2 * p + 2, :].rearrange("p s h d -> p s (h d)"),
                     bs[e % 3][:, 0:NS * 2 * V1].rearrange("p (s n) -> p s n", s=NS)).then_inc(b_rd, 1)

            def attention0():
                for kind, n in fills0:
                    e = fill0[kind, n]
                    if kind == "q":
                        pair_queries(n, e, b_ready, b_read)
                    elif kind == "c":
                        if n == NP - 1:
                            evacuate(n, pv_done, oT_ready, NG * NP)
                        combined(n, e, b_ready, b_read)
                    else:
                        act.wait_ge(b_ready, e + 1)
                        if n >= NPS:
                            act.wait_ge(pv_done, group(n - NPS) + 1)
                        p, c = divmod(n, KC)
                        kn = rows(c, NK)
                        act.activation(probs[0:kn, n % NPS, :], bs[e % 3][0:kn, :], ACT.Exp).then_inc(b_read, 1)
                        if c == O_AT and p >= 1:
                            evacuate(p - 1, pv_done, oT_ready, NG * p)

            def attention1():
                all_queries(0, 1)
                for kind, n in fills1:
                    e = fill1[kind, n]
                    if kind == "q":
                        pair_queries(n, e, b1_ready, b1_read)
                    elif kind == "c":
                        if n >= NP - 2:
                            evacuate(n, pv1_done, oT1_ready, n + 1)
                        combined(n, e, b1_ready, b1_read)
                    else:
                        act.wait_ge(b1_ready, e + 1)
                        if n >= NPS:
                            act.wait_ge(pv1_done, (n - NPS) // 2 + 1)
                        act.activation(probs[:, n % NPS, :], bs[e % 3][:, :], ACT.Exp).then_inc(b1_read, 1)
                        if n % 2 == 0 and n >= 4:
                            evacuate(n // 2 - 2, pv1_done, oT1_ready, n // 2 - 1)

            def next_context():
                for g in range(4):
                    n = min(MMAX, NK - g * MMAX)
                    act.wait_ge(ctxT_psum, g + 1)
                    copy(ctxT[:, g * MMAX:g * MMAX + n], bs[g % 3][:, 0:n]).then_inc(ctxT_ready, 1)

            def next_keys(g):
                n = min(MMAX, NK - g * MMAX)
                act.wait_ge(side_psum, g + 1)
                act.activation(kf[:, g * MMAX:g * MMAX + n], side_bank[g % 2][:, 0:n], ACT.Identity,
                               bias=bk_col[:, 0:1]).then_inc(side_act, 1)

            def key_part(g):
                n = min(MMAX, NK - g * MMAX)
                act.wait_ge(side_act, g + 1)
                m = copy(kpart[0][:, g * MMAX:g * MMAX + n], kf[:, g * MMAX:g * MMAX + n])
                if g == 3:
                    m.then_inc(kp_ready, 1)

            def next_values():
                for g in range(4):
                    act.wait_ge(side_psum, g + 5)
                    nc_ = min(4, KC - 4 * g)
                    kn = rows(4 * g, NK)
                    copy(vaug[0:kn, 4 * g:4 * g + nc_, :, 0:HD],
                         side_bank[g % 2][0:kn, 0:nc_ * P].rearrange("p (c h d) -> p c h d", c=nc_, h=H)).then_inc(side_act, 1)

            def next_keys1():
                act.wait_ge(side1_psum, 1)
                copy(cT[:, :], side_bank[0][:, 0:NK1]).then_inc(side1_act, 1)
                act.wait_ge(side1_psum, 2)
                copy(kf1, side_bank[1][:, 0:NK1]).then_inc(side1_act, 1)
                act.wait_ge(side1_act, 2)
                copy(kpart1[0], kf1).then_inc(kp1_ready, 1)
                act.wait_ge(side1_psum, 3)
                copy(v1aug[:, :, :, 0:HD], side_bank[0][:, 0:NK1].rearrange("p (c h d) -> p c h d", c=KC1, h=H)).then_inc(side1_act, 1)

            def experts(l):
                nch, ftot = ((NC0, F0), (NC1, F1))[l]
                act.wait_ge(lz_ready[l], 1)
                act.activation(le[:, :, :], lz[:, :, :], ACT.Exp).then_inc(le_ready[l], 1)
                for c in range(nch):
                    n = rows(c, ftot)
                    act.wait_ge(gu_ready[l], c + 1)
                    if c >= 3:
                        act.wait_ge(gt_done[l], c - 2)
                    act.activation(th[0:n, c % 3, :], gu_bank[c % 3][0:n, 0:NQ], ACT.Tanh, scale=0.5).then_inc(th_ready[l], 1)
                    if l == 0 and 4 <= c < 8:
                        next_keys(c - 4)
                    if l == 0 and 5 <= c < 9:
                        key_part(c - 5)

            for l in range(2):
                act.wait_ge(sel_part, l + 1)
                for t in (1, 2):
                    copy(sel[l][CWP * t:CWP * t + NE, :], sel[l][0:NE, :]).then_inc(sel_done, 1)
            for g, (dst, srcs) in enumerate(stages):
                if g % 2 == 1:
                    act.wait_ge(stage_psum, g + 1)
                    np_, w = dst.shape
                    copy(dst, quarter[g % 4][0:np_, 0:w]).then_inc(stage_act, 1)
            act.wait_ge(w2_in, 16 * 15)
            act.wait_ge(stage_psum, len(stages))
            next_context()
            for g in range(4):
                next_keys(g)
            for g in range(4):
                key_part(g)
            act.wait_ge(pre_dve, 2)
            next_values()
            next_keys1()
            all_queries(0, 0)
            meet(act, 1)
            with act.Fori(0, NB):
                next_context()
                attention0()
                experts(0)
                next_values()
                attention1()
                next_keys1()
                experts(1)
                all_queries(2, 0)
                meet(act, 1)

        @block.vector
        def _(dve):
            def norm_stats(src, st):
                for s in range(NS):
                    st.do(dve.bn_stats(stats[:, s, :], src[:, s, :]))
                st.wait()
                for s in range(NS):
                    st.do(dve.bn_aggr(mv[:, s, :], stats[:, s, :]))
                st.wait()
                dve.tensor_scalar(veps[:, :, :], mv[:, :, 1:2], EPS, None, ALU.add).then_inc(mv_ready, 1)

            def norm_apply(n, src):
                dve.wait_ge(rstd_ready, n)
                for s in range(NS):
                    m = dve.tensor_scalar(xn[:, s, :], src[:, s, :], mv[:, s, 0:1], rstd[:, s, :], ALU.subtract, ALU.mult)
                m.then_inc(ln_ready, 1)

            def norm_T(n, dst, last):
                dve.wait_ge(xT_psum, n)
                if last:
                    dve.wait_ge(idxT_psum, 1)
                    dve.tensor_copy(idx_t[:, :], quarter[3][:, NQ:NQ + P]).then_inc(idxt_ready, 1)
                dve.tensor_copy(dst, norm_bank[not last][:, 0:NQ]).then_inc(xT_ready, 1)

            def norm(n, src, st):
                norm_stats(src, st)
                if n == 2:
                    dve.wait_ge(maskq_psum, 1)
                    dve.tensor_copy(maskq[:, :, :].rearrange("p s k -> p (s k)"),
                                    ob[:, :].bitcast(bf16)[:, 0:NS * NK1]).then_inc(maskq_ready, 1)
                norm_apply(n, src)
                norm_T(n, xnT[:, :], False)

            def scale_queries(n, layer, st):
                st.do(dve.memset(qst[:, :, :, KROWS:MROWS], 0.0))
                dve.wait_ge(q_psum, n)
                if layer == 0:
                    st.link(dve.scalar_tensor_tensor(out=qs[:, :, :, :].rearrange("p s h d -> p s (h d)"),
                                                     in0=q_bank[0][:, 0:NQ].rearrange("p (s n) -> p s n", s=NS), scalar=SCALE,
                                                     in1=bqs[:, :].unsqueeze(1).to_broadcast([P, NS, D]),
                                                     op0=ALU.mult, op1=ALU.add))
                else:
                    st.link(dve.tensor_scalar(qs[:, :, :, :], q_bank[1][:, 0:NQ].rearrange("p (s h d) -> p s h d", s=NS, h=H),
                                              SCALE, None, ALU.mult))

            def high_parts(st):
                st.link(dve.tensor_copy(qst[:, :, :, 0:8], qs[:, :, :, :]))
                return dve.tensor_tensor(qres[:, :, :, :], qs[:, :, :, :], qst[:, :, :, 0:8], ALU.subtract)

            def low_parts(st):
                st.link(dve.tensor_copy(qst[:, :, :, 8:16], qres[:, :, :, :]))
                st.do(dve.tensor_tensor(qst[:, :, :, 16:24], qres[:, :, :, :], qst[:, :, :, 8:16], ALU.subtract))
                st.do(dve.tensor_copy(qst[:, :, :, 24:40], qst[:, :, :, 0:16]))
                dve.tensor_copy(qst[:, :, :, 40:48], qst[:, :, :, 0:8]).then_inc(qst_ready, 1)

            def normalise(layer, h0, h1, st):
                dve.wait_ge((b_read, b1_read)[layer], (fill0, fill1)[layer]["c", h1 // 2 - 1] + 1)
                st.link(dve.reciprocal(rec[:, :, h0:h1], raw[:, :, h0:h1, HD]))
                return dve.tensor_tensor(att[:, :, h0:h1, :], raw[:, :, h0:h1, 0:HD],
                                         rec[:, :, h0:h1].unsqueeze(3).to_broadcast([P, NS, h1 - h0, HD]), ALU.mult)

            def attend_out(layer, xin, xout, st):
                normalise(layer, H - 2, H, st).then_inc(at_ready, 1)
                dve.wait_ge(atT_psum, layer + 1)
                dve.tensor_copy(attT[:, :], quarter[0][:, 0:NQ]).then_inc(atT_ready, 1)
                dve.wait_ge(o_psum, layer + 1)
                dve.tensor_tensor(xout[:, :, :], quarter[2][:, 0:NQ].rearrange("p (s d) -> p s d", s=NS), xin[:, :, :],
                                  ALU.add).then_inc(x_ready, 1)
                dve.wait_ge(x_ready, 2 * layer + 1)

            def attention0():
                def join(p):
                    dve.wait_ge(part_read, PARTS * (p + 1))
                    if p >= 2:
                        dve.wait_ge(m_ready, p - 1)
                    dve.tensor_reduce(nm[:, p % 2, :, :].rearrange("p s h -> p (s h)"), mx[:, p % 2, :, :, :].rearrange("p s h j -> p (s h) j"),
                                      AX, ALU.min).then_inc(nm_ready, 1)

                for k in range(NH0):
                    u, j = divmod(k, NM)
                    p, s = divmod(u, NS)
                    dve.wait_ge(part_ready, k + 1)
                    if k % PARTS == 0 and p >= 2:
                        dve.wait_ge(nm_ready, p - 1)
                    n = min(KM, NK - j * KM)
                    dve.tensor_reduce(mx[:, p % 2, s, :, j], (a0, a1)[k % 2][:, :].rearrange("p (h k) -> p h k", h=2)[:, :, 0:n], AX, ALU.max,
                                      negate=True).then_inc(part_read, 1)
                    if k % PARTS == PARTS - 1:
                        join(p)
                    if k % PARTS < NHV:
                        q = 16 * p + k % PARTS
                        m = dve.tensor_scalar(onehot[:, q, :], iotab[:, :], idx_lo[:, q:q + 1], None, ALU.is_equal)
                        if k % PARTS == NHV - 1:
                            m.then_inc(onehotv_ready, 1)

            def attention1(st):
                for p in range(NP + 2):
                    if p < NP:
                        dve.wait_ge(pair_ready, p + 1)
                        dve.tensor_reduce(mx1[:, p, :, :].rearrange("p h s -> p (h s)"), (a0, a1)[p % 2][:, :].rearrange("p (n k) -> p n k", k=NK1),
                                          AX, ALU.max, negate=True).then_inc(pair_read, 1)
                    if p >= 2:
                        x = KC1 * (p - 2)
                        dve.wait_ge(b1_read, fill1["e", x] + 1)
                        dve.tensor_tensor(pair_rows(x), pair_rows(x), cntT[:, 0, :].unsqueeze(1).to_broadcast([P, 2, NQ]),
                                          ALU.mult).then_inc(mulv, 1)

            def routing(l, st):
                dve.wait_ge(gate_psum[l], 1)
                g = bs[0][:, 0:NS * NE].rearrange("p (s e) -> p s e", s=NS)
                if l == 0:
                    st.link(dve.tensor_tensor(ls[:, :, :], g, gb_bc[:, :].unsqueeze(1).to_broadcast([P, NS, NE]), ALU.add))
                    dve.tensor_scalar(lz[:, :, :], ls[:, :, :], -1.0, None, ALU.mult).then_inc(lz_ready[l], 1)
                    dve.wait_ge(le_ready[l], 1)
                    st.link(dve.tensor_scalar(lz[:, :, :], le[:, :, :], 1.0, None, ALU.add))
                    st.link(dve.reciprocal(ls[:, :, :], lz[:, :, :]))
                else:
                    st.link(dve.tensor_reduce(lneg[:, :], g[:, :, 0:8], AX, ALU.max, negate=True))
                    dve.tensor_tensor(lz[:, :, 0:8], g[:, :, 0:8], lneg[:, :].unsqueeze(2).to_broadcast([P, NS, 8]), ALU.add)
                    dve.tensor_scalar(lz[:, :, 8:9], g[:, :, 8:9], -1.0, None, ALU.mult).then_inc(lz_ready[l], 1)
                    dve.wait_ge(le_ready[l], 1)
                    st.link(dve.tensor_reduce(lsum[:, :], le[:, :, 0:8], AX, ALU.add))
                    st.link(dve.reciprocal(lrec[:, :], lsum[:, :]))
                    st.link(dve.tensor_tensor(ls[:, :, 0:8], le[:, :, 0:8], lrec[:, :].unsqueeze(2).to_broadcast([P, NS, 8]), ALU.mult))
                    st.do(dve.tensor_scalar(lz[:, :, 8:9], le[:, :, 8:9], 1.0, 2.0, ALU.add, ALU.mult))
                n = (NE, 8)[l]
                for s in range(NS):
                    st.do(dve.max(top[:, s, :], ls[:, s, 0:n]))
                st.wait()
                for s in range(NS):
                    st.do(dve.max_index(topi[:, s, :], top[:, s, :], ls[:, s, 0:n]))
                st.do(dve.scalar_tensor_tensor(out=wden[:, :], in0=top[:, :, 0], scalar=(1e-20, 0.0)[l], in1=top[:, :, 1],
                                               op0=ALU.add, op1=ALU.add))
                st.wait()
                st.do(dve.tensor_copy(topf[:, :, :], topi[:, :, 0:2]))
                st.link(dve.reciprocal(wrec[:, :], wden[:, :]))
                st.do(dve.scalar_tensor_tensor(out=wtop[:, :, :], in0=top[:, :, 0:2], scalar=0.5, in1=wrec[:, :].unsqueeze(2).to_broadcast([P, NS, 2]),
                                               op0=ALU.mult, op1=ALU.mult))
                st.link(dve.tensor_tensor(pick[:, :, :, 0:n].rearrange("p s t e -> p (s t) e"), iota_f[:, 0:n].unsqueeze(1).to_broadcast([P, 2 * NS, n]),
                                          topf[:, :, :].rearrange("p s t -> p (s t)").unsqueeze(2).to_broadcast([P, 2 * NS, n]), ALU.is_equal))
                st.link(dve.tensor_tensor(pick[:, :, :, 0:n].rearrange("p s t e -> p (s t) e"), pick[:, :, :, 0:n].rearrange("p s t e -> p (s t) e"),
                                          wtop[:, :, :].rearrange("p s t -> p (s t)").unsqueeze(2).to_broadcast([P, 2 * NS, n]), ALU.mult))
                st.do(dve.tensor_tensor(cw[:, :, 0:n], pick[:, :, 0, 0:n], pick[:, :, 1, 0:n], ALU.add))
                if l == 1:
                    st.do(dve.reciprocal(cw[:, :, 8:9], lz[:, :, 8:9]))
                st.wait()
                st.link(dve.tensor_copy(cwp[:, :, 0:NE], cw[:, :, :]))
                st.link(dve.tensor_tensor(cwr[:, :, :], cw[:, :, :], cwp[:, :, 0:NE], ALU.subtract))
                st.link(dve.tensor_copy(cwp[:, :, CWP:CWP + NE], cwr[:, :, :]))
                dve.tensor_tensor(cwp[:, :, 2 * CWP:2 * CWP + NE], cwr[:, :, :], cwp[:, :, CWP:CWP + NE], ALU.subtract).then_inc(cwp_ready[l], 1)

            def take_counts(st):
                dve.wait_ge(cnt_psum, 1)
                for s in range(NS):
                    st.do(dve.tensor_copy(cntT[:, :, s * P:(s + 1) * P].rearrange("p c q -> p q c"),
                                          cnt_bank[s][:, 0:P * KC1].rearrange("p (q c) -> p q c", c=KC1)))
                st.wait()
                dve.tensor_scalar(maskT[:, :, :], cntT[:, :, :], 0.0, NEG, ALU.is_equal, ALU.mult).then_inc(cnt_ready, 1)

            def experts(l, xin, xout, st):
                nch, ftot = ((NC0, F0), (NC1, F1))[l]
                routing(l, st)
                if l == 0:
                    take_counts(st)

                def hidden(c):
                    n = rows(c, ftot)
                    dve.wait_ge(hu_done[l], c + 1)
                    dve.wait_ge(cb_ready[l], c + 1)
                    if c >= 4:
                        dve.wait_ge(down_done[l], c - 3)
                    dve.tensor_tensor(hid[0:n, c % 4, :], hu[0:n, c % 3, :], cb_bank[c % 2][0:n, 0:NQ], ALU.mult).then_inc(hid_ready[l], 1)

                for c in range(nch):
                    n = rows(c, ftot)
                    g = gu_bank[c % 3]
                    dve.wait_ge(th_ready[l], c + 1)
                    dve.scalar_tensor_tensor(out=gt[0:n, c % 3, :], in0=th[0:n, c % 3, :], scalar=1.0, in1=g[0:n, 0:NQ],
                                             op0=ALU.add, op1=ALU.mult).then_inc(gt_done[l], 1)
                    if c == 0:
                        dve.wait_ge(cwT_psum[l], 1)
                        dve.tensor_copy(cwT[:, :], bsb[0][0:CWR, 0:NQ]).then_inc(cwT_ready[l], 1)
                    if c >= 1:
                        hidden(c - 1)
                    dve.wait_ge(gt_done[l], c + 1)
                    dve.tensor_tensor(hu[0:n, c % 3, :], gt[0:n, c % 3, :], g[0:n, NQ:2 * NQ], ALU.mult).then_inc(hu_done[l], 1)
                    if l == 1:
                        if c == 1:
                            dve.wait_ge(x_in, 16)
                            norm_stats(xs[0], st)
                        if c == 3:
                            norm_apply(4, xs[0])
                        if c == 5:
                            norm_T(4, attT[:, :], True)
                        if c == 8:
                            scale_queries(2, 0, st)
                        if c == 9:
                            high_parts(st).then_inc(qres_ready, 1)
                hidden(nch - 1)
                dve.wait_ge(down_done[l], nch)
                if l == 1:
                    dve.wait_ge(xo_free, 1)
                dve.tensor_tensor(xout[:, :, :], ob[:, 0:NQ].rearrange("p (s d) -> p s d", s=NS), xin[:, :, :], ALU.add).then_inc(x_ready, 1)
                dve.wait_ge(x_ready, 2 * l + 2)

            st = Steps(dve, dve_step)
            for l in range(2):
                dve.memset(sel[l][:, :], 0.0).then_inc(sel_zero, 1)
            for g, (dst, srcs) in enumerate(stages):
                if g % 2 == 0:
                    dve.wait_ge(stage_psum, g + 1)
                    np_, w = dst.shape
                    dve.tensor_copy(dst, quarter[g % 4][0:np_, 0:w]).then_inc(stage_dve, 1)
            dve.memset(gb_bc[:, 0:8], 0.0).then_inc(pre_dve, 1)
            dve.memset(vaug[:, :, :, HD:V1], 1.0).then_inc(pre_dve, 1)
            dve.memset(v1aug[:, :, :, HD:V1], 1.0).then_inc(pre_dve, 1)
            dve.memset(qst[:, :, :, :], 0.0).then_inc(pre_dve, 1)
            dve.memset(cwp[:, :, :], 0.0).then_inc(pre_dve, 1)
            dve.memset(qb[:, :, :, :], 0.0).then_inc(pre_dve, 1)
            dve.memset(neg_half[:, :, :], -0.5).then_inc(pre_dve, 1)
            dve.memset(ob[:, :], 0.0).then_inc(pre_dve, 1)
            dve.wait_ge(w2_in, 16 * 15)
            dve.tensor_copy(xn[:, 0, :], bv_col[:, 0:1].to_broadcast([P, P])).then_inc(pre_bv, 1)
            dve.wait_ge(pre_dve, 8)
            st.do(dve.tensor_scalar(bqs[:, :], bqs[:, :], SCALE, None, ALU.mult))
            dve.wait_ge(pre_psum, 1)
            dve.tensor_tensor(bo_bc[:, :], quarter[1][:, 0:D], bo_bc[:, :], ALU.add).then_inc(pre_bo, 1)
            dve.wait_ge(x_in, 16)
            norm_stats(xs[0], st)
            norm_apply(1, xs[0])
            dve.wait_ge(stage_psum, len(stages))
            dve.memset(kst[:, :, :].rearrange("p a k -> p (a k)").bitcast(f32), TWO_ONES).then_inc(kst_one, 1)
            dve.memset(k1st[:, :, :].rearrange("p a k -> p (a k)").bitcast(f32), TWO_ONES).then_inc(kst_one, 1)
            norm_T(1, attT[:, :], True)
            scale_queries(1, 0, st)
            high_parts(st).then_inc(qres_ready, 1)
            meet(dve, 2)
            with dve.Fori(0, NB):
                st = Steps(dve, dve_step)
                attention0()
                st.do(normalise(0, 0, H - 2, st))
                attend_out(0, x0b, xs[1], st)
                norm(1, xs[1], st)
                experts(0, xs[1], xs[2], st)
                norm(2, xs[2], st)
                scale_queries(1, 1, st)
                st.link(high_parts(st))
                low_parts(st)
                attention1(st)
                st.do(normalise(1, 0, H - 4, st))
                st.do(normalise(1, H - 4, H - 2, st))
                attend_out(1, xs[2], xs[3], st)
                norm(3, xs[3], st)
                experts(1, xs[3], xs[4], st)
                meet(dve, 2)

        @block.gpsimd
        def _(pool):
            def rstd_of(n):
                pool.wait_ge(mv_ready, n)
                pool.tensor_tensor(rstd[:, :, :], veps[:, :, :], neg_half[:, :, :], ALU.pow).then_inc(rstd_ready, 1)

            def next_x():
                pool.wait_ge(idx_in, 16)
                pool.tensor_copy(idx_f[:, :, :], idx_i[:, :, :]).then_inc(idxf_ready, 1)
                pool.wait_ge(x_in, 16)
                st.link(pool.tensor_tensor(x0b[:, :, :], xs[0][:, :, :], bo_bc[:, :].unsqueeze(1).to_broadcast([P, NS, D]), ALU.add))

            def next_indices():
                pool.wait_ge(idxt_ready, 1)
                st.link(pool.tensor_scalar(idx_hi[:, :], idx_t[:, :], float(P), None, ALU.is_ge))
                st.link(pool.tensor_copy(idx_c[:, :, 1], idx_hi[:, :]))
                st.link(pool.tensor_scalar(idx_c[:, :, 0], idx_t[:, :], float(P), None, ALU.is_lt))
                st.link(pool.tensor_scalar(idx_hi[:, :], idx_hi[:, :], float(P), None, ALU.mult))
                st.link(pool.tensor_tensor(idx_lo[:, :], idx_t[:, :], idx_hi[:, :], ALU.subtract))

            def low_parts():
                pool.wait_ge(qres_ready, 1)
                st.link(pool.tensor_copy(qst[:, :, :, 8:16], qres[:, :, :, :]))
                st.link(pool.tensor_tensor(qst[:, :, :, 16:24], qres[:, :, :, :], qst[:, :, :, 8:16], ALU.subtract))
                st.link(pool.tensor_copy(qst[:, :, :, 24:40], qst[:, :, :, 0:16]))
                pool.tensor_copy(qst[:, :, :, 40:48], qst[:, :, :, 0:8]).then_inc(qst_ready, 1)

            def max_parts(src, p, ready, st):
                def col(t):
                    return qst[:, :, 2 * p:2 * p + 2, KROWS + t]
                st.link(pool.tensor_copy(col(0), src))
                st.link(pool.tensor_tensor(nmr[:, :, :], src, col(0), ALU.subtract))
                st.link(pool.tensor_copy(col(1), nmr[:, :, :]))
                pool.tensor_tensor(col(2), nmr[:, :, :], col(1), ALU.subtract).then_inc(ready, 1)
                pool.wait_ge(ready, p + 1)

            def attention0(st):
                for p in range(NP):
                    pool.wait_ge(nm_ready, p + 1)
                    max_parts(nm[:, p % 2, :, :], p, m_ready, st)
                    for q in range(16 * p + NHV, 16 * p + 16):
                        m = pool.tensor_scalar(onehot[:, q, :], iotab[:, :], idx_lo[:, q:q + 1], None, ALU.is_equal)
                    m.then_inc(onehot_ready, 1)

            def attention1(st):
                for p in range(NP + 1):
                    if p < NP:
                        pool.wait_ge(pair_read, p + 1)
                        max_parts(mx1[:, p, :, :].rearrange("p h s -> p s h"), p, m1_ready, st)
                    if p >= 1:
                        x = KC1 * (p - 1) + 1
                        pool.wait_ge(b1_read, fill1["e", x] + 1)
                        pool.tensor_tensor(pair_rows(x), pair_rows(x), cntT[:, 1, :].unsqueeze(1).to_broadcast([P, 2, NQ]),
                                           ALU.mult).then_inc(mulp, 1)

            def split(src, res, parts, ready, res_ready):
                pool.wait_ge(ready, 1)
                pool.tensor_tensor(res, src, parts[0], ALU.subtract).then_inc(res_ready, 1)
                pool.wait_ge(res_ready, 1)
                pool.tensor_copy(parts[1], res).then_inc(ready, 1)
                pool.wait_ge(ready, 2)
                pool.tensor_tensor(parts[2], res, parts[1], ALU.subtract).then_inc(ready, 1)
                pool.wait_ge(ready, 3)

            def next_keys():
                split(kf, kres, kpart, kp_ready, kres_ready)

            def next_keys1():
                split(kf1, kres1, kpart1, kp1_ready, kres1_ready)

            st = Steps(pool, pool_step)
            st.do(pool.memset(ident[:, :], 0.0))
            st.do(pool.memset(identb[:, :], 0.0))
            st.do(pool.iota(iota_i[:, :], pattern=[[1, P]], base=0, channel_multiplier=0))
            st.wait()
            pool.affine_select(out=ident[:, :], in_=ident[:, :], compare_op=ALU.not_equal, fill=1.0, base=0,
                               pattern=[[-1, P]], channel_multiplier=1).then_inc(const_ready, 1)
            pool.affine_select(out=identb[:, :], in_=identb[:, :], compare_op=ALU.not_equal, fill=1.0, base=0,
                               pattern=[[-1, P]], channel_multiplier=1).then_inc(const_ready, 1)
            st.do(pool.tensor_copy(iota_f[:, :], iota_i[:, :]))
            st.do(pool.tensor_copy(iotab[:, :], iota_i[:, :]))
            st.link(pool.memset(comb[:, :], 0.0))
            for t in range(4):
                part = comb[QD * t:QD * (t + 1), V1 * (t // 2):V1 * (t // 2 + 1)]
                st.link(pool.affine_select(out=part, in_=part, compare_op=ALU.not_equal, fill=1.0, base=0,
                                           pattern=[[-1, V1]], channel_multiplier=1))
            for l, width, ftot in ((0, I0, F0), (1, I1, F1)):
                pool.wait_ge(sel_zero, l + 1)
                part = sel[l][0:NE, :]
                st.link(pool.memset(part, 1.0))
                st.link(pool.affine_select(out=part, in_=part, compare_op=ALU.is_ge, fill=0.0, base=0,
                                           pattern=[[1, ftot]], channel_multiplier=-width))
                pool.affine_select(out=part, in_=part, compare_op=ALU.is_ge, fill=0.0, base=width - 1,
                                   pattern=[[-1, ftot]], channel_multiplier=width).then_inc(sel_part, 1)
                pool.wait_ge(sel_part, l + 1)
            pool.wait_ge(pre_bo, 1)
            next_x()
            rstd_of(1)
            next_keys()
            next_keys1()
            next_indices()
            low_parts()
            meet(pool, 3)
            with pool.Fori(0, NB):
                st = Steps(pool, pool_step)
                attention0(st)
                rstd_of(1)
                next_keys()
                rstd_of(2)
                attention1(st)
                rstd_of(3)
                next_keys1()
                next_x()
                rstd_of(4)
                next_indices()
                low_parts()
                meet(pool, 3)


_INS = ['x', 'ctx_1024', 'itok_BxSx64_0_2047', 'L0_xattn_Wq', 'L0_xattn_bq', 'L0_xattn_Wkv', 'L0_xattn_bkv', 'L0_xattn_Wo',
        'L0_xattn_bo', 'L0_ffn_w1', 'L0_ffn_w2', 'L0_ffn_w3', 'L0_ffn_new_w1', 'L0_ffn_new_w2', 'L0_ffn_new_w3',
        'L0_ffn_gate_weight', 'L0_ffn_new_gate_weight', 'L0_ffn_gate_bias', 'L1_xattn_W_q', 'L1_xattn_W_kv_down',
        'L1_xattn_W_kv_up', 'L1_xattn_W_out', 'L1_ffn_gate_w', 'L1_ffn_w_gate', 'L1_ffn_w_up', 'L1_ffn_w_down',
        'L1_ffn_sw_gate', 'L1_ffn_sw_up', 'L1_ffn_sw_down', 'L1_ffn_shared_gate_w']


def kernel(**inputs):
    import numpy as _np
    import concourse.bacc as _bacc
    from concourse.bass_utils import run_bass_kernel_spmd as _run

    nc = _bacc.Bacc("TRN2", target_bir_lowering=False, num_devices=1)
    arrays, args = {}, []
    for name in _INS:
        a = _np.ascontiguousarray(inputs[name])
        arrays[f"in_{name}"] = a
        args.append(nc.dram_tensor(f"in_{name}", a.shape, mybir.dt.from_np(a.dtype), kind="ExternalInput").ap())
    args.append(nc.dram_tensor("out_0", (NB, NQ, D), mybir.dt.float32, kind="ExternalOutput").ap())
    build(nc, *args)
    r = _run(nc, [arrays], core_ids=[0])
    return r.results[0]["out_0"]
```
